# Optimizing a Trainium2 kernel written in Bass

```python
import numpy as np
import jax
import jax.numpy as jnp

def _softmax(x, axis=-1):
    return jax.nn.softmax(x, axis=axis)

def _gelu(x):
    return jax.nn.gelu(x, approximate=True)

def _silu(x):
    return jax.nn.silu(x)

def _sigmoid(x):
    return jax.nn.sigmoid(x)

def _layernorm(x, axis=-1, eps=1e-05):
    m = jnp.mean(x, axis=axis, keepdims=True)
    v = jnp.var(x, axis=axis, keepdims=True)
    return (x - m) / jnp.sqrt(v + eps)

def _scatter_add(tgt, idx, src, axis=0):
    return tgt.at[idx].add(src)

def _segment_sum(src, seg, n):
    return jax.ops.segment_sum(src, seg, n)
kernel_name = 'mk_gnn_ffn_d2_gnn_r8_358b96'

def setup_inputs(seed: int=0):
    np.random.seed(seed)
    _w = jnp.asarray

    def _rec_inputs():
        import jax
        import jax.numpy as jnp
        _gk = jax.random.key(seed)
        x = -8.776e-05 + 1 * jax.random.normal(jax.random.fold_in(_gk, 1), (6250, 256), jnp.float32)
        src = jax.random.randint(jax.random.fold_in(_gk, 2), (100000,), 0, 6250, jnp.int32)
        dst = jnp.minimum((6250 * jax.random.uniform(jax.random.fold_in(_gk, 3), (100000,)) ** 2.0).astype(jnp.int32), 49999)
        _o = jnp.argsort(dst, stable=True)
        src = src[_o]
        dst = dst[_o]
        return (x, src, dst)
    x, src, dst = _rec_inputs()

    def _L0_gnn_setup():
        import jax, jax.numpy as jnp
        import numpy as np
        N, E, D, H, DK, DV, L, HUS = (2500, 40000, 256, 8, 32, 32, 2, 1024)

        def _layer_norm(x, g, b, eps=1e-05):
            mu = jnp.mean(x, axis=-1, keepdims=True)
            var = jnp.mean((x - mu) ** 2, axis=-1, keepdims=True)
            return (x - mu) * jax.lax.rsqrt(var + eps) * g + b

        def _ga_layer(h, src, dst, Wq, Wk, Wv, Wo, g, b):
            n = h.shape[0]
            q = (h @ Wq).reshape(n, H, DK)
            k = (h @ Wk).reshape(n, H, DK)
            v = (h @ Wv).reshape(n, H, DV)
            e = jnp.sum(q[dst] * k[src], axis=-1) / np.sqrt(DK).astype(np.float32)
            m = jax.ops.segment_max(e, dst, num_segments=n)
            a = jnp.exp(e - m[dst])
            z = jax.ops.segment_sum(a, dst, num_segments=n)
            alpha = a / (z[dst] + 1e-09)
            msg = v[src] * alpha[:, :, None]
            agg = jax.ops.segment_sum(msg, dst, num_segments=n).reshape(n, H * DV)
            out = agg @ Wo
            return _layer_norm(out + h, g, b)
        key = jax.random.key(seed)
        ks = jax.random.split(key, 12)
        s = 0.02
        return {'h': jax.random.normal(ks[0], (N, D), jnp.float32), 'src': jax.random.randint(ks[1], (E,), 0, N, jnp.int32), 'dst': jax.random.randint(ks[2], (E,), 0, N, jnp.int32), 'Wq': jax.random.normal(ks[3], (L, D, H * DK), jnp.float32) * s, 'Wk': jax.random.normal(ks[4], (L, D, H * DK), jnp.float32) * s, 'Wv': jax.random.normal(ks[5], (L, D, H * DV), jnp.float32) * s, 'Wo': jax.random.normal(ks[6], (L, H * DV, D), jnp.float32) * s, 'ln_g': jnp.ones((L, D), jnp.float32), 'ln_b': jnp.zeros((L, D), jnp.float32), 'w1': jax.random.normal(ks[7], (D, HUS), jnp.float32) * s, 'b1': jnp.zeros((HUS,), jnp.float32), 'w2': jax.random.normal(ks[8], (HUS, D), jnp.float32) * s, 'b2': jnp.zeros((D,), jnp.float32)}
    _L0_gnn_all = _L0_gnn_setup()
    _L0_gnn_in = {k: v for k, v in _L0_gnn_all.items() if k in ('Wq', 'Wk', 'Wv', 'Wo', 'ln_g', 'ln_b', 'w1', 'b1', 'w2', 'b2')}
    del _L0_gnn_all

    def _L0_ffn_setup():
        import math
        import jax, jax.numpy as jnp
        import numpy as np
        CAPACITY_FACTOR = 1.25
        TOP_K = 2
        LN_EPS = 1e-05

        def _layer_norm(x, gamma, beta):
            mu = jnp.mean(x, axis=-1, keepdims=True)
            var = jnp.var(x, axis=-1, keepdims=True)
            return (x - mu) * jax.lax.rsqrt(var + LN_EPS) * gamma + beta
        key = jax.random.key(seed)
        ks = jax.random.split(key, 4)
        B, S, D, F, E = (8, 512, 256, 512, 8)
        x = jax.random.normal(ks[0], (B, S, D), dtype=jnp.float32)
        Wr = jax.random.normal(ks[1], (D, E), dtype=jnp.float32) / np.sqrt(D)
        br = jnp.zeros((E,), jnp.float32)
        W1 = jax.random.normal(ks[2], (E, D, F), dtype=jnp.float32) / np.sqrt(D)
        b1 = jnp.zeros((E, F), jnp.float32)
        W2 = jax.random.normal(ks[3], (E, F, D), dtype=jnp.float32) / np.sqrt(F)
        b2 = jnp.zeros((E, D), jnp.float32)
        gamma = jnp.ones((D,), jnp.float32)
        beta = jnp.zeros((D,), jnp.float32)
        return {'x': x, 'Wr': Wr, 'br': br, 'W1': W1, 'b1': b1, 'W2': W2, 'b2': b2, 'gamma': gamma, 'beta': beta}
    _L0_ffn_all = _L0_ffn_setup()
    _L0_ffn_in = {k: v for k, v in _L0_ffn_all.items() if k in ('Wr', 'br', 'W1', 'b1', 'W2', 'b2', 'gamma', 'beta')}
    del _L0_ffn_all

    def _L1_gnn_setup():
        import jax, jax.numpy as jnp
        import numpy as np
        N = 12500
        E = 200000
        IN_FEATS = 256
        OUT_FEATS = 256
        MAXK = 32

        def _maxk(x, k):
            _, idx = jax.lax.top_k(x, k)
            rows = jnp.arange(x.shape[0])[:, None]
            mask = jnp.zeros_like(x).at[rows, idx].set(1.0)
            return x * mask
        key = jax.random.key(seed)
        k1, k2, k3, k4, k5 = jax.random.split(key, 5)
        feat = jax.random.normal(k1, (N, IN_FEATS), dtype=jnp.float32)
        W_self = jax.random.normal(k2, (IN_FEATS, OUT_FEATS), dtype=jnp.float32) * (1.0 / np.sqrt(IN_FEATS))
        W_neigh = jax.random.normal(k3, (IN_FEATS, OUT_FEATS), dtype=jnp.float32) * (1.0 / np.sqrt(IN_FEATS))
        src = jax.random.randint(k4, (E,), 0, N, dtype=jnp.int64)
        dst = jax.random.randint(k5, (E,), 0, N, dtype=jnp.int64)
        return {'feat': feat, 'W_self': W_self, 'W_neigh': W_neigh, 'src': src, 'dst': dst}
    _L1_gnn_all = _L1_gnn_setup()
    _L1_gnn_in = {k: v for k, v in _L1_gnn_all.items() if k in ('W_self', 'W_neigh')}
    del _L1_gnn_all

    def _L1_ffn_setup():
        import jax, jax.numpy as jnp
        import numpy as np
        E = 8
        K = 2
        D = 256
        H = 512
        DOUT = 256
        EPS = 1e-05
        key = jax.random.key(seed)
        ks = jax.random.split(key, 9)
        s = 0.02
        return {'x': jax.random.normal(ks[0], (4, 1024, D), jnp.float32), 'gamma': 1.0 + 0.05 * jax.random.normal(ks[1], (D,), jnp.float32), 'beta': 0.05 * jax.random.normal(ks[2], (D,), jnp.float32), 'Wr': 0.01 * jax.random.normal(ks[3], (D, E), jnp.float32), 'br': jnp.zeros((E,), jnp.float32), 'W1': s * jax.random.normal(ks[4], (E, D, H), jnp.float32), 'b1': s * jax.random.normal(ks[5], (E, H), jnp.float32), 'W2': s * jax.random.normal(ks[6], (E, H, DOUT), jnp.float32), 'b2': s * jax.random.normal(ks[7], (E, DOUT), jnp.float32)}
    _L1_ffn_all = _L1_ffn_setup()
    _L1_ffn_in = {k: v for k, v in _L1_ffn_all.items() if k in ('gamma', 'beta', 'Wr', 'br', 'W1', 'b1', 'W2', 'b2')}
    del _L1_ffn_all
    return {'x': x, 'src': src, 'dst': dst, 'L0_gnn_Wq': _L0_gnn_in['Wq'], 'L0_gnn_Wk': _L0_gnn_in['Wk'], 'L0_gnn_Wv': _L0_gnn_in['Wv'], 'L0_gnn_Wo': _L0_gnn_in['Wo'], 'L0_gnn_ln_g': _L0_gnn_in['ln_g'], 'L0_gnn_ln_b': _L0_gnn_in['ln_b'], 'L0_gnn_w1': _L0_gnn_in['w1'], 'L0_gnn_b1': _L0_gnn_in['b1'], 'L0_gnn_w2': _L0_gnn_in['w2'], 'L0_gnn_b2': _L0_gnn_in['b2'], 'L0_ffn_Wr': _L0_ffn_in['Wr'], 'L0_ffn_br': _L0_ffn_in['br'], 'L0_ffn_W1': _L0_ffn_in['W1'], 'L0_ffn_b1': _L0_ffn_in['b1'], 'L0_ffn_W2': _L0_ffn_in['W2'], 'L0_ffn_b2': _L0_ffn_in['b2'], 'L0_ffn_gamma': _L0_ffn_in['gamma'], 'L0_ffn_beta': _L0_ffn_in['beta'], 'L1_gnn_W_self': _L1_gnn_in['W_self'], 'L1_gnn_W_neigh': _L1_gnn_in['W_neigh'], 'L1_ffn_gamma': _L1_ffn_in['gamma'], 'L1_ffn_beta': _L1_ffn_in['beta'], 'L1_ffn_Wr': _L1_ffn_in['Wr'], 'L1_ffn_br': _L1_ffn_in['br'], 'L1_ffn_W1': _L1_ffn_in['W1'], 'L1_ffn_b1': _L1_ffn_in['b1'], 'L1_ffn_W2': _L1_ffn_in['W2'], 'L1_ffn_b2': _L1_ffn_in['b2']}

def reference(x, src, dst, L0_gnn_Wq, L0_gnn_Wk, L0_gnn_Wv, L0_gnn_Wo, L0_gnn_ln_g, L0_gnn_ln_b, L0_gnn_w1, L0_gnn_b1, L0_gnn_w2, L0_gnn_b2, L0_ffn_Wr, L0_ffn_br, L0_ffn_W1, L0_ffn_b1, L0_ffn_W2, L0_ffn_b2, L0_ffn_gamma, L0_ffn_beta, L1_gnn_W_self, L1_gnn_W_neigh, L1_ffn_gamma, L1_ffn_beta, L1_ffn_Wr, L1_ffn_br, L1_ffn_W1, L1_ffn_b1, L1_ffn_W2, L1_ffn_b2):
    import jax
    import jax.numpy as jnp

    def _L0_gnn_ref(h, src, dst, Wq, Wk, Wv, Wo, ln_g, ln_b, w1, b1, w2, b2):
        import jax, jax.numpy as jnp
        import numpy as np
        N, E, D, H, DK, DV, L, HUS = (2500, 40000, 256, 8, 32, 32, 2, 1024)

        def _layer_norm(x, g, b, eps=1e-05):
            mu = jnp.mean(x, axis=-1, keepdims=True)
            var = jnp.mean((x - mu) ** 2, axis=-1, keepdims=True)
            return (x - mu) * jax.lax.rsqrt(var + eps) * g + b

        def _ga_layer(h, src, dst, Wq, Wk, Wv, Wo, g, b):
            n = h.shape[0]
            q = (h @ Wq).reshape(n, H, DK)
            k = (h @ Wk).reshape(n, H, DK)
            v = (h @ Wv).reshape(n, H, DV)
            e = jnp.sum(q[dst] * k[src], axis=-1) / np.sqrt(DK).astype(np.float32)
            m = jax.ops.segment_max(e, dst, num_segments=n)
            a = jnp.exp(e - m[dst])
            z = jax.ops.segment_sum(a, dst, num_segments=n)
            alpha = a / (z[dst] + 1e-09)
            msg = v[src] * alpha[:, :, None]
            agg = jax.ops.segment_sum(msg, dst, num_segments=n).reshape(n, H * DV)
            out = agg @ Wo
            return _layer_norm(out + h, g, b)
        for l in range(Wq.shape[0]):
            h = _ga_layer(h, src, dst, Wq[l], Wk[l], Wv[l], Wo[l], ln_g[l], ln_b[l])
        return jax.nn.relu(h @ w1 + b1) @ w2 + b2

    def _L0_ffn_ref(x, Wr, br, W1, b1, W2, b2, gamma, beta):
        import math
        import jax, jax.numpy as jnp
        import numpy as np
        CAPACITY_FACTOR = 1.25
        TOP_K = 2
        LN_EPS = 1e-05

        def _layer_norm(x, gamma, beta):
            mu = jnp.mean(x, axis=-1, keepdims=True)
            var = jnp.var(x, axis=-1, keepdims=True)
            return (x - mu) * jax.lax.rsqrt(var + LN_EPS) * gamma + beta
        B, S, D = x.shape
        E = Wr.shape[1]
        N = B * S
        K = TOP_K
        logits = jnp.mean(x, axis=1) @ Wr + br
        routing_weights = jax.nn.softmax(logits, axis=-1)
        capacity = float(math.ceil(N * CAPACITY_FACTOR / E))
        expected_loads = routing_weights.sum(axis=0) * (N / B)
        scale = jnp.where(expected_loads > capacity, capacity / expected_loads, 1.0)
        routing_weights = jax.nn.softmax(routing_weights * scale, axis=-1)
        rw_tok = jnp.broadcast_to(routing_weights[:, None, :], (B, S, E)).reshape(N, E)
        top_w, top_i = jax.lax.top_k(rw_tok, K)
        top_w = jax.nn.softmax(top_w, axis=-1)
        xf = x.reshape(N, D)
        h = jax.nn.gelu(jnp.einsum('nd,edf->enf', xf, W1) + b1[:, None, :], approximate=False)
        y = jnp.einsum('enf,efd->end', h, W2) + b2[:, None, :]
        w_dense = jnp.zeros((N, E), x.dtype).at[jnp.arange(N)[:, None], top_i].add(top_w)
        out = jnp.einsum('ne,end->nd', w_dense, y).reshape(B, S, D)
        out = _layer_norm(out + x, gamma, beta)
        return out

    def _L1_gnn_ref(feat, W_self, W_neigh, src, dst):
        import jax, jax.numpy as jnp
        import numpy as np
        N = 12500
        E = 200000
        IN_FEATS = 256
        OUT_FEATS = 256
        MAXK = 32

        def _maxk(x, k):
            _, idx = jax.lax.top_k(x, k)
            rows = jnp.arange(x.shape[0])[:, None]
            mask = jnp.zeros_like(x).at[rows, idx].set(1.0)
            return x * mask
        n = feat.shape[0]
        h_self = feat @ W_self
        h_neigh = feat @ W_neigh
        h_sparse = _maxk(h_neigh, MAXK)
        msg = h_sparse[src]
        summed = jax.ops.segment_sum(msg, dst, num_segments=n)
        deg = jax.ops.segment_sum(jnp.ones((src.shape[0],), dtype=feat.dtype), dst, num_segments=n)
        neigh = summed / jnp.maximum(deg, 1.0)[:, None]
        return h_self + neigh

    def _L1_ffn_ref(x, gamma, beta, Wr, br, W1, b1, W2, b2):
        import jax, jax.numpy as jnp
        import numpy as np
        E = 8
        K = 2
        D = 256
        H = 512
        DOUT = 256
        EPS = 1e-05
        mu = jnp.mean(x, axis=-1, keepdims=True)
        var = jnp.mean(jnp.square(x - mu), axis=-1, keepdims=True)
        xn = (x - mu) * jax.lax.rsqrt(var + EPS) * gamma + beta
        logits = jnp.einsum('bsd,de->bse', xn, Wr) + br
        top_vals, top_idx = jax.lax.top_k(logits, K)
        w = jax.nn.softmax(top_vals, axis=-1)
        w_full = jnp.einsum('bsk,bske->bse', w, jax.nn.one_hot(top_idx, E, dtype=w.dtype))
        y = jnp.zeros(x.shape[:-1] + (DOUT,), x.dtype)
        for e in range(E):
            h = jax.nn.gelu(jnp.einsum('bsd,dh->bsh', xn, W1[e]) + b1[e], approximate=False)
            y_e = jnp.einsum('bsh,hd->bsd', h, W2[e]) + b2[e]
            y = y + y_e * w_full[..., e, None]
        return y
    x = x + _L0_gnn_ref(_layernorm(x, axis=-1), src, dst, L0_gnn_Wq, L0_gnn_Wk, L0_gnn_Wv, L0_gnn_Wo, L0_gnn_ln_g, L0_gnn_ln_b, L0_gnn_w1, L0_gnn_b1, L0_gnn_w2, L0_gnn_b2)
    x = x + _L0_ffn_ref(_layernorm(x, axis=-1)[None], L0_ffn_Wr, L0_ffn_br, L0_ffn_W1, L0_ffn_b1, L0_ffn_W2, L0_ffn_b2, L0_ffn_gamma, L0_ffn_beta)[0]
    x = x + _L1_gnn_ref(_layernorm(x, axis=-1), L1_gnn_W_self, L1_gnn_W_neigh, src, dst)
    x = x + _L1_ffn_ref(_layernorm(x, axis=-1)[None], L1_ffn_gamma, L1_ffn_beta, L1_ffn_Wr, L1_ffn_br, L1_ffn_W1, L1_ffn_b1, L1_ffn_W2, L1_ffn_b2)[0]
    return x

_drawn_inputs = setup_inputs


def setup_inputs(seed=0):
    import zlib

    import numpy as np

    out = dict(_drawn_inputs(seed))
    spreads = {'L0_gnn_ln_g': (1.0, 0.2),
     'L0_gnn_ln_b': (0.0, 0.382),
     'L0_gnn_b1': (0.0, 0.1),
     'L0_gnn_b2': (0.0, 0.1),
     'L0_ffn_br': (0.0, 0.1),
     'L0_ffn_b1': (0.0, 0.332),
     'L0_ffn_b2': (0.0, 0.1),
     'L0_ffn_gamma': (1.0, 0.2),
     'L0_ffn_beta': (0.0, 0.1),
     'L1_ffn_br': (0.0, 0.453)}
    factors = {'L0_gnn_Wq': 8.0,
     'L0_gnn_Wk': 8.0,
     'L0_gnn_Wv': 6.763,
     'L0_gnn_Wo': 6.717,
     'L1_ffn_gamma': 8.0,
     'L1_ffn_beta': 8.0,
     'L1_ffn_Wr': 2.726,
     'L1_ffn_b1': 23.962,
     'L1_ffn_b2': 8.0}
    for name, (base, spread) in spreads.items():
        noise = np.random.default_rng([zlib.crc32(name.encode()), seed]).standard_normal(out[name].shape)
        drawn = base * np.exp(spread * noise) if base else spread * noise
        out[name] = jnp.asarray(drawn.astype(out[name].dtype))
    for name, factor in factors.items():
        out[name] = (out[name] * factor).astype(out[name].dtype)
    return out
```

```python
import concourse.bass as bass
from concourse import mybir
from contextlib import ExitStack

F32 = mybir.dt.float32
BF16 = mybir.dt.bfloat16
I32 = mybir.dt.int32
U32 = mybir.dt.uint32
ALU = mybir.AluOpType
ACT = mybir.ActivationFunctionType
AX = mybir.AxisListType

P = 128
N, D, E = 6250, 256, 100000
H, DK = 8, 32
NODE_TILES = -(-N // P)
NT = NODE_TILES + 1
FULL_ROWS = (N // P) * P
LAST_ROWS = N - FULL_ROWS
EDGE_TILES = -(-E // P)
EC = -(-EDGE_TILES // P)
ITEMS = -(-(EDGE_TILES + NODE_TILES - 1) // 16) * 16
IC = -(-(ITEMS + 16) // P)
BATCH = 4
BATCHES = ITEMS // BATCH
RING = 16
GROUPS = ITEMS // 16
GROUPS2 = NT // 2
BIG = 1e30
TILE_BITS = 6
PAD_DST = 60000
HID = 1024
LN_EPS = 1e-5


def bc(ap, shape):
    return ap.broadcast_to(shape)


class Core:

    def __init__(self, nc, ctx):
        def sb(name, shape, dt=F32):
            return ctx.enter_context(nc.sbuf_tensor(name, shape, dt))

        self.nc = nc
        self.rows_a = sb("rows_a", [P, NT * D])
        self.rows_b = sb("rows_b", [P, GROUPS * P * 2])
        self.rows_c = sb("rows_c", [P, GROUPS * P * 2])
        self.scores = sb("scores", [P, (ITEMS + 16) * H])
        self.ident = sb("ident", [P, P])
        self.iota_n = sb("iota_n", [P, P])
        self.rel_dst = sb("rel_dst", [P, IC * P])
        self.src_idx = sb("src_idx", [P, IC * P], U32)
        self.item_tile = sb("item_tile", [1, IC * P], I32)
        self.batch_tiles = sb("batch_tiles", [1, IC * P // BATCH], I32)
        self.stats = sb("stats", [P, NT * 6])
        self.mean = sb("mean", [P, NT])
        self.rstd = sb("rstd", [P, NT])
        self.nbias = sb("nbias", [P, NT])
        self.small = sb("small", [P, 4 * NT])
        self.eps_col = sb("eps_col", [P, 1])
        self.ps = ctx.enter_context(nc.psum_tensor("ps", [P, 8 * 512], F32))
        self.h_dram = nc.dram_tensor("h_scratch", [NT * P, D], F32, kind="Internal").ap()
        self.k_dram = nc.dram_tensor("k_scratch", [NT * P, D], F32, kind="Internal").ap()
        self.v_dram = nc.dram_tensor("v_scratch", [NT * P, D], F32, kind="Internal").ap()
        self.sid_dram = nc.dram_tensor("sid_scratch", [IC * P, P], F32, kind="Internal").ap()
        self.dstp_dram = nc.dram_tensor("dst_scratch", [EDGE_TILES, P], I32, kind="Internal").ap()
        self.srcp_dram = nc.dram_tensor("src_scratch", [EDGE_TILES, P], I32, kind="Internal").ap()
        self.tile_dram = nc.dram_tensor("tile_scratch", [IC * P], I32, kind="Internal").ap()
        self.edge_sid_dram = nc.dram_tensor("edge_sid_scratch", [2, IC * P], F32, kind="Internal").ap()
        self.ends_dram = nc.dram_tensor("ends_scratch", [16, H, 2, GROUPS], F32, kind="Internal").ap()
        self.carry_dram = nc.dram_tensor("carry_scratch", [16, H, 2, GROUPS], F32, kind="Internal").ap()


class Semaphores(ExitStack):

    def __init__(self, nc):
        super().__init__()
        self.nc, self.all = nc, []

    def sem(self, name):
        one = self.nc.alloc_semaphore(name)
        self.all.append(one)
        return one

    def __exit__(self, *error):
        if not error[0]:
            self.nc.clear_and_free_semaphores(self.all)
            self.nc.all_engine_barrier()
        return super().__exit__(*error)


class Chain:

    def __init__(self, eng, sem):
        self.eng, self.sem, self.n = eng, sem, 0

    def __call__(self, ins):
        self.n += 1
        ins.then_inc(self.sem, 1)
        self.eng.wait_ge(self.sem, self.n)


def load_and_constants(c, x):
    nc = c.nc
    with Semaphores(nc) as s:
        zeroed, loaded, iotas, ready = (s.sem(n) for n in
                                        ("pad_zeroed", "x_loaded", "const_iotas", "ident_ready"))
        ip = s.enter_context(nc.sbuf_tensor("iota_p", [P, 1], F32))
        with nc.Block() as block:
            @block.sync
            def _(sp):
                rows = c.rows_a[:, :].rearrange("p (t d) -> p t d", d=D)
                sp.dma_start(rows[:, 0:FULL_ROWS // P, :],
                             x[0:FULL_ROWS, :].rearrange("(t p) d -> p t d", p=P)).then_inc(loaded, 16)
                sp.wait_ge(zeroed, 1)
                sp.dma_start(rows[0:LAST_ROWS, FULL_ROWS // P, :], x[FULL_ROWS:N, :]).then_inc(loaded, 16)
                sp.wait_ge(loaded, 32)

            @block.gpsimd
            def _(pool):
                pool.iota(c.iota_n[:, :], [[1, P]], base=0, channel_multiplier=0,
                          allow_small_or_imprecise_dtypes=True).then_inc(iotas, 1)
                pool.iota(ip[:, :], [[1, 1]], base=0, channel_multiplier=1,
                          allow_small_or_imprecise_dtypes=True).then_inc(iotas, 1)

            @block.vector
            def _(v):
                v.memset(c.rows_a[:, FULL_ROWS // P * D:NT * D], 0.0).then_inc(zeroed, 1)
                v.memset(c.eps_col[:, :], LN_EPS)
                v.wait_ge(iotas, 2)
                v.tensor_scalar(c.ident[:, :], c.iota_n[:, :], ip[:, 0:1], None, ALU.is_equal).then_inc(ready, 1)
                v.wait_ge(ready, 1)


def item_tables(c, src, dst):
    nc = c.nc
    whole = EDGE_TILES - 1
    tail = E - whole * P
    cols, rest = whole // P, whole % P
    b = c.rows_b
    at = [0]

    def take(n, dt=F32):
        a = b[:, at[0]:at[0] + n]
        at[0] += n
        return a if dt == F32 else a.bitcast(dt)

    dt_i = take(EC * P, I32).rearrange("p (c e) -> p c e", e=P)
    st_i = take(EC * P, I32).rearrange("p (c e) -> p c e", e=P)
    d_i = take(IC * P, I32).rearrange("p (c e) -> p c e", e=P)
    s_i = take(IC * P, I32).rearrange("p (c e) -> p c e", e=P)
    ends = take(2 * EC).rearrange("p (k c) -> p k c", k=2)
    limits = take(2 * NODE_TILES).rearrange("p (k j) -> p k j", k=2)
    below = take(2 * EC * NODE_TILES).rearrange("p (k c j) -> p k c j", k=2, c=EC)
    ones = take(P)
    counts = take(2 * NODE_TILES).rearrange("p (k j) -> p k j", k=2)
    size, upto, first, shift = (take(NODE_TILES) for _ in range(4))
    item_no = take(IC)
    past = take(IC * NODE_TILES).rearrange("p (c j) -> p c j", c=IC)
    moved = take(IC * NODE_TILES).rearrange("p (c j) -> p c j", c=IC)
    tile_no = take(IC)
    edge_tile = take(IC)
    edge_tile_u = take(IC, U32)
    tile_i = take(IC, I32)
    dst_f = take(IC * P).rearrange("p (c e) -> p c e", e=P)
    src_f = take(IC * P).rearrange("p (c e) -> p c e", e=P)
    rel = take(IC * P).rearrange("p (c e) -> p c e", e=P)
    valid = take(IC * P).rearrange("p (c e) -> p c e", e=P)
    sid = take(IC * P).rearrange("p (c e) -> p c e", e=P)
    row_f = take(IC * P)[0:1]
    with Semaphores(nc) as s:
        def sem(n):
            return s.sem(n)
        padded, loaded, saved, iotas = sem("padded"), sem("edges_loaded"), sem("edges_saved"), sem("iotas")
        step, summed, rows_at, gathered = sem("table_step"), sem("ends_summed"), sem("edge_tile_ready"), sem("rows_gathered")
        turned, copied, sid_ready, written = sem("turned"), sem("turned_copied"), sem("sid_ready"), sem("tables_written")
        rel_ready, tiles_back = sem("rel_ready"), sem("tiles_back")
        with nc.Block() as block:
            @block.sync
            def _(sp):
                sp.wait_ge(padded, 2)
                for flat, to in ((dst, dt_i), (src, st_i)):
                    rows = flat[0:whole * P].rearrange("(k e) -> k e", e=P)
                    sp.dma_start(to[:, 0:cols, :], rows[0:cols * P, :].rearrange("(c p) e -> p c e", p=P)).then_inc(loaded, 16)
                    sp.dma_start(to[0:rest, cols, :], rows[cols * P:whole, :]).then_inc(loaded, 16)
                    sp.dma_start(to[rest:rest + 1, cols, 0:tail], flat[whole * P:E].rearrange("(a e) -> a e", a=1)).then_inc(loaded, 16)
                sp.wait_ge(loaded, 96)
                for ap, to in ((dt_i, c.dstp_dram), (st_i, c.srcp_dram)):
                    sp.dma_start(to[0:cols * P, :].rearrange("(c p) e -> p c e", p=P), ap[:, 0:cols, :]).then_inc(saved, 16)
                    sp.dma_start(to[cols * P:EDGE_TILES, :], ap[0:rest + 1, cols, :]).then_inc(saved, 16)
                sp.wait_ge(sid_ready, 1)
                sp.dma_start(c.sid_dram[:, :].rearrange("(c p) e -> p c e", p=P), sid).then_inc(written, 16)
                with nc.allow_non_contiguous_dma("one number an item"):
                    sp.dma_start(c.tile_dram.rearrange("(c p) -> p c", p=P), tile_i).then_inc(written, 16)
                    sp.dma_start(c.edge_sid_dram[0].rearrange("(c p) -> p c", p=P), sid[:, :, 0]).then_inc(written, 16)
                    sp.dma_start(c.edge_sid_dram[1].rearrange("(c p) -> p c", p=P), sid[:, :, P - 1]).then_inc(written, 16)
                sp.wait_ge(written, 64)
                sp.dma_start(c.item_tile[:, :], c.tile_dram.rearrange("(a i) -> a i", a=1)).then_inc(tiles_back, 16)

            @block.gpsimd
            def _(pool):
                pool.iota(limits[:, 0, :], [[P, NODE_TILES]], base=0, channel_multiplier=0,
                          allow_small_or_imprecise_dtypes=True).then_inc(iotas, 1)
                pool.iota(limits[:, 1, :], [[P, NODE_TILES]], base=P, channel_multiplier=0,
                          allow_small_or_imprecise_dtypes=True).then_inc(iotas, 1)
                pool.iota(item_no, [[P, IC]], base=0, channel_multiplier=1,
                          allow_small_or_imprecise_dtypes=True).then_inc(iotas, 1)
                pool.wait_ge(saved, 64)
                pool.wait_ge(rows_at, 1)
                for i in range(IC):
                    at_row = bass.IndirectOffsetOnAxis(ap=edge_tile_u[:, i:i + 1], axis=0)
                    pool.indirect_dma_start(d_i[:, i, :], None, c.dstp_dram[:, :], at_row).then_inc(gathered, 16)
                    pool.indirect_dma_start(s_i[:, i, :], None, c.srcp_dram[:, :], at_row).then_inc(gathered, 16)

            @block.vector
            def _(v):
                do = Chain(v, step)
                v.memset(dt_i, PAD_DST).then_inc(padded, 1)
                v.memset(st_i, 0).then_inc(padded, 1)
                do(v.memset(ones, 1.0))
                v.wait_ge(loaded, 96)
                do(v.tensor_copy(ends[:, 0, :], dt_i[:, :, P - 1]))
                do(v.tensor_copy(ends[:, 1, :], dt_i[:, :, 0]))
                v.wait_ge(iotas, 3)
                for k in range(2):
                    do(v.tensor_tensor(below[:, k], bc(ends[:, k].unsqueeze(2), [P, EC, NODE_TILES]),
                                       bc(limits[:, k].unsqueeze(1), [P, EC, NODE_TILES]), ALU.is_lt))
                v.wait_ge(summed, 1)
                do(v.tensor_copy(counts.rearrange("p k j -> p (k j)"), c.ps[:, 0:2 * NODE_TILES]))
                do(v.tensor_tensor(size, counts[:, 1], counts[:, 0], ALU.subtract))
                do(v.tensor_tensor_scan(upto, ones[:, 0:NODE_TILES], size, 0.0, ALU.mult, ALU.add))
                do(v.tensor_tensor(first, upto, size, ALU.subtract))
                do(v.tensor_tensor(first, counts[:, 0], first, ALU.subtract))
                do(v.memset(shift, 0.0))
                do(v.tensor_tensor(shift[:, 0:NODE_TILES - 1], first[:, 1:], first[:, :NODE_TILES - 1], ALU.subtract))
                do(v.tensor_tensor(past, bc(upto.unsqueeze(1), [P, IC, NODE_TILES]),
                                   bc(item_no.unsqueeze(2), [P, IC, NODE_TILES]), ALU.is_le))
                do(v.tensor_reduce(tile_no, past, AX.X, ALU.add))
                do(v.tensor_tensor(moved, past, bc(shift.unsqueeze(1), [P, IC, NODE_TILES]), ALU.mult))
                do(v.tensor_reduce(edge_tile, moved, AX.X, ALU.add))
                do(v.tensor_tensor(edge_tile, edge_tile, item_no, ALU.add))
                do(v.tensor_scalar(edge_tile, edge_tile, 0.0, float(EDGE_TILES - 1), ALU.max, ALU.min))
                v.tensor_copy(edge_tile_u, edge_tile).then_inc(rows_at, 1)
                do(v.tensor_copy(tile_i, tile_no))
                do(v.tensor_scalar(tile_no, tile_no, float(P), None, ALU.mult))
                v.wait_ge(gathered, 32 * IC)
                do(v.tensor_copy(dst_f, d_i))
                do(v.tensor_copy(src_f, s_i))
                do(v.tensor_tensor(rel, dst_f, bc(tile_no.unsqueeze(2), [P, IC, P]), ALU.subtract))
                v.sem_inc(rel_ready, 1)
                do(v.tensor_scalar(valid, rel, 0.0, None, ALU.is_ge))
                do(v.tensor_scalar(sid, rel, float(P), None, ALU.is_lt))
                do(v.tensor_tensor(valid, valid, sid, ALU.mult))
                do(v.tensor_scalar(dst_f, dst_f, 1.0, None, ALU.add))
                do(v.tensor_tensor(valid, valid, dst_f, ALU.mult))
                do(v.tensor_scalar(sid, valid, 1.0, None, ALU.subtract))
                v.sem_inc(sid_ready, 1)
                v.wait_ge(turned, 1)
                v.tensor_copy(c.rel_dst[:, :], c.ps[:, 1024:1024 + IC * P]).then_inc(copied, 1)
                v.tensor_copy(c.src_idx[:, :], c.ps[:, 2048:2048 + IC * P]).then_inc(copied, 1)
                v.wait_ge(copied, 2)
                v.wait_ge(tiles_back, 16)
                do(v.tensor_copy(row_f, c.item_tile[:, :]))
                each = row_f.rearrange("p (b u) -> p u b", u=BATCH)
                for u in range(1, BATCH):
                    do(v.scalar_tensor_tensor(each[:, 0], each[:, u], float(1 << (TILE_BITS * u)), each[:, 0],
                                              ALU.mult, ALU.add))
                do(v.tensor_copy(c.batch_tiles[:, :], each[:, 0]))

            @block.tensor
            def _(pe):
                pe.wait_ge(step, 5)
                for k in range(2):
                    for i in range(EC):
                        mm = pe.matmul(c.ps[:, k * NODE_TILES:(k + 1) * NODE_TILES], ones, below[:, k, i, :],
                                       start=(i == 0), stop=(i == EC - 1))
                mm.then_inc(summed, 1)
                pe.wait_ge(rel_ready, 1)
                for k, tab in ((0, rel), (1, src_f)):
                    for i in range(IC):
                        to = 1024 * (1 + k) + i * P
                        mm = pe.transpose(c.ps[:, to:to + P], tab[:, i, :], c.ident[:, :])
                mm.then_inc(turned, 1)


def layer_norm(c, src, dst, name, tiles=NT):
    nc = c.nc
    with Semaphores(nc) as s:
        taken, step, rooted, var_ready = (s.sem(f"{name}_{n}")
                                          for n in ("stats", "step", "root", "var"))
        with nc.Block() as block:
            @block.vector
            def _(v):
                ln_vector(c, v, src, dst, taken, step, rooted, var_ready, tiles)

            @block.scalar
            def _(a):
                a.wait_ge(var_ready, 1)
                a.activation(c.rstd[:, 0:tiles], c.rstd[:, 0:tiles], ACT.Sqrt,
                             bias=c.eps_col[:, 0:1]).then_inc(rooted, 1)


def ln_vector(c, v, src, dst, taken, step, rooted, var_ready, tiles):
    do = Chain(v, step)
    with v.Fori(0, tiles // 10) as i:
        for u in range(10):
            v.bn_stats(c.stats[:, bass.ds(i * 60 + u * 6, 6)], src[:, bass.ds(i * 10 * D + u * D, D)]).then_inc(taken, 1)
    v.wait_ge(taken, tiles)
    st = c.stats[:, :].rearrange("p (t k) -> p k t", k=6)
    tmp = c.small[:, 0:NT]
    do(v.tensor_tensor(c.mean[:, :], st[:, 1, :], st[:, 4, :], ALU.add))
    do(v.tensor_scalar(c.mean[:, :], c.mean[:, :], 0.5, None, ALU.mult))
    do(v.tensor_tensor(tmp, st[:, 1, :], st[:, 4, :], ALU.subtract))
    do(v.tensor_tensor(tmp, tmp, tmp, ALU.mult))
    do(v.tensor_tensor(c.rstd[:, :], st[:, 2, :], st[:, 5, :], ALU.add))
    do(v.tensor_scalar(tmp, tmp, D / 4.0, None, ALU.mult))
    do(v.tensor_tensor(c.rstd[:, :], c.rstd[:, :], tmp, ALU.add))
    do(v.tensor_scalar(c.rstd[:, :], c.rstd[:, :], 1.0 / D, None, ALU.mult))
    v.sem_inc(var_ready, 1)
    v.wait_ge(rooted, 1)
    do(v.reciprocal(c.rstd[:, :], c.rstd[:, :]))
    with v.Fori(0, tiles // 10) as i:
        for u in range(10):
            at, t = bass.ds(i * 10 * D + u * D, D), bass.ds(i * 10 + u, 1)
            v.tensor_scalar(dst[:, at], src[:, at], c.mean[:, t], c.rstd[:, t], ALU.subtract, ALU.mult).then_inc(taken, 1)
    v.wait_ge(taken, 2 * tiles)



def groups(eng, body):
    with eng.Fori(0, GROUPS2 // 2) as i:
        body(i * 2, 0, False)
        body(i * 2 + 1, 1, False)
    body(GROUPS2 - 1, (GROUPS2 - 1) % 2, True)


def turn(pe, c, staged_rows, parity):
    for k in range(2):
        for u in range(2):
            to = parity * 512 + k * 2 * P + u * P
            mm = pe.transpose(c.ps[:, to:to + P], staged_rows[:, u * D + k * P:u * D + k * P + P], c.ident[:, :])
    return mm


def load_tiles(eng, c, b):
    packed = eng.value_load(c.batch_tiles[0:1, bass.ds(b, 1)], min_val=0, max_val=(1 << TILE_BITS * BATCH) - 1)
    why = "the item table counts node tiles from 0 to NODE_TILES"
    return [c.nc.s_assert_within((packed >> (TILE_BITS * u)) & ((1 << TILE_BITS) - 1), 0, NODE_TILES,
                                 skip_runtime_bounds_check_because=why) for u in range(BATCH)]


class Front:

    def __init__(self, c, s, name, rows, turned_rows, source):
        self.c, self.rows, self.turned_rows, self.source = c, rows, turned_rows, source
        self.staged, self.turned, self.copied, self.used = (
            s.sem(f"{name}_{n}") for n in ("staged", "turned", "copied", "used"))

    def start_pe(self, pe):
        pe.sem_inc(self.turned, 2)
        pe.sem_inc(self.used, 2)

    def start_vector(self, v):
        v.sem_inc(self.copied, 2)

    def stage(self, a, g, parity):
        a.wait_ge(self.turned, g + 1)
        a.activation(self.rows[parity], self.source[:, bass.ds(g * 2 * D, 2 * D)],
                     ACT.Copy).then_inc(self.staged, 1)

    def turn(self, pe, g, parity):
        pe.wait_ge(self.staged, g + 1)
        pe.wait_ge(self.copied, g + 1)
        turn(pe, self.c, self.rows[parity], parity).then_inc(self.turned, 1)

    def copy(self, v, g, parity):
        v.wait_ge(self.used, g + 1)
        v.wait_ge(self.turned, g + 3)
        v.tensor_copy(self.turned_rows[:, parity], self.c.ps[:, parity * 512:parity * 512 + 512]).then_inc(self.copied, 1)


def qkv(c, wq, wk, wv, name):
    nc = c.nc
    w = c.scores[:, 0:2 * 3 * D].rearrange("p (k n) -> p k n", k=2)
    rows = [c.scores[:, 1536 + k * 512:2048 + k * 512] for k in range(2)]
    rows_t = c.scores[:, 2560:3584].rearrange("p (b n) -> p b n", b=2)
    kv = c.scores[:, 3584:3584 + 4 * 2 * D].rearrange("p (b n) -> p b n", b=4)
    scale = float(DK) ** -0.5
    with Semaphores(nc) as s:
        def sem(n):
            return s.sem(f"{name}_{n}")
        loaded, saved, out_done, kv_ready = sem("w_loaded"), sem("h_saved"), sem("out_done"), sem("kv_ready")
        stored, kv_free = [sem(f"stored{u}") for u in range(4)], sem("kv_free")
        f = Front(c, s, name, rows, rows_t, c.rows_a)
        with nc.Block() as block:
            @block.sync
            def _(sp):
                for j, m in enumerate((wq, wk, wv)):
                    sp.dma_start(w[:, :, j * D:(j + 1) * D], m.rearrange("(k p) n -> p k n", p=P)).then_inc(loaded, 16)
                sp.dma_start(c.h_dram.rearrange("(t p) d -> p t d", p=P),
                             c.rows_a[:, :].rearrange("p (t d) -> p t d", d=D)).then_inc(saved, 16)

                def body(g, parity, last):
                    for u in range(2):
                        b = 2 * parity + u
                        sp.wait_ge(kv_ready, g * 2 + u + 1)
                        for to, n in ((c.k_dram, 0), (c.v_dram, D)):
                            sp.dma_start(to[bass.ds(g * 2 * P + u * P, P), :], kv[:, b, n:n + D]).then_inc(stored[b], 16)
                    for u in range(2):
                        sp.wait_ge(stored[2 * parity + u], (g - parity) * 16 + 32)
                        sp.sem_inc(kv_free, 1)
                groups(sp, body)
                sp.wait_ge(saved, 16)

            @block.scalar
            def _(a):
                groups(a, lambda g, parity, last: f.stage(a, g, parity))

            @block.tensor
            def _(pe):
                f.start_pe(pe)
                pe.wait_ge(loaded, 48)
                f.turn(pe, 0, 0)

                def body(g, parity, last):
                    if not last:
                        f.turn(pe, g + 1, 1 - parity)
                    pe.wait_ge(f.copied, g + 3)
                    pe.wait_ge(out_done, g + 1)
                    for u in range(2):
                        for k in range(2):
                            x = rows_t[:, parity, k * 2 * P + u * P:k * 2 * P + u * P + P]
                            q = (2 + parity) * 512 + u * D
                            pe.matmul(c.ps[:, q:q + D], x, w[:, k, 0:D], start=(k == 0), stop=(k == 1))
                        for k in range(2):
                            x = rows_t[:, parity, k * 2 * P + u * P:k * 2 * P + u * P + P]
                            to = (4 + 2 * parity + u) * 512
                            mm = pe.matmul(c.ps[:, to:to + 512], x, w[:, k, D:3 * D], start=(k == 0), stop=(k == 1))
                    mm.then_inc(f.used, 1)
                groups(pe, body)

            @block.vector
            def _(v):
                f.start_vector(v)
                v.sem_inc(out_done, 2)
                v.sem_inc(kv_free, 4)
                f.copy(v, 0, 0)

                def body(g, parity, last):
                    if not last:
                        f.copy(v, g + 1, 1 - parity)
                    v.wait_ge(f.used, g + 3)
                    for u in range(2):
                        b = 2 * parity + u
                        v.wait_ge(kv_free, g * 2 + u + 1)
                        to = (4 + b) * 512
                        v.tensor_copy(kv[:, b, :], c.ps[:, to:to + 512]).then_inc(kv_ready, 1)
                    q = (2 + parity) * 512
                    v.tensor_scalar(c.rows_b[:, bass.ds(g * 2 * D, 2 * D)], c.ps[:, q:q + 512], scale, None,
                                    ALU.mult).then_inc(out_done, 1)
                groups(v, body)
                v.wait_ge(out_done, GROUPS2 + 2)


def one_hot(c, v, s_buf, b, parity):
    return v.tensor_tensor(s_buf[:, parity], bc(c.iota_n[:, :].unsqueeze(1), [P, BATCH, P]),
                           bc(c.rel_dst[:, bass.ds(b * BATCH, BATCH)].unsqueeze(2), [P, BATCH, P]), ALU.is_equal)


def gather_rows(c, pool, table, ring, width, idx, staged, free, gate, landed, extra, per_batch=1):
    half = RING // 2

    def fetch(i, h, n):
        pool.wait_ge(free, (i * (RING // BATCH) + (h + 1) * (half // BATCH)) * per_batch)
        pool.sem_inc(gate, 1)
        pool.tensor_copy(idx[:, h * half:h * half + n], c.src_idx[:, bass.ds(i * RING + h * half, n)]).then_inc(staged, 1)
        pool.wait_ge(staged, i * 2 + h + 1)
        pool.sem_inc(gate, 1)
        for u in range(n):
            slot = h * half + u
            pool.indirect_dma_start(ring[:, slot, 0:width], None, table,
                                    bass.IndirectOffsetOnAxis(ap=idx[:, slot:slot + 1], axis=0)).then_inc(landed[slot], 16)

    with pool.Fori(0, ITEMS // RING) as i:
        fetch(i, 0, half)
        fetch(i, 1, half)
    if extra:
        fetch(ITEMS // RING, 0, half)


def edge_scores(c, name):
    nc = c.nc
    BW = BATCH * D
    ring = c.rows_a[:, 0:RING * D].rearrange("p (s d) -> p s d", d=D)
    s_buf = c.rows_a[:, RING * D:RING * D + 2048].rearrange("p (b i n) -> p b i n", b=4, i=BATCH)
    st_buf = c.rows_a[:, RING * D + 2048:RING * D + 3072].rearrange("p (b i n) -> p b i n", b=2, i=BATCH)
    prod = c.rows_a[:, RING * D + 3072:RING * D + 5120].rearrange("p (b n) -> p b n", b=2)
    QPS = 1024
    with Semaphores(nc) as s:
        def sem(n):
            return s.sem(f"{name}_{n}")
        free, staged, gate, made, turned = sem("slots_free"), sem("idx"), sem("gate"), sem("onehot"), sem("turned")
        copied, expanded, multiplied, reduced = sem("copied"), sem("expanded"), sem("multiplied"), sem("reduced")
        landed = [sem(f"landed{u}") for u in range(RING)]
        idx = s.enter_context(nc.sbuf_tensor(f"{name}_idx", [P, RING], U32))
        with nc.Block() as block:
            @block.gpsimd
            def _(pool):
                gather_rows(c, pool, c.k_dram[:, :], ring, D, idx, staged, free, gate, landed, False)

            @block.vector
            def _(v):
                v.sem_inc(free, RING // BATCH)
                v.sem_inc(multiplied, 2)
                v.sem_inc(reduced, 2)
                one_hot(c, v, s_buf, 0, 0).then_inc(made, 1)
                one_hot(c, v, s_buf, 1, 1).then_inc(made, 1)
                with v.Fori(0, BATCHES // 4) as i:
                    for q in range(4):
                        b, par = i * 4 + q, q % 2
                        v.wait_ge(turned, b + 1)
                        one_hot(c, v, s_buf, b + 2, (q + 2) % 4).then_inc(made, 1)
                        v.wait_ge(expanded, b + 3)
                        for u in range(BATCH):
                            v.wait_ge(landed[q * BATCH + u], i * 16 + 16)
                        v.wait_ge(reduced, b + 1)
                        v.tensor_tensor(prod[:, par], c.ps[:, QPS + par * BW:QPS + (par + 1) * BW],
                                        ring[:, q * BATCH:(q + 1) * BATCH, :].rearrange("p s d -> p (s d)"),
                                        ALU.mult).then_inc(multiplied, 1)
                        v.wait_ge(multiplied, b + 3)
                        v.sem_inc(free, 1)
                        v.tensor_reduce(c.scores[:, bass.ds(b * BATCH * H, BATCH * H)],
                                        prod[:, par].rearrange("p (h k) -> p h k", k=DK), AX.X, ALU.add).then_inc(reduced, 1)
                v.wait_ge(reduced, BATCHES + 2)

            @block.scalar
            def _(a):
                a.sem_inc(copied, 2)
                with a.Fori(0, BATCHES // 2) as i:
                    for par in range(2):
                        b = i * 2 + par
                        a.wait_ge(expanded, b + 1)
                        a.wait_ge(turned, b + 3)
                        a.activation(st_buf[:, par].rearrange("p i n -> p (i n)"), c.ps[:, par * 512:par * 512 + 512],
                                     ACT.Copy).then_inc(copied, 1)

            @block.tensor
            def _(pe):
                pe.sem_inc(turned, 2)
                pe.sem_inc(expanded, 2)

                def flip(b, slot):
                    par = slot % 2
                    pe.wait_ge(made, b + 1)
                    pe.wait_ge(copied, b + 1)
                    for u in range(BATCH):
                        mm = pe.transpose(c.ps[:, par * 512 + u * P:par * 512 + u * P + P], s_buf[:, slot, u, :], c.ident[:, :])
                    mm.then_inc(turned, 1)
                flip(0, 0)
                with pe.Fori(0, BATCHES // 4) as i:
                    for q in range(4):
                        b, par = i * 4 + q, q % 2
                        flip(b + 1, (q + 1) % 4)
                        tiles = load_tiles(pe, c, b)
                        pe.wait_ge(copied, b + 3)
                        pe.wait_ge(multiplied, b + 1)
                        for u in range(BATCH):
                            to = QPS + par * BW + u * D
                            mm = pe.matmul(c.ps[:, to:to + D], st_buf[:, par, u, :], c.rows_b[:, bass.ds(tiles[u] * D, D)],
                                           start=True, stop=True)
                        mm.then_inc(expanded, 1)


def segment_masks(c):
    nc = c.nc
    n = GROUPS * P
    sid = c.rows_b[:, 0:n]
    sid3 = sid.rearrange("p (g e) -> p g e", e=P)
    c.link = c.rows_c[:, 0:n // 2 + 1].bitcast(BF16)
    c.to_first = c.rows_c[:, n // 2 + 1:n + 1].bitcast(BF16)
    c.to_last = c.rows_c[:, n + 1:n + 1 + n // 2].bitcast(BF16)
    o = n + 1 + n // 2
    c.item_link = c.rows_c[0:H, o:o + ITEMS + 1]
    c.item_whole = c.rows_c[0:H, o + ITEMS + 1:o + 2 * ITEMS + 1]
    assert o + 2 * ITEMS + 1 <= 2 * n
    ends = c.rows_b[0:H, n:n + 2 * ITEMS].rearrange("p (k i) -> p k i", k=2)
    with Semaphores(nc) as s:
        loaded, step = s.sem("sid_loaded"), s.sem("mask_step")
        with nc.Block() as block:
            @block.sync
            def _(sp):
                for h in range(H):
                    sp.dma_start(sid3[h * 16:(h + 1) * 16], c.sid_dram[0:ITEMS, :].rearrange("(g i) e -> i g e", i=16)).then_inc(loaded, 16)
                for h in range(H):
                    sp.dma_start(ends[h:h + 1], c.edge_sid_dram[:, 0:ITEMS].rearrange("(a k) i -> a k i", a=1)).then_inc(loaded, 16)

            @block.vector
            def _(v):
                do = Chain(v, step)
                v.wait_ge(loaded, 32 * H)

                def masked(out, a, b):
                    do(v.tensor_tensor(out, a, b, ALU.is_equal))
                    do(v.tensor_scalar(out, out, 1.0, BIG, ALU.subtract, ALU.mult))
                link3 = c.link[:, 0:n].rearrange("p (g e) -> p g e", e=P)
                do(v.memset(c.link, 0.0))
                masked(link3[:, :, 1:], sid3[:, :, 1:], sid3[:, :, :P - 1])
                do(v.memset(link3[:, :, 0:1], -BIG))
                do(v.memset(c.link[:, n:n + 2], -BIG))
                for out, e in ((c.to_first, 0), (c.to_last, P - 1)):
                    masked(out.rearrange("p (g e) -> p g e", e=P), sid3, bc(sid3[:, :, e:e + 1], [P, GROUPS, P]))
                do(v.memset(c.item_link, -BIG))
                masked(c.item_link[:, 1:ITEMS], ends[:, 0, 1:ITEMS], ends[:, 1, 0:ITEMS - 1])
                masked(c.item_whole, ends[:, 0, :], ends[:, 1, :])


def segment_softmax(c, name):
    nc = c.nc
    n = GROUPS * P
    e = c.rows_b[:, 0:n]
    f = c.rows_b[:, n:2 * n]
    m = c.rows_a[:, 0:n]
    ends = c.rows_a[:, n:n + 2 * GROUPS].rearrange("p (k g) -> p k g", k=2)
    t = [n + 2 * GROUPS]

    def take(k):
        a = c.rows_a[0:H, t[0]:t[0] + k]
        t[0] += k
        return a
    ends_t = take(2 * ITEMS).rearrange("p (k i g) -> p k i g", k=2, i=16)
    seq = take(2 * ITEMS).rearrange("p (k i) -> p k i", k=2)
    assert t[0] <= NT * D
    fwd, back = (c.scores[0:H, k * ITEMS:(k + 1) * ITEMS] for k in range(2))
    wl, wr = (c.scores[0:H, (2 + k) * ITEMS:(3 + k) * ITEMS] for k in range(2))
    rounds = GROUPS // 4
    by_group = c.scores[:, 0:ITEMS * H].rearrange("p (g i h) -> p g h i", g=GROUPS, i=16)
    turned_in = c.rows_a
    with Semaphores(nc) as s:
        def sem(x):
            return s.sem(f"{name}_{x}")
        arranged, turned, copied, step, saved = sem("arranged"), sem("turned"), sem("copied"), sem("step"), sem("saved")
        sent, carried, seq_done, ready, exped = sem("sent"), sem("carried"), sem("seq_done"), sem("ready"), sem("exped")
        back_turned, back_copied = sem("back_turned"), sem("back_copied")
        with nc.Block() as block:
            @block.tensor
            def _(pe):
                for r in range(rounds):
                    pe.wait_ge(arranged, r + 1)
                    if r >= 2:
                        pe.wait_ge(copied, r - 1)
                    for u in range(4):
                        to = (r % 2) * 512 + u * P
                        g = r * 4 + u
                        mm = pe.transpose(c.ps[:, to:to + P], f[:, g * P:(g + 1) * P], c.ident[:, :])
                    mm.then_inc(turned, 1)
                for r in range(rounds):
                    if r == 0:
                        pe.wait_ge(exped, 1)
                        pe.wait_ge(copied, rounds)
                    if r >= 2:
                        pe.wait_ge(back_copied, r - 1)
                    for u in range(4):
                        to = (r % 2) * 512 + u * P
                        g = r * 4 + u
                        mm = pe.transpose(c.ps[:, to:to + P], e[:, g * P:(g + 1) * P], c.ident[:, :])
                    mm.then_inc(back_turned, 1)

            @block.scalar
            def _(a):
                for r in range(rounds):
                    a.wait_ge(turned, r + 1)
                    a.activation(e[:, r * 512:(r + 1) * 512], c.ps[:, (r % 2) * 512:(r % 2) * 512 + 512], ACT.Copy).then_inc(copied, 1)
                a.wait_ge(copied, rounds)
                a.wait_ge(ready, 1)
                a.activation(e, e, ACT.Exp).then_inc(exped, 1)

            @block.sync
            def _(sp):
                sp.wait_ge(saved, 1)
                for h in range(H):
                    sp.dma_start(c.ends_dram[:, h, :, :], ends[h * 16:(h + 1) * 16]).then_inc(sent, 16)
                sp.wait_ge(sent, 16 * H)
                for k in range(2):
                    sp.dma_start(ends_t[:, k], c.ends_dram[:, :, k, :].rearrange("i h g -> h i g")).then_inc(carried, 16)
                sp.wait_ge(seq_done, 1)
                for k in range(2):
                    sp.dma_start(c.carry_dram[:, :, k, :].rearrange("i h g -> h i g"), ends_t[:, k]).then_inc(sent, 16)
                sp.wait_ge(sent, 16 * H + 32)
                for h in range(H):
                    sp.dma_start(ends[h * 16:(h + 1) * 16], c.carry_dram[:, h, :, :]).then_inc(carried, 16)
                sp.wait_ge(carried, 32 + 16 * H)

            @block.vector
            def _(v):
                do = Chain(v, step)
                for r in range(rounds):
                    v.tensor_copy(f[:, r * 512:(r + 1) * 512].rearrange("p (g h i) -> p g h i", g=4, h=H),
                                  by_group[:, r * 4:(r + 1) * 4]).then_inc(arranged, 1)
                v.wait_ge(copied, rounds)
                do(v.tensor_tensor_scan(f, c.link[:, 0:n], e, -BIG, ALU.add, ALU.max))
                do(v.tensor_tensor_scan(m[:, ::-1], c.link[:, 1:n + 1][:, ::-1], f[:, ::-1], -BIG, ALU.add, ALU.max))
                m3 = m.rearrange("p (g e) -> p g e", e=P)
                do(v.tensor_copy(ends[:, 0, :], m3[:, :, 0]))
                do(v.tensor_copy(ends[:, 1, :], m3[:, :, P - 1]))
                v.sem_inc(saved, 1)
                do(v.tensor_tensor(wl, c.item_whole, c.item_link[:, 0:ITEMS], ALU.add))
                do(v.tensor_tensor(wr, c.item_whole, c.item_link[:, 1:ITEMS + 1], ALU.add))
                v.wait_ge(carried, 32)
                for k in range(2):
                    do(v.tensor_copy(seq[:, k].rearrange("p (g i) -> p i g", i=16), ends_t[:, k]))
                do(v.tensor_tensor_scan(fwd, wl, seq[:, 1], -BIG, ALU.add, ALU.max))
                do(v.tensor_tensor_scan(back[:, ::-1], wr[:, ::-1], seq[:, 0][:, ::-1], -BIG, ALU.add, ALU.max))
                do(v.memset(seq.rearrange("p k i -> p (k i)"), -BIG))
                do(v.tensor_tensor(seq[:, 0, 1:], fwd[:, 0:ITEMS - 1], c.item_link[:, 1:ITEMS], ALU.add))
                do(v.tensor_tensor(seq[:, 1, 0:ITEMS - 1], back[:, 1:], c.item_link[:, 1:ITEMS], ALU.add))
                for k in range(2):
                    do(v.tensor_copy(ends_t[:, k], seq[:, k].rearrange("p (g i) -> p i g", i=16)))
                v.sem_inc(seq_done, 1)
                v.wait_ge(carried, 32 + 16 * H)
                for k, mask in enumerate((c.to_first, c.to_last)):
                    do(v.tensor_tensor(f.rearrange("p (g e) -> p g e", e=P), mask.rearrange("p (g e) -> p g e", e=P),
                                       bc(ends[:, k, :].unsqueeze(2), [P, GROUPS, P]), ALU.add))
                    do(v.tensor_tensor(m, m, f, ALU.max))
                do(v.tensor_tensor(e, e, m, ALU.subtract))
                v.sem_inc(ready, 1)
                do(v.memset(c.scores[:, ITEMS * H:(ITEMS + 16) * H], 0.0))
                for r in range(rounds):
                    v.wait_ge(back_turned, r + 1)
                    v.tensor_copy(by_group[:, r * 4:(r + 1) * 4],
                                  c.ps[:, (r % 2) * 512:(r % 2) * 512 + 512].rearrange("p (g h i) -> p g h i", g=4, h=H)
                                  ).then_inc(back_copied, 1)
                v.wait_ge(back_copied, rounds)


SUMW = D + H


def edge_sums(c, table, weighted, name):
    nc = c.nc
    width = D if weighted else D + 2
    ring = c.rows_a[:, 0:RING * SUMW].rearrange("p (s d) -> p s d", d=SUMW)
    o = RING * SUMW
    s_buf = c.rows_a[:, o:o + 2048].rearrange("p (b i n) -> p b i n", b=4, i=BATCH)
    msg = c.rows_a[:, o + 2048:o + 2048 + 4 * BATCH * SUMW].rearrange("p (b i n) -> p b i n", b=4, i=BATCH)
    nw = SUMW if weighted else width
    with Semaphores(nc) as s:
        def sem(n):
            return s.sem(f"{name}_{n}")
        staged, gate, made, weights = sem("idx"), sem("gate"), sem("onehot"), sem("weights")
        msgs, summed, added, cleared = sem("messages"), sem("summed"), sem("added"), sem("cleared")
        landed = [sem(f"landed{u}") for u in range(RING)]
        idx = s.enter_context(nc.sbuf_tensor(f"{name}_idx", [P, RING], U32))
        with nc.Block() as block:
            @block.gpsimd
            def _(pool):
                if not weighted:
                    pool.wait_ge(cleared, 2)
                    pool.sem_inc(gate, 1)
                gather_rows(c, pool, table, ring, D, idx, staged, msgs if weighted else summed, gate, landed,
                            weighted, 2 if weighted else 1)

            @block.scalar
            def _(a):
                if weighted:
                    with a.Fori(0, BATCHES // 4) as i:
                        for q in range(4):
                            b = i * 4 + q
                            a.wait_ge(summed, b + 1)
                            a.activation(msg[:, q, :, D:SUMW],
                                         c.scores[:, bass.ds(b * BATCH * H, BATCH * H)].rearrange("p (i h) -> p i h", h=H),
                                         ACT.Copy).then_inc(weights, 1)

            @block.vector
            def _(v):
                v.sem_inc(added, 2 * BATCH)
                v.sem_inc(msgs, 2 * (RING // BATCH))
                v.memset(c.rows_b[:, 0:NT * SUMW], 0.0).then_inc(cleared, 1)
                if not weighted:
                    v.memset(ring[:, :, D:SUMW], 1.0).then_inc(cleared, 1)
                v.wait_ge(cleared, 1)

                def message(i, q, b, half):
                    lo, hi = half * BATCH // 2, (half + 1) * BATCH // 2
                    for u in range(lo, hi):
                        v.wait_ge(landed[q * BATCH + u], i * 16 + 16)
                    v.tensor_tensor(msg[:, q, lo:hi, 0:D].rearrange("p i (h k) -> p i h k", k=DK),
                                    ring[:, q * BATCH + lo:q * BATCH + hi, 0:D].rearrange("p i (h k) -> p i h k", k=DK),
                                    bc(c.scores[:, bass.ds(b * BATCH * H + lo * H, BATCH // 2 * H)]
                                       .rearrange("p (i h) -> p i h", h=H).unsqueeze(3), [P, BATCH // 2, H, DK]),
                                    ALU.mult).then_inc(msgs, 1)

                for b in range(2):
                    one_hot(c, v, s_buf, b, b).then_inc(made, 1)
                    if weighted:
                        message(0, b, b, 0)
                        message(0, b, b, 1)
                with v.Fori(0, BATCHES // 4) as i:
                    for q in range(4):
                        b, par = i * 4 + q, q % 2
                        one_hot(c, v, s_buf, b + 2, (q + 2) % 4).then_inc(made, 1)
                        tiles = load_tiles(v, c, b)
                        v.wait_ge(summed, b + 5)
                        for u in range(BATCH):
                            ps = c.ps[:, (par * BATCH + u) * 512:(par * BATCH + u) * 512 + nw]
                            to = c.rows_b[:, bass.ds(tiles[u] * SUMW, nw)]
                            v.wait_ge(added, b * BATCH + u + 2 * BATCH)
                            v.tensor_tensor(to, to, ps, ALU.add).then_inc(added, 1)
                            if weighted and u < 2:
                                message(i + (q + 2) // 4, (q + 2) % 4, b + 2, u)
                v.wait_ge(added, ITEMS + 2 * BATCH)

            @block.tensor
            def _(pe):
                pe.sem_inc(summed, 4)
                with pe.Fori(0, BATCHES // 4) as i:
                    for q in range(4):
                        b, par = i * 4 + q, q % 2
                        pe.wait_ge(made, b + 1)
                        pe.wait_ge(added, b * BATCH + BATCH)
                        if weighted:
                            pe.wait_ge(weights, b + 1)
                            pe.wait_ge(msgs, b * 2 + 2 + 2 * (RING // BATCH))
                        else:
                            for u in range(BATCH):
                                pe.wait_ge(landed[q * BATCH + u], i * 16 + 16)
                        for u in range(BATCH):
                            to = (par * BATCH + u) * 512
                            rhs = msg[:, q, u, :] if weighted else ring[:, q * BATCH + u, 0:nw]
                            mm = pe.matmul(c.ps[:, to:to + nw], s_buf[:, q, u, :], rhs, start=True, stop=True)
                        mm.then_inc(summed, 1)


def rows3(ap, tiles=NT):
    return ap[:, 0:tiles * D].rearrange("p (t d) -> p t d", d=D)


def row_bc(ap):
    return ap.rearrange("(a n) -> a n", a=1).broadcast_to([P, ap.shape[0]])


def attention_out(c, wo, name):
    nc = c.nc
    w = c.scores[:, 0:512].rearrange("p (k n) -> p k n", k=2)
    rows = c.scores[:, 512:1536].rearrange("p (b t d) -> p b t d", b=2, t=2)
    rows_t = c.scores[:, 1536:2560].rearrange("p (b n) -> p b n", b=2)
    inv = c.scores[:, 2560:2592].rearrange("p (b t h) -> p b t h", b=2, t=2)
    with Semaphores(nc) as s:
        def sem(n):
            return s.sem(f"{name}_{n}")
        loaded, staged, turned, copied = sem("loaded"), sem("staged"), sem("turned"), sem("copied")
        used, out_done, step = sem("used"), sem("out_done"), sem("step")
        with nc.Block() as block:
            @block.sync
            def _(sp):
                sp.dma_start(w, wo.rearrange("(k p) n -> p k n", p=P)).then_inc(loaded, 16)
                sp.dma_start(rows3(c.rows_a), c.h_dram.rearrange("(t p) d -> p t d", p=P)).then_inc(loaded, 16)

            @block.scalar
            def _(a):
                a.sem_inc(copied, 2)

                def body(g, parity, last):
                    a.wait_ge(turned, g + 3)
                    a.wait_ge(used, g + 1)
                    a.activation(rows_t[:, parity], c.ps[:, parity * 512:parity * 512 + 512], ACT.Copy).then_inc(copied, 1)
                groups(a, body)

            @block.tensor
            def _(pe):
                pe.sem_inc(turned, 2)
                pe.sem_inc(used, 2)
                pe.wait_ge(loaded, 32)

                def flip(g, parity):
                    pe.wait_ge(staged, g + 1)
                    pe.wait_ge(copied, g + 1)
                    turn(pe, c, rows[:, parity].rearrange("p t d -> p (t d)"), parity).then_inc(turned, 1)
                flip(0, 0)

                def body(g, parity, last):
                    if not last:
                        flip(g + 1, 1 - parity)
                    pe.wait_ge(copied, g + 3)
                    pe.wait_ge(out_done, g + 1)
                    for u in range(2):
                        for k in range(2):
                            to = (2 + parity) * 512 + u * D
                            x = rows_t[:, parity, k * 2 * P + u * P:k * 2 * P + u * P + P]
                            mm = pe.matmul(c.ps[:, to:to + D], x, w[:, k, :], start=(k == 0), stop=(k == 1))
                    mm.then_inc(used, 1)
                groups(pe, body)

            @block.vector
            def _(v):
                v.sem_inc(out_done, 2)

                def norm(g, parity):
                    sums = c.rows_b[:, bass.ds(g * 2 * SUMW, 2 * SUMW)].rearrange("p (t n) -> p t n", t=2)
                    v.tensor_scalar(inv[:, parity], sums[:, :, D:SUMW], 1e-9, None, ALU.add).then_inc(step, 1)
                    v.wait_ge(step, g * 2 + 1)
                    v.reciprocal(inv[:, parity], inv[:, parity]).then_inc(step, 1)
                    v.wait_ge(step, g * 2 + 2)
                    v.wait_ge(turned, g + 1)
                    v.tensor_tensor(rows[:, parity].rearrange("p t (h k) -> p t h k", k=DK),
                                    sums[:, :, 0:D].rearrange("p t (h k) -> p t h k", k=DK),
                                    bc(inv[:, parity].unsqueeze(3), [P, 2, H, DK]), ALU.mult).then_inc(staged, 1)
                norm(0, 0)
                v.wait_ge(loaded, 32)

                def body(g, parity, last):
                    if not last:
                        norm(g + 1, 1 - parity)
                    v.wait_ge(used, g + 3)
                    to = c.rows_a[:, bass.ds(g * 2 * D, 2 * D)]
                    v.tensor_tensor(to, to, c.ps[:, (2 + parity) * 512:(2 + parity) * 512 + 512], ALU.add).then_inc(out_done, 1)
                groups(v, body)
                v.wait_ge(out_done, GROUPS2 + 2)


def affine(c, gamma, beta, name, add_to=None):
    nc = c.nc
    gb, bb = c.scores[:, 0:D], c.scores[:, D:2 * D]
    with Semaphores(nc) as s:
        loaded, step = s.sem(f"{name}_loaded"), s.sem(f"{name}_step")
        with nc.Block() as block:
            @block.sync
            def _(sp):
                sp.dma_start(gb, row_bc(gamma)).then_inc(loaded, 16)
                sp.dma_start(bb, row_bc(beta)).then_inc(loaded, 16)

            @block.vector
            def _(v):
                do = Chain(v, step)
                v.wait_ge(loaded, 32)
                r = rows3(c.rows_a)
                do(v.tensor_tensor(r, r, bc(gb.unsqueeze(1), [P, NT, D]), ALU.mult))
                do(v.tensor_tensor(r, r, bc(bb.unsqueeze(1), [P, NT, D]), ALU.add))
                if add_to is not None:
                    do(v.tensor_tensor(rows3(add_to), rows3(add_to), r, ALU.add))


class FfnRoom:

    def __init__(self, c):
        sc = c.scores
        self.w1 = sc[:, 0:2048].rearrange("p (k n) -> p k n", k=2)
        self.w2 = sc[:, 2048:4096].rearrange("p (k n) -> p k n", k=8)
        self.rows = [sc[:, 4096 + k * 512:4608 + k * 512] for k in range(2)]
        self.rows_t = sc[:, 5120:6144].rearrange("p (b n) -> p b n", b=2)
        self.b1 = sc[:, 6144:6152]
        self.b2 = sc[:, 6152:6152 + D]
        self.hid = c.rows_b[:, 0:4096].rearrange("p (b k n) -> p b k n", b=2, k=8)


def ffn(c, room, func, target, name, load=None):
    nc = c.nc
    K2 = HID // P
    with Semaphores(nc) as s:
        def sem(n):
            return s.sem(f"{name}_{n}")
        loaded, chunk, acted, summed, out_done = sem("loaded"), sem("chunk"), sem("acted"), sem("summed"), sem("out_done")
        step, zeroed = sem("step"), sem("zeroed")
        f = Front(c, s, name, room.rows, room.rows_t, c.rows_a)
        with nc.Block() as block:
            if load:
                @block.sync
                def _(sp):
                    load(sp, loaded, zeroed)

            @block.scalar
            def _(a):
                a.sem_inc(acted, 4)
                if load:
                    a.wait_ge(loaded, 96)
                f.stage(a, 0, 0)

                def body(g, parity, last):
                    if not last:
                        f.stage(a, g + 1, 1 - parity)
                    a.wait_ge(summed, g + 1)
                    for k in range(K2):
                        a.wait_ge(chunk, g * K2 + k + 1)
                        at = (2 + k % 4) * 512
                        a.activation(room.hid[:, parity, k, :], c.ps[:, at:at + 2 * P], func,
                                     bias=room.b1[:, k:k + 1]).then_inc(acted, 1)
                groups(a, body)

            @block.tensor
            def _(pe):
                f.start_pe(pe)
                pe.sem_inc(summed, 2)
                if load:
                    pe.wait_ge(loaded, 96)
                f.turn(pe, 0, 0)

                def body(g, parity, last):
                    if not last:
                        f.turn(pe, g + 1, 1 - parity)
                    pe.wait_ge(f.copied, g + 3)
                    for n in range(K2):
                        pe.wait_ge(acted, g * K2 + n + 1)
                        at = (2 + n % 4) * 512
                        for k in range(2):
                            mm = pe.matmul(c.ps[:, at:at + 2 * P], room.w1[:, k, n * P:(n + 1) * P],
                                           room.rows_t[:, parity, k * 2 * P:(k + 1) * 2 * P], start=(k == 0), stop=(k == 1))
                        mm.then_inc(chunk, 1)
                    pe.wait_ge(out_done, g + 1)
                    for u in range(2):
                        at = (6 + parity) * 512 + u * D
                        for n in range(K2):
                            if u == 0:
                                pe.wait_ge(acted, g * K2 + n + 5)
                            mm = pe.matmul(c.ps[:, at:at + D], room.hid[:, parity, n, u * P:(u + 1) * P], room.w2[:, n, :],
                                           start=(n == 0), stop=(n == K2 - 1))
                            if u == 0 and n == 0:
                                mm.then_inc(f.used, 1)
                    mm.then_inc(summed, 1)
                groups(pe, body)

            @block.vector
            def _(v):
                do = Chain(v, step)
                f.start_vector(v)
                v.sem_inc(out_done, 2)
                if load:
                    v.memset(c.rows_c[:, FULL_ROWS // P * D:NT * D], 0.0).then_inc(zeroed, 1)
                    v.wait_ge(loaded, 96)
                f.copy(v, 0, 0)

                def body(g, parity, last):
                    if not last:
                        f.copy(v, g + 1, 1 - parity)
                    v.wait_ge(summed, g + 3)
                    v.wait_ge(f.turned, g + 3)
                    to = target[:, bass.ds(g * 2 * D, 2 * D)]
                    v.tensor_tensor(to, to, c.ps[:, (6 + parity) * 512:(7 + parity) * 512], ALU.add).then_inc(out_done, 1)
                groups(v, body)
                v.wait_ge(out_done, GROUPS2 + 2)
                t = rows3(target)
                do(v.tensor_tensor(t, t, bc(room.b2.unsqueeze(1), [P, NT, D]), ALU.add))


def load_ffn(c, room, x, w1, b1, w2, b2):
    def load(sp, loaded, zeroed):
        nc = c.nc
        sp.dma_start(room.w1, w1.rearrange("(k p) n -> p k n", p=P)).then_inc(loaded, 16)
        sp.dma_start(room.w2, w2.rearrange("(k p) n -> p k n", p=P)).then_inc(loaded, 16)
        with nc.allow_non_contiguous_dma("a bias, one number a partition"):
            sp.dma_start(room.b1, b1.rearrange("(k p) -> p k", p=P)).then_inc(loaded, 16)
        sp.dma_start(room.b2, row_bc(b2)).then_inc(loaded, 16)
        sp.wait_ge(zeroed, 1)
        rows = rows3(c.rows_c)
        sp.dma_start(rows[:, 0:FULL_ROWS // P, :], x[0:FULL_ROWS, :].rearrange("(t p) d -> p t d", p=P)).then_inc(loaded, 16)
        sp.dma_start(rows[0:LAST_ROWS, FULL_ROWS // P, :], x[FULL_ROWS:N, :]).then_inc(loaded, 16)
    return load


def route_all(c, room, wr, br, w1, b1, w2, b2):
    nc = c.nc
    NE, HE = 8, 512
    capacity = float(-(-int(N * 1.25) // NE)) if (N * 1.25) == int(N * 1.25) else float(-(-(N * 5) // (NE * 4)))
    o = [0]

    def take(n, dt=F32):
        a = c.rows_b[:, o[0]:o[0] + n]
        o[0] += n
        return a if dt == F32 else a.bitcast(dt)
    total, wr_sb, br_sb, ones = take(D), take(2 * NE).rearrange("p (k n) -> p k n", k=2), take(NE), take(1)
    mean_t, wide = take(2), take(2 * P).rearrange("p (k n) -> p k n", k=2)
    lg, t8, m8, p8, one = take(NE), take(NE), take(NE), take(NE), take(1)
    best, best_i, best_f = take(8), take(8, U32), take(8)
    weight = take(2)
    row_no = take(4)
    idx1 = take(4).rearrange("p (j k) -> p j k", j=2)
    idx2 = take(8).rearrange("p (j k) -> p j k", j=2)
    idx1u, idx2u = take(4, U32).rearrange("p (j k) -> p j k", j=2), take(8, U32).rearrange("p (j k) -> p j k", j=2)
    b2_rows = take(2 * D).rearrange("p (j n) -> p j n", j=2)
    with Semaphores(nc) as s:
        def sem(n):
            return s.sem(f"route_{n}")
        loaded, step, total_ready, mean_ps, wide_ready = sem("loaded"), sem("step"), sem("total"), sem("mean"), sem("wide")
        logits_ps, ask, exped, idx_ready, landed, rowno = sem("logits"), sem("ask"), sem("exped"), sem("idx"), sem("landed"), sem("rowno")
        with nc.Block() as block:
            @block.sync
            def _(sp):
                sp.dma_start(wr_sb, wr.rearrange("(k p) n -> p k n", p=P)).then_inc(loaded, 16)
                sp.dma_start(br_sb, row_bc(br)).then_inc(loaded, 16)

            @block.gpsimd
            def _(pool):
                pool.iota(row_no, [[P, 4]], base=0, channel_multiplier=1, allow_small_or_imprecise_dtypes=True).then_inc(rowno, 1)
                pool.wait_ge(idx_ready, 1)
                w1_rows, w2_rows = w1.rearrange("e d n -> (e d) n"), w2.rearrange("e n d -> (e n) d")
                b1_rows = b1.rearrange("e (n a) -> (e n) a", a=1)

                def fetch(to, table, idx):
                    pool.indirect_dma_start(to, None, table, bass.IndirectOffsetOnAxis(ap=idx, axis=0)).then_inc(landed, 16)
                for j in range(2):
                    for k in range(2):
                        fetch(room.w1[:, k, j * HE:(j + 1) * HE], w1_rows, idx1u[:, j, k:k + 1])
                    for k in range(4):
                        fetch(room.w2[:, j * 4 + k, :], w2_rows, idx2u[:, j, k:k + 1])
                        fetch(room.b1[:, j * 4 + k:j * 4 + k + 1], b1_rows, idx2u[:, j, k:k + 1])
                    fetch(b2_rows[:, j, :], b2, best_i[:, j:j + 1])

            @block.tensor
            def _(pe):
                pe.wait_ge(total_ready, 1)
                for k in range(2):
                    mm = pe.matmul(c.ps[:, k:k + 1], total[:, k * P:(k + 1) * P], ones, start=True, stop=True)
                mm.then_inc(mean_ps, 1)
                pe.wait_ge(wide_ready, 1)
                pe.wait_ge(loaded, 32)
                for k in range(2):
                    mm = pe.matmul(c.ps[:, 512:512 + NE], wide[:, k, :], wr_sb[:, k, :], start=(k == 0), stop=(k == 1))
                mm.then_inc(logits_ps, 1)

            @block.scalar
            def _(a):
                for n, x in enumerate((lg, p8, weight[:, 1:2])):
                    a.wait_ge(ask, n + 1)
                    a.activation(x, x, ACT.Exp).then_inc(exped, 1)

            @block.vector
            def _(v):
                do = Chain(v, step)
                do(v.memset(ones, 1.0))
                do(v.tensor_reduce(total, c.rows_a[:, 0:FULL_ROWS // P * D].rearrange("p (t d) -> p d t", d=D), AX.X, ALU.add))
                last = FULL_ROWS // P * D
                do(v.tensor_tensor(total[0:LAST_ROWS], total[0:LAST_ROWS], c.rows_a[0:LAST_ROWS, last:last + D], ALU.add))
                v.sem_inc(total_ready, 1)
                v.wait_ge(mean_ps, 1)
                do(v.tensor_scalar(mean_t, c.ps[:, 0:2], 1.0 / N, None, ALU.mult))
                do(v.tensor_copy(wide, bc(mean_t.unsqueeze(2), [P, 2, P])))
                v.sem_inc(wide_ready, 1)
                v.wait_ge(logits_ps, 1)
                do(v.tensor_tensor(lg, c.ps[:, 512:512 + NE], br_sb, ALU.add))

                def softmax(x, n):
                    do(v.tensor_reduce(one, x, AX.X, ALU.max))
                    do(v.tensor_scalar(x, x, one, None, ALU.subtract))
                    v.sem_inc(ask, 1)
                    v.wait_ge(exped, n)
                    do(v.tensor_reduce(one, x, AX.X, ALU.add))
                    do(v.reciprocal(one, one))
                    do(v.tensor_scalar(x, x, one, None, ALU.mult))
                softmax(lg, 1)
                do(v.tensor_scalar(t8, lg, float(N), capacity, ALU.mult, ALU.max))
                do(v.reciprocal(t8, t8))
                do(v.tensor_scalar(t8, t8, capacity, None, ALU.mult))
                do(v.tensor_tensor(p8, lg, t8, ALU.mult))
                softmax(p8, 2)
                do(v.max(best, p8))
                do(v.max_index(best_i, best, p8))
                do(v.tensor_copy(best_f, best_i))
                do(v.tensor_tensor(weight[:, 1:2], best[:, 1:2], best[:, 0:1], ALU.subtract))
                v.sem_inc(ask, 1)
                v.wait_ge(rowno, 1)
                for j in range(2):
                    do(v.tensor_scalar(one, best_f[:, j:j + 1], float(D), None, ALU.mult))
                    do(v.tensor_scalar(idx1[:, j], row_no[:, 0:2], one, None, ALU.add))
                    do(v.tensor_scalar(one, best_f[:, j:j + 1], float(HE), None, ALU.mult))
                    do(v.tensor_scalar(idx2[:, j], row_no, one, None, ALU.add))
                do(v.tensor_copy(idx1u, idx1))
                do(v.tensor_copy(idx2u, idx2))
                v.sem_inc(idx_ready, 1)
                v.wait_ge(exped, 3)
                do(v.tensor_scalar(one, weight[:, 1:2], 1.0, None, ALU.add))
                do(v.reciprocal(weight[:, 0:1], one))
                do(v.tensor_tensor(weight[:, 1:2], weight[:, 1:2], weight[:, 0:1], ALU.mult))
                v.wait_ge(landed, 22 * 16)
                for j in range(2):
                    r = room.w2[:, j * 4:j * 4 + 4, :]
                    do(v.tensor_scalar(r, r, weight[:, j:j + 1], None, ALU.mult))
                    do(v.tensor_scalar(b2_rows[:, j], b2_rows[:, j], weight[:, j:j + 1], None, ALU.mult))
                do(v.tensor_tensor(room.b2, b2_rows[:, 0], b2_rows[:, 1], ALU.add))


def sage_products(c, w_self, w_neigh):
    nc = c.nc
    w = c.scores[:, 0:1024].rearrange("p (k n) -> p k n", k=2)
    rows = [c.scores[:, 1024 + k * 512:1536 + k * 512] for k in range(2)]
    rows_t = c.scores[:, 2048:3072].rearrange("p (b n) -> p b n", b=2)
    neigh = c.scores[:, 3072:4096].rearrange("p (b n) -> p b n", b=4)
    left = c.scores[:, 4096:5120].rearrange("p (b n) -> p b n", b=4)
    top = c.scores[:, 5120:5128]
    NEG = -3.0e38
    with Semaphores(nc) as s:
        def sem(n):
            return s.sem(f"sage_{n}")
        loaded, out_done, ready, step, neigh_out = sem("loaded"), sem("out_done"), sem("ready"), sem("step"), sem("neigh_out")
        stored, buf_free, gate = [sem(f"stored{u}") for u in range(4)], sem("buf_free"), sem("gate")
        f = Front(c, s, "sage", rows, rows_t, c.rows_a)
        with nc.Block() as block:
            @block.sync
            def _(sp):
                sp.dma_start(w[:, :, 0:D], w_self.rearrange("(k p) n -> p k n", p=P)).then_inc(loaded, 16)
                sp.dma_start(w[:, :, D:2 * D], w_neigh.rearrange("(k p) n -> p k n", p=P)).then_inc(loaded, 16)

                def body(g, parity, last):
                    for u in range(2):
                        b = 2 * parity + u
                        sp.wait_ge(ready, g * 2 + u + 1)
                        sp.dma_start(c.k_dram[bass.ds(g * 2 * P + u * P, P), :], left[:, b, :]).then_inc(stored[b], 16)
                    for u in range(2):
                        sp.wait_ge(stored[2 * parity + u], (g - parity) * 8 + 16)
                        sp.sem_inc(buf_free, 1)
                groups(sp, body)

            @block.scalar
            def _(a):
                a.sem_inc(neigh_out, 4)
                f.stage(a, 0, 0)

                def body(g, parity, last):
                    if not last:
                        f.stage(a, g + 1, 1 - parity)
                    a.wait_ge(f.used, g + 3)
                    for u in range(2):
                        b = 2 * parity + u
                        a.wait_ge(buf_free, g * 2 + u + 1)
                        at = (4 + parity) * 512 + u * D
                        a.activation(neigh[:, b, :], c.ps[:, at:at + D], ACT.Copy).then_inc(neigh_out, 1)
                groups(a, body)

            @block.tensor
            def _(pe):
                f.start_pe(pe)
                pe.wait_ge(loaded, 32)
                f.turn(pe, 0, 0)

                def body(g, parity, last):
                    if not last:
                        f.turn(pe, g + 1, 1 - parity)
                    pe.wait_ge(f.copied, g + 3)
                    pe.wait_ge(out_done, g + 1)
                    pe.wait_ge(neigh_out, g * 2 + 2)
                    for u in range(2):
                        for half in range(2):
                            at = (2 + 2 * half + parity) * 512 + u * D
                            for k in range(2):
                                x = rows_t[:, parity, k * 2 * P + u * P:k * 2 * P + u * P + P]
                                mm = pe.matmul(c.ps[:, at:at + D], x, w[:, k, half * D:(half + 1) * D],
                                               start=(k == 0), stop=(k == 1))
                    mm.then_inc(f.used, 1)
                groups(pe, body)

            @block.vector
            def _(v):
                f.start_vector(v)
                v.sem_inc(out_done, 2)
                v.sem_inc(buf_free, 4)
                f.copy(v, 0, 0)
                STEPS = 8

                def body(g, parity, last):
                    if not last:
                        f.copy(v, g + 1, 1 - parity)
                    v.wait_ge(f.used, g + 3)
                    to = c.rows_c[:, bass.ds(g * 2 * D, 2 * D)]
                    v.tensor_tensor(to, to, c.ps[:, (2 + parity) * 512:(3 + parity) * 512], ALU.add).then_inc(out_done, 1)
                    for u in range(2):
                        b = 2 * parity + u
                        v.wait_ge(neigh_out, g * 2 + u + 5)
                        for r in range(4):
                            n = g * 2 * STEPS + u * STEPS + 2 * r
                            src = neigh[:, b, :] if r == 0 else left[:, b, :]
                            v.sem_inc(gate, 1)
                            v.max(top, src).then_inc(step, 1)
                            v.wait_ge(step, n + 1)
                            v.sem_inc(gate, 1)
                            v.match_replace(left[:, b, :], top, src, NEG).then_inc(step, 1)
                            v.wait_ge(step, n + 2)
                        v.scalar_tensor_tensor(left[:, b, :], left[:, b, :], NEG, neigh[:, b, :], ALU.is_equal,
                                               ALU.mult).then_inc(ready, 1)
                groups(v, body)
                v.wait_ge(ready, NT)


def add_neighbours(c):
    nc = c.nc
    sums = c.rows_b[:, 0:NT * SUMW].rearrange("p (t n) -> p t n", t=NT)
    inv = c.small[:, 0:NT]
    with Semaphores(nc) as s:
        step = s.sem("neigh_step")
        with nc.Block() as block:
            @block.vector
            def _(v):
                do = Chain(v, step)
                do(v.tensor_scalar(inv, sums[:, :, D], 1.0, None, ALU.max))
                do(v.reciprocal(inv, inv))
                do(v.tensor_tensor(sums[:, :, 0:D], sums[:, :, 0:D], bc(inv.unsqueeze(2), [P, NT, D]), ALU.mult))
                do(v.tensor_tensor(rows3(c.rows_c), rows3(c.rows_c), sums[:, :, 0:D], ALU.add))


def token_routes(c, gates, wr, br, b2):
    nc = c.nc
    NE = 8
    wr_sb = c.scores[:, 0:16].rearrange("p (k n) -> p k n", k=2)
    br_sb = c.scores[:, 16:24]
    lg = c.scores[:, 24:56].rearrange("p (b t n) -> p b t n", b=2, t=2)
    mx = c.scores[:, 56:88].rearrange("p (b t n) -> p b t n", b=2, t=2)
    mi = c.scores[:, 88:120].bitcast(U32).rearrange("p (b t n) -> p b t n", b=2, t=2)
    rows = [c.scores[:, 128 + k * 512:640 + k * 512] for k in range(2)]
    rows_t = c.scores[:, 1152:2176].rearrange("p (b n) -> p b n", b=2)
    iota8 = c.scores[:, 2176:2184]
    val = c.scores[:, 2184:2184 + 2 * NT].rearrange("p (t n) -> p t n", n=2)
    sel = c.scores[:, 2284:2284 + 2 * NT].rearrange("p (t n) -> p t n", n=2)
    w0, w1 = c.small[:, 0:NT], c.small[:, NT:2 * NT]
    pick = c.scores[:, 2384:2384 + NT * NE].rearrange("p (t n) -> p t n", n=NE)
    b2_sb = c.scores[0:NE, 2784:2784 + D]
    g_buf = c.scores[:, 3040:3072].rearrange("p (b t n) -> p b t n", b=2, t=2)
    g_t = c.scores[0:NE, 3072:3072 + 512].rearrange("p (b n) -> p b n", b=2)
    g3 = gates.rearrange("p (t n) -> p t n", n=NE)
    with Semaphores(nc) as s:
        def sem(n):
            return s.sem(f"tok_{n}")
        loaded, iotas, lg_done, step, kept = sem("loaded"), sem("iotas"), sem("lg_done"), sem("step"), sem("kept")
        gate = sem("gate")
        s1, ask, exped = sem("s1"), sem("ask"), sem("exped")
        gated, g_staged, g_turned, g_copied, b_summed, b_added = (sem(n) for n in ("gated", "gs", "gt", "gc", "bs", "ba"))
        f = Front(c, s, "tok", rows, rows_t, c.rows_a)
        with nc.Block() as block:
            @block.sync
            def _(sp):
                sp.dma_start(wr_sb, wr.rearrange("(k p) n -> p k n", p=P)).then_inc(loaded, 16)
                sp.dma_start(br_sb, row_bc(br)).then_inc(loaded, 16)
                sp.dma_start(b2_sb, b2).then_inc(loaded, 16)

            @block.gpsimd
            def _(pool):
                pool.iota(iota8, [[1, NE]], base=0, channel_multiplier=0, allow_small_or_imprecise_dtypes=True).then_inc(iotas, 1)

            @block.scalar
            def _(a):
                groups(a, lambda g, parity, last: f.stage(a, g, parity))
                a.wait_ge(ask, 1)
                a.activation(w1, w1, ACT.Exp).then_inc(exped, 1)
                a.wait_ge(gated, 1)

                def stage(g, parity, last):
                    a.wait_ge(g_turned, g + 1)
                    a.activation(g_buf[:, parity], gates[:, bass.ds(g * 2 * NE, 2 * NE)].rearrange("p (t n) -> p t n", n=NE),
                                 ACT.Copy).then_inc(g_staged, 1)
                groups(a, stage)

            @block.tensor
            def _(pe):
                f.start_pe(pe)
                pe.sem_inc(g_turned, 2)
                pe.sem_inc(b_summed, 2)
                pe.wait_ge(loaded, 48)
                f.turn(pe, 0, 0)

                def body(g, parity, last):
                    if not last:
                        f.turn(pe, g + 1, 1 - parity)
                    pe.wait_ge(f.copied, g + 3)
                    pe.wait_ge(lg_done, g + 1)
                    for u in range(2):
                        at = (2 + parity) * 512 + u * NE
                        for k in range(2):
                            x = rows_t[:, parity, k * 2 * P + u * P:k * 2 * P + u * P + P]
                            mm = pe.matmul(c.ps[:, at:at + NE], x, wr_sb[:, k, :], start=(k == 0), stop=(k == 1))
                    mm.then_inc(f.used, 1)
                groups(pe, body)

                def bias(g, parity, last):
                    pe.wait_ge(g_staged, g + 1)
                    pe.wait_ge(g_copied, g + 1)
                    for u in range(2):
                        at = (4 + parity) * 512 + u * P
                        mm = pe.transpose(c.ps[0:NE, at:at + P], g_buf[:, parity, u, :], c.ident[:, :])
                    mm.then_inc(g_turned, 1)
                    pe.wait_ge(g_copied, g + 3)
                    pe.wait_ge(b_added, g + 1)
                    for u in range(2):
                        at = (6 + parity) * 512 + u * D
                        mm = pe.matmul(c.ps[:, at:at + D], g_t[:, parity, u * P:(u + 1) * P], b2_sb, start=True, stop=True)
                    mm.then_inc(b_summed, 1)
                groups(pe, bias)

            @block.vector
            def _(v):
                do = Chain(v, step)
                f.start_vector(v)
                v.sem_inc(lg_done, 2)
                v.sem_inc(g_copied, 2)
                v.sem_inc(b_added, 2)
                v.wait_ge(loaded, 48)
                v.wait_ge(iotas, 1)
                f.copy(v, 0, 0)
                S1 = 6

                def body(g, parity, last):
                    if not last:
                        f.copy(v, g + 1, 1 - parity)
                    v.wait_ge(f.used, g + 3)
                    at = (2 + parity) * 512
                    v.tensor_tensor(lg[:, parity], c.ps[:, at:at + 2 * NE].rearrange("p (t n) -> p t n", t=2),
                                    bc(br_sb.unsqueeze(1), [P, 2, NE]), ALU.add).then_inc(lg_done, 1)
                    v.wait_ge(lg_done, g + 3)
                    v.sem_inc(gate, 1)
                    for u in range(2):
                        v.max(mx[:, parity, u, :], lg[:, parity, u, :]).then_inc(s1, 1)
                    v.wait_ge(s1, g * S1 + 2)
                    v.sem_inc(gate, 1)
                    for u in range(2):
                        v.max_index(mi[:, parity, u, :], mx[:, parity, u, :], lg[:, parity, u, :]).then_inc(s1, 1)
                    v.wait_ge(s1, g * S1 + 4)
                    v.tensor_copy(val[:, bass.ds(g * 2, 2), :], mx[:, parity, :, 0:2]).then_inc(s1, 1)
                    v.tensor_copy(sel[:, bass.ds(g * 2, 2), :], mi[:, parity, :, 0:2]).then_inc(s1, 1)
                groups(v, body)
                v.wait_ge(s1, GROUPS2 * S1)
                do(v.tensor_tensor(w1, val[:, :, 1], val[:, :, 0], ALU.subtract))
                v.sem_inc(ask, 1)
                v.wait_ge(exped, 1)
                do(v.tensor_scalar(w0, w1, 1.0, None, ALU.add))
                do(v.reciprocal(w0, w0))
                do(v.tensor_tensor(w1, w1, w0, ALU.mult))
                wide8 = bc(iota8.unsqueeze(1), [P, NT, NE])
                for j, (w, to) in enumerate(((w0, g3), (w1, pick))):
                    do(v.tensor_tensor(to, wide8, bc(sel[:, :, j:j + 1], [P, NT, NE]), ALU.is_equal))
                    do(v.tensor_tensor(to, to, bc(w.unsqueeze(2), [P, NT, NE]), ALU.mult))
                do(v.tensor_tensor(g3, g3, pick, ALU.add))
                v.sem_inc(gated, 1)

                def bias(g, parity, last):
                    v.wait_ge(g_turned, g + 3)
                    v.wait_ge(b_summed, g + 1)
                    at = (4 + parity) * 512
                    v.tensor_copy(g_t[:, parity, :], c.ps[0:NE, at:at + 2 * P]).then_inc(g_copied, 1)
                    v.wait_ge(b_summed, g + 3)
                    to = c.rows_c[:, bass.ds(g * 2 * D, 2 * D)]
                    v.tensor_tensor(to, to, c.ps[:, (6 + parity) * 512:(7 + parity) * 512], ALU.add).then_inc(b_added, 1)
                groups(v, bias)
                v.wait_ge(b_added, GROUPS2 + 2)


def token_experts(c, gates, w1, b1, w2, out):
    nc = c.nc
    NE, HE = 8, 512
    K2 = HE // P
    w1_sb = c.rows_b[:, 0:NE * 2 * HE].rearrange("p (e k n) -> p e k n", e=NE, k=2)
    low = 5
    w2_low = c.rows_b[:, NE * 2 * HE:NE * 2 * HE + low * K2 * D].rearrange("p (e k n) -> p e k n", e=low, k=K2)
    w2_high = c.scores[:, 0:(NE - low) * K2 * D].rearrange("p (e k n) -> p e k n", e=NE - low, k=K2)
    hid = c.scores[:, 3072:5120].rearrange("p (b k n) -> p b k n", b=2, k=K2)
    rows_t = c.scores[:, 5120:6144].rearrange("p (b n) -> p b n", b=2)
    b1_sb = c.scores[:, 6144:6144 + NE * K2].rearrange("p (e k) -> p e k", e=NE)
    rows = [c.rel_dst[:, 0:512], c.src_idx[:, 0:512].bitcast(F32)]

    def w2_of(e):
        return w2_low[:, e] if e < low else w2_high[:, e - low]
    with Semaphores(nc) as s:
        def sem(n):
            return s.sem(f"moe_{n}")
        loaded, chunk, acted, summed, added, written = (sem(n) for n in ("loaded", "chunk", "acted", "summed", "added", "written"))
        f = Front(c, s, "moe", rows, rows_t, c.rows_a)
        with nc.Block() as block:
            @block.sync
            def _(sp):
                sp.dma_start(w1_sb, w1.rearrange("e (k p) n -> p e k n", p=P)).then_inc(loaded, 16)
                for e in range(NE):
                    sp.dma_start(w2_of(e), w2[e].rearrange("(k p) n -> p k n", p=P)).then_inc(loaded, 16)
                with nc.allow_non_contiguous_dma("biases, one number a partition"):
                    for e in range(NE):
                        sp.dma_start(b1_sb[:, e], b1[e].rearrange("(k p) -> p k", p=P)).then_inc(loaded, 16)

                def body(g, parity, last):
                    sp.wait_ge(added, g * 2 * NE + 2 * NE + 4)
                    for u in range(2):
                        if last and u == 1:
                            continue
                        n = LAST_ROWS if last else P
                        src = c.rows_c[0:n, bass.ds(g * 2 * D + u * D, D)]
                        sp.dma_start(out[bass.ds(g * 2 * P + u * P, n), :], src).then_inc(written, 16)
                groups(sp, body)
                sp.wait_ge(written, 16 * NODE_TILES)

            @block.scalar
            def _(a):
                a.sem_inc(acted, 4)
                f.stage(a, 0, 0)
                a.wait_ge(loaded, 16 * (1 + 2 * NE))

                def body(g, parity, last):
                    if not last:
                        f.stage(a, g + 1, 1 - parity)
                    for e in range(NE):
                        a.wait_ge(summed, g * NE + e + 1)
                        for k in range(K2):
                            a.wait_ge(chunk, g * NE * K2 + e * K2 + k + 1)
                            at = (2 + k) * 512
                            a.activation(hid[:, e % 2, k, :], c.ps[:, at:at + 2 * P], ACT.Gelu,
                                         bias=b1_sb[:, e, k:k + 1]).then_inc(acted, 1)
                groups(a, body)

            @block.tensor
            def _(pe):
                f.start_pe(pe)
                pe.sem_inc(summed, 2)
                pe.wait_ge(loaded, 16 * (1 + 2 * NE))
                f.turn(pe, 0, 0)

                def up(g, e, parity):
                    for n in range(K2):
                        pe.wait_ge(acted, g * NE * K2 + e * K2 + n + 1)
                        at = (2 + n) * 512
                        for k in range(2):
                            mm = pe.matmul(c.ps[:, at:at + 2 * P], w1_sb[:, e, k, n * P:(n + 1) * P],
                                           rows_t[:, parity, k * 2 * P:(k + 1) * 2 * P], start=(k == 0), stop=(k == 1))
                        mm.then_inc(chunk, 1)

                def down(g, e):
                    pe.wait_ge(added, g * 2 * NE + e * 2 + 2)
                    for u in range(2):
                        at = (6 + e % 2) * 512 + u * D
                        for n in range(K2):
                            if u == 0:
                                pe.wait_ge(acted, g * NE * K2 + e * K2 + n + 5)
                            mm = pe.matmul(c.ps[:, at:at + D], hid[:, e % 2, n, u * P:(u + 1) * P], w2_of(e)[:, n, :],
                                           start=(n == 0), stop=(n == K2 - 1))
                    mm.then_inc(summed, 1)

                def body(g, parity, last):
                    if not last:
                        f.turn(pe, g + 1, 1 - parity)
                    pe.wait_ge(f.copied, g + 3)
                    up(g, 0, parity)
                    for e in range(NE):
                        if e + 1 < NE:
                            up(g, e + 1, parity)
                        if e == NE - 1:
                            pe.sem_inc(f.used, 1)
                        down(g, e)
                groups(pe, body)

            @block.vector
            def _(v):
                f.start_vector(v)
                v.sem_inc(added, 4)
                f.copy(v, 0, 0)

                def body(g, parity, last):
                    for e in range(NE):
                        if e == 1 and not last:
                            f.copy(v, g + 1, 1 - parity)
                        v.wait_ge(summed, g * NE + e + 3)
                        for u in range(2):
                            to = c.rows_c[:, bass.ds(g * 2 * D + u * D, D)]
                            at = (6 + e % 2) * 512 + u * D
                            v.wait_ge(added, g * 2 * NE + e * 2 + u + 3)
                            v.scalar_tensor_tensor(to, c.ps[:, at:at + D], gates[:, bass.ds(g * 2 * NE + u * NE + e, 1)],
                                                   to, ALU.mult, ALU.add).then_inc(added, 1)
                groups(v, body)


def build(nc, x, src, dst, L0_gnn_Wq, L0_gnn_Wk, L0_gnn_Wv, L0_gnn_Wo, L0_gnn_ln_g, L0_gnn_ln_b, L0_gnn_w1, L0_gnn_b1,
          L0_gnn_w2, L0_gnn_b2, L0_ffn_Wr, L0_ffn_br, L0_ffn_W1, L0_ffn_b1, L0_ffn_W2, L0_ffn_b2, L0_ffn_gamma,
          L0_ffn_beta, L1_gnn_W_self, L1_gnn_W_neigh, L1_ffn_gamma, L1_ffn_beta, L1_ffn_Wr, L1_ffn_br, L1_ffn_W1,
          L1_ffn_b1, L1_ffn_W2, L1_ffn_b2, out, probe=None):
    with ExitStack() as ctx:
        c = Core(nc, ctx)
        say = probe or (lambda c, what: None)
        load_and_constants(c, x)
        item_tables(c, src, dst)
        say(c, "tables")
        layer_norm(c, c.rows_a, c.rows_a, "ln_in")
        say(c, "ln_in")
        segment_masks(c)
        for l in range(L0_gnn_Wq.shape[0]):
            qkv(c, L0_gnn_Wq[l], L0_gnn_Wk[l], L0_gnn_Wv[l], f"qkv{l}")
            say(c, f"qkv{l}")
            edge_scores(c, f"score{l}")
            say(c, f"score{l}")
            segment_softmax(c, f"soft{l}")
            say(c, f"soft{l}")
            edge_sums(c, c.v_dram[:, :], True, f"sum{l}")
            say(c, f"sum{l}")
            attention_out(c, L0_gnn_Wo[l], f"out{l}")
            layer_norm(c, c.rows_a, c.rows_a, f"ln_l{l}")
            affine(c, L0_gnn_ln_g[l], L0_gnn_ln_b[l], f"aff{l}")
            say(c, f"layer{l}")
        room = FfnRoom(c)
        ffn(c, room, ACT.Relu, c.rows_c, "mlp", load_ffn(c, room, x, L0_gnn_w1, L0_gnn_b1, L0_gnn_w2, L0_gnn_b2))
        say(c, "x1")
        layer_norm(c, c.rows_c, c.rows_a, "ln_x1")
        route_all(c, room, L0_ffn_Wr, L0_ffn_br, L0_ffn_W1, L0_ffn_b1, L0_ffn_W2, L0_ffn_b2)
        say(c, "route")
        ffn(c, room, ACT.Gelu, c.rows_a, "moe_all")
        layer_norm(c, c.rows_a, c.rows_a, "ln_ffn")
        affine(c, L0_ffn_gamma, L0_ffn_beta, "aff_ffn", c.rows_c)
        say(c, "x2")
        layer_norm(c, c.rows_c, c.rows_a, "ln_x2")
        sage_products(c, L1_gnn_W_self, L1_gnn_W_neigh)
        edge_sums(c, c.k_dram[:, :], False, "sage_sum")
        add_neighbours(c)
        say(c, "x3")
        layer_norm(c, c.rows_c, c.rows_a, "ln_x3")
        layer_norm(c, c.rows_a, c.rows_a, "ln_tok")
        affine(c, L1_ffn_gamma, L1_ffn_beta, "aff_tok")
        gates = ctx.enter_context(nc.sbuf_tensor("gates", [P, NT * 8], F32))
        token_routes(c, gates[:, :], L1_ffn_Wr, L1_ffn_br, L1_ffn_b2)
        say(c, "gates")
        token_experts(c, gates[:, :], L1_ffn_W1, L1_ffn_b1, L1_ffn_W2, out)


_INS = ['x', 'src', 'dst', 'L0_gnn_Wq', 'L0_gnn_Wk', 'L0_gnn_Wv', 'L0_gnn_Wo', 'L0_gnn_ln_g', 'L0_gnn_ln_b',
        'L0_gnn_w1', 'L0_gnn_b1', 'L0_gnn_w2', 'L0_gnn_b2', 'L0_ffn_Wr', 'L0_ffn_br', 'L0_ffn_W1', 'L0_ffn_b1',
        'L0_ffn_W2', 'L0_ffn_b2', 'L0_ffn_gamma', 'L0_ffn_beta', 'L1_gnn_W_self', 'L1_gnn_W_neigh', 'L1_ffn_gamma',
        'L1_ffn_beta', 'L1_ffn_Wr', 'L1_ffn_br', 'L1_ffn_W1', 'L1_ffn_b1', 'L1_ffn_W2', 'L1_ffn_b2']
_OUTS = [((N, D), 'float32')]


def kernel(**inputs):
    import numpy as _np
    import concourse.bacc as _bacc
    from concourse import mybir as _mybir
    from concourse.bass_utils import run_bass_kernel_spmd as _run

    nc = _bacc.Bacc("TRN2", target_bir_lowering=False, num_devices=1)
    arrays, args = {}, []
    for name in _INS:
        a = _np.ascontiguousarray(inputs[name])
        arrays[f"in_{name}_dram"] = a
        args.append(nc.dram_tensor(f"in_{name}_dram", a.shape, _mybir.dt.from_np(a.dtype), kind="ExternalInput").ap())
    for i, (shape, dtype) in enumerate(_OUTS):
        dt = _mybir.dt.from_np(_np.dtype(dtype))
        args.append(nc.dram_tensor(f"out_{i}_dram", shape, dt, kind="ExternalOutput").ap())
    build(nc, *args)
    r = _run(nc, [arrays], core_ids=[0])
    return r.results[0]["out_0_dram"]
```

```python
import concourse.bass as bass
from concourse import mybir
from contextlib import ExitStack

F32 = mybir.dt.float32
BF16 = mybir.dt.bfloat16
I32 = mybir.dt.int32
U32 = mybir.dt.uint32
ALU = mybir.AluOpType
ACT = mybir.ActivationFunctionType
AX = mybir.AxisListType

P = 128
N, D, E = 6250, 256, 100000
H, DK = 8, 32
NODE_TILES = -(-N // P)
NT = NODE_TILES + 1
FULL_ROWS = (N // P) * P
LAST_ROWS = N - FULL_ROWS
EDGE_TILES = -(-E // P)
EC = -(-EDGE_TILES // P)
ITEMS = -(-(EDGE_TILES + NODE_TILES - 1) // 16) * 16
IC = -(-(ITEMS + 16) // P)
BATCH = 4
BATCHES = ITEMS // BATCH
RING = 16
GROUPS = ITEMS // 16
GROUPS2 = NT // 2
BIG = 1e30
TILE_BITS = 6
PAD_DST = 60000
HID = 1024
LN_EPS = 1e-5
NE, HE = 8, 512
SLOT_TILES = (2 * N + NE * (P - 1)) // P
SLOT_TILES += -SLOT_TILES % 2


def bc(ap, shape):
    return ap.broadcast_to(shape)


class Core:

    def __init__(self, nc, ctx):
        def sb(name, shape, dt=F32):
            return ctx.enter_context(nc.sbuf_tensor(name, shape, dt))

        self.nc = nc
        self.rows_a = sb("rows_a", [P, NT * D])
        self.rows_b = sb("rows_b", [P, GROUPS * P * 2])
        self.rows_c = sb("rows_c", [P, GROUPS * P * 2])
        self.scores = sb("scores", [P, (ITEMS + 16) * H])
        self.ident = sb("ident", [P, P])
        self.iota_n = sb("iota_n", [P, P])
        self.rel_dst = sb("rel_dst", [P, IC * P])
        self.src_idx = sb("src_idx", [P, IC * P], U32)
        self.item_tile = sb("item_tile", [1, IC * P], I32)
        self.batch_tiles = sb("batch_tiles", [1, IC * P // BATCH], I32)
        self.stats = sb("stats", [P, NT * 6])
        self.mean = sb("mean", [P, NT])
        self.rstd = sb("rstd", [P, NT])
        self.nbias = sb("nbias", [P, NT])
        self.small = sb("small", [P, 4 * NT])
        self.eps_col = sb("eps_col", [P, 1])
        self.iota_p = sb("iota_p", [P, 1])
        self.slots = sb("slots", [P, 2 * NT], U32)
        self.slot_expert = sb("slot_expert", [1, SLOT_TILES], I32)
        self.ps = ctx.enter_context(nc.psum_tensor("ps", [P, 8 * 512], F32))
        self.h_dram = nc.dram_tensor("h_scratch", [NT * P, D], F32, kind="Internal").ap()
        self.k_dram = nc.dram_tensor("k_scratch", [NT * P, D], F32, kind="Internal").ap()
        self.v_dram = nc.dram_tensor("v_scratch", [NT * P, D], F32, kind="Internal").ap()
        self.sid_dram = nc.dram_tensor("sid_scratch", [IC * P, P], F32, kind="Internal").ap()
        self.dstp_dram = nc.dram_tensor("dst_scratch", [EDGE_TILES, P], I32, kind="Internal").ap()
        self.srcp_dram = nc.dram_tensor("src_scratch", [EDGE_TILES, P], I32, kind="Internal").ap()
        self.tile_dram = nc.dram_tensor("tile_scratch", [IC * P], I32, kind="Internal").ap()
        self.edge_sid_dram = nc.dram_tensor("edge_sid_scratch", [2, IC * P], F32, kind="Internal").ap()
        self.ends_dram = nc.dram_tensor("ends_scratch", [16, H, 2, GROUPS], F32, kind="Internal").ap()
        self.slot_in = nc.dram_tensor("slot_in", [SLOT_TILES * P, D], F32, kind="Internal").ap()
        self.slot_out = nc.dram_tensor("slot_out", [SLOT_TILES * P, D], F32, kind="Internal").ap()
        self.carry_dram = nc.dram_tensor("carry_scratch", [16, H, 2, GROUPS], F32, kind="Internal").ap()


class Semaphores(ExitStack):

    def __init__(self, nc):
        super().__init__()
        self.nc, self.all = nc, []

    def sem(self, name):
        one = self.nc.alloc_semaphore(name)
        self.all.append(one)
        return one

    def __exit__(self, *error):
        if not error[0]:
            self.nc.clear_and_free_semaphores(self.all)
            self.nc.all_engine_barrier()
        return super().__exit__(*error)


class Chain:

    def __init__(self, eng, sem):
        self.eng, self.sem, self.n = eng, sem, 0

    def __call__(self, ins):
        self.n += 1
        ins.then_inc(self.sem, 1)
        self.eng.wait_ge(self.sem, self.n)


def load_and_constants(c, x):
    nc = c.nc
    with Semaphores(nc) as s:
        zeroed, loaded, iotas, ready = (s.sem(n) for n in
                                        ("pad_zeroed", "x_loaded", "const_iotas", "ident_ready"))
        with nc.Block() as block:
            @block.sync
            def _(sp):
                rows = c.rows_a[:, :].rearrange("p (t d) -> p t d", d=D)
                sp.dma_start(rows[:, 0:FULL_ROWS // P, :],
                             x[0:FULL_ROWS, :].rearrange("(t p) d -> p t d", p=P)).then_inc(loaded, 16)
                sp.wait_ge(zeroed, 1)
                sp.dma_start(rows[0:LAST_ROWS, FULL_ROWS // P, :], x[FULL_ROWS:N, :]).then_inc(loaded, 16)
                sp.wait_ge(loaded, 32)

            @block.gpsimd
            def _(pool):
                pool.iota(c.iota_n[:, :], [[1, P]], base=0, channel_multiplier=0,
                          allow_small_or_imprecise_dtypes=True).then_inc(iotas, 1)
                pool.iota(c.iota_p[:, :], [[1, 1]], base=0, channel_multiplier=1,
                          allow_small_or_imprecise_dtypes=True).then_inc(iotas, 1)

            @block.vector
            def _(v):
                v.memset(c.rows_a[:, FULL_ROWS // P * D:NT * D], 0.0).then_inc(zeroed, 1)
                v.memset(c.eps_col[:, :], LN_EPS)
                v.wait_ge(iotas, 2)
                v.tensor_scalar(c.ident[:, :], c.iota_n[:, :], c.iota_p[:, 0:1], None, ALU.is_equal).then_inc(ready, 1)
                v.wait_ge(ready, 1)


def item_tables(c, src, dst):
    nc = c.nc
    whole = EDGE_TILES - 1
    tail = E - whole * P
    cols, rest = whole // P, whole % P
    b = c.rows_b
    at = [0]

    def take(n, dt=F32):
        a = b[:, at[0]:at[0] + n]
        at[0] += n
        return a if dt == F32 else a.bitcast(dt)

    dt_i = take(EC * P, I32).rearrange("p (c e) -> p c e", e=P)
    st_i = take(EC * P, I32).rearrange("p (c e) -> p c e", e=P)
    d_i = take(IC * P, I32).rearrange("p (c e) -> p c e", e=P)
    s_i = take(IC * P, I32).rearrange("p (c e) -> p c e", e=P)
    ends = take(2 * EC).rearrange("p (k c) -> p k c", k=2)
    limits = take(2 * NODE_TILES).rearrange("p (k j) -> p k j", k=2)
    below = take(2 * EC * NODE_TILES).rearrange("p (k c j) -> p k c j", k=2, c=EC)
    ones = take(P)
    counts = take(2 * NODE_TILES).rearrange("p (k j) -> p k j", k=2)
    size, upto, first, shift = (take(NODE_TILES) for _ in range(4))
    item_no = take(IC)
    past = take(IC * NODE_TILES).rearrange("p (c j) -> p c j", c=IC)
    moved = take(IC * NODE_TILES).rearrange("p (c j) -> p c j", c=IC)
    tile_no = take(IC)
    edge_tile = take(IC)
    edge_tile_u = take(IC, U32)
    tile_i = take(IC, I32)
    dst_f = take(IC * P).rearrange("p (c e) -> p c e", e=P)
    src_f = take(IC * P).rearrange("p (c e) -> p c e", e=P)
    rel = take(IC * P).rearrange("p (c e) -> p c e", e=P)
    valid = take(IC * P).rearrange("p (c e) -> p c e", e=P)
    sid = take(IC * P).rearrange("p (c e) -> p c e", e=P)
    row_f = take(IC * P)[0:1]
    with Semaphores(nc) as s:
        def sem(n):
            return s.sem(n)
        padded, loaded, saved, iotas = sem("padded"), sem("edges_loaded"), sem("edges_saved"), sem("iotas")
        step, summed, rows_at, gathered = sem("table_step"), sem("ends_summed"), sem("edge_tile_ready"), sem("rows_gathered")
        turned, copied, sid_ready, written = sem("turned"), sem("turned_copied"), sem("sid_ready"), sem("tables_written")
        rel_ready, tiles_back = sem("rel_ready"), sem("tiles_back")
        with nc.Block() as block:
            @block.sync
            def _(sp):
                sp.wait_ge(padded, 2)
                for flat, to in ((dst, dt_i), (src, st_i)):
                    rows = flat[0:whole * P].rearrange("(k e) -> k e", e=P)
                    sp.dma_start(to[:, 0:cols, :], rows[0:cols * P, :].rearrange("(c p) e -> p c e", p=P)).then_inc(loaded, 16)
                    sp.dma_start(to[0:rest, cols, :], rows[cols * P:whole, :]).then_inc(loaded, 16)
                    sp.dma_start(to[rest:rest + 1, cols, 0:tail], flat[whole * P:E].rearrange("(a e) -> a e", a=1)).then_inc(loaded, 16)
                sp.wait_ge(loaded, 96)
                for ap, to in ((dt_i, c.dstp_dram), (st_i, c.srcp_dram)):
                    sp.dma_start(to[0:cols * P, :].rearrange("(c p) e -> p c e", p=P), ap[:, 0:cols, :]).then_inc(saved, 16)
                    sp.dma_start(to[cols * P:EDGE_TILES, :], ap[0:rest + 1, cols, :]).then_inc(saved, 16)
                sp.wait_ge(sid_ready, 1)
                sp.dma_start(c.sid_dram[:, :].rearrange("(c p) e -> p c e", p=P), sid).then_inc(written, 16)
                with nc.allow_non_contiguous_dma("one number an item"):
                    sp.dma_start(c.tile_dram.rearrange("(c p) -> p c", p=P), tile_i).then_inc(written, 16)
                    sp.dma_start(c.edge_sid_dram[0].rearrange("(c p) -> p c", p=P), sid[:, :, 0]).then_inc(written, 16)
                    sp.dma_start(c.edge_sid_dram[1].rearrange("(c p) -> p c", p=P), sid[:, :, P - 1]).then_inc(written, 16)
                sp.wait_ge(written, 64)
                sp.dma_start(c.item_tile[:, :], c.tile_dram.rearrange("(a i) -> a i", a=1)).then_inc(tiles_back, 16)

            @block.gpsimd
            def _(pool):
                pool.iota(limits[:, 0, :], [[P, NODE_TILES]], base=0, channel_multiplier=0,
                          allow_small_or_imprecise_dtypes=True).then_inc(iotas, 1)
                pool.iota(limits[:, 1, :], [[P, NODE_TILES]], base=P, channel_multiplier=0,
                          allow_small_or_imprecise_dtypes=True).then_inc(iotas, 1)
                pool.iota(item_no, [[P, IC]], base=0, channel_multiplier=1,
                          allow_small_or_imprecise_dtypes=True).then_inc(iotas, 1)
                pool.wait_ge(saved, 64)
                pool.wait_ge(rows_at, 1)
                for i in range(IC):
                    at_row = bass.IndirectOffsetOnAxis(ap=edge_tile_u[:, i:i + 1], axis=0)
                    pool.indirect_dma_start(d_i[:, i, :], None, c.dstp_dram[:, :], at_row).then_inc(gathered, 16)
                    pool.indirect_dma_start(s_i[:, i, :], None, c.srcp_dram[:, :], at_row).then_inc(gathered, 16)

            @block.vector
            def _(v):
                do = Chain(v, step)
                v.memset(dt_i, PAD_DST).then_inc(padded, 1)
                v.memset(st_i, 0).then_inc(padded, 1)
                do(v.memset(ones, 1.0))
                v.wait_ge(loaded, 96)
                do(v.tensor_copy(ends[:, 0, :], dt_i[:, :, P - 1]))
                do(v.tensor_copy(ends[:, 1, :], dt_i[:, :, 0]))
                v.wait_ge(iotas, 3)
                for k in range(2):
                    do(v.tensor_tensor(below[:, k], bc(ends[:, k].unsqueeze(2), [P, EC, NODE_TILES]),
                                       bc(limits[:, k].unsqueeze(1), [P, EC, NODE_TILES]), ALU.is_lt))
                v.wait_ge(summed, 1)
                do(v.tensor_copy(counts.rearrange("p k j -> p (k j)"), c.ps[:, 0:2 * NODE_TILES]))
                do(v.tensor_tensor(size, counts[:, 1], counts[:, 0], ALU.subtract))
                do(v.tensor_tensor_scan(upto, ones[:, 0:NODE_TILES], size, 0.0, ALU.mult, ALU.add))
                do(v.tensor_tensor(first, upto, size, ALU.subtract))
                do(v.tensor_tensor(first, counts[:, 0], first, ALU.subtract))
                do(v.memset(shift, 0.0))
                do(v.tensor_tensor(shift[:, 0:NODE_TILES - 1], first[:, 1:], first[:, :NODE_TILES - 1], ALU.subtract))
                do(v.tensor_tensor(past, bc(upto.unsqueeze(1), [P, IC, NODE_TILES]),
                                   bc(item_no.unsqueeze(2), [P, IC, NODE_TILES]), ALU.is_le))
                do(v.tensor_reduce(tile_no, past, AX.X, ALU.add))
                do(v.tensor_tensor(moved, past, bc(shift.unsqueeze(1), [P, IC, NODE_TILES]), ALU.mult))
                do(v.tensor_reduce(edge_tile, moved, AX.X, ALU.add))
                do(v.tensor_tensor(edge_tile, edge_tile, item_no, ALU.add))
                do(v.tensor_scalar(edge_tile, edge_tile, 0.0, float(EDGE_TILES - 1), ALU.max, ALU.min))
                v.tensor_copy(edge_tile_u, edge_tile).then_inc(rows_at, 1)
                do(v.tensor_copy(tile_i, tile_no))
                do(v.tensor_scalar(tile_no, tile_no, float(P), None, ALU.mult))
                v.wait_ge(gathered, 32 * IC)
                do(v.tensor_copy(dst_f, d_i))
                do(v.tensor_copy(src_f, s_i))
                do(v.tensor_tensor(rel, dst_f, bc(tile_no.unsqueeze(2), [P, IC, P]), ALU.subtract))
                v.sem_inc(rel_ready, 1)
                do(v.tensor_scalar(valid, rel, 0.0, None, ALU.is_ge))
                do(v.tensor_scalar(sid, rel, float(P), None, ALU.is_lt))
                do(v.tensor_tensor(valid, valid, sid, ALU.mult))
                do(v.tensor_scalar(dst_f, dst_f, 1.0, None, ALU.add))
                do(v.tensor_tensor(valid, valid, dst_f, ALU.mult))
                do(v.tensor_scalar(sid, valid, 1.0, None, ALU.subtract))
                v.sem_inc(sid_ready, 1)
                v.wait_ge(turned, 1)
                v.tensor_copy(c.rel_dst[:, :], c.ps[:, 1024:1024 + IC * P]).then_inc(copied, 1)
                v.tensor_copy(c.src_idx[:, :], c.ps[:, 2048:2048 + IC * P]).then_inc(copied, 1)
                v.wait_ge(copied, 2)
                v.wait_ge(tiles_back, 16)
                do(v.tensor_copy(row_f, c.item_tile[:, :]))
                each = row_f.rearrange("p (b u) -> p u b", u=BATCH)
                for u in range(1, BATCH):
                    do(v.scalar_tensor_tensor(each[:, 0], each[:, u], float(1 << (TILE_BITS * u)), each[:, 0],
                                              ALU.mult, ALU.add))
                do(v.tensor_copy(c.batch_tiles[:, :], each[:, 0]))

            @block.tensor
            def _(pe):
                pe.wait_ge(step, 5)
                for k in range(2):
                    for i in range(EC):
                        mm = pe.matmul(c.ps[:, k * NODE_TILES:(k + 1) * NODE_TILES], ones, below[:, k, i, :],
                                       start=(i == 0), stop=(i == EC - 1))
                mm.then_inc(summed, 1)
                pe.wait_ge(rel_ready, 1)
                for k, tab in ((0, rel), (1, src_f)):
                    for i in range(IC):
                        to = 1024 * (1 + k) + i * P
                        mm = pe.transpose(c.ps[:, to:to + P], tab[:, i, :], c.ident[:, :])
                mm.then_inc(turned, 1)


def layer_norm(c, src, dst, name, tiles=NT):
    nc = c.nc
    with Semaphores(nc) as s:
        taken, step, rooted, var_ready = (s.sem(f"{name}_{n}")
                                          for n in ("stats", "step", "root", "var"))
        with nc.Block() as block:
            @block.vector
            def _(v):
                ln_vector(c, v, src, dst, taken, step, rooted, var_ready, tiles)

            @block.scalar
            def _(a):
                a.wait_ge(var_ready, 1)
                a.activation(c.rstd[:, 0:tiles], c.rstd[:, 0:tiles], ACT.Sqrt,
                             bias=c.eps_col[:, 0:1]).then_inc(rooted, 1)


def ln_vector(c, v, src, dst, taken, step, rooted, var_ready, tiles):
    do = Chain(v, step)
    with v.Fori(0, tiles // 10) as i:
        for u in range(10):
            v.bn_stats(c.stats[:, bass.ds(i * 60 + u * 6, 6)], src[:, bass.ds(i * 10 * D + u * D, D)]).then_inc(taken, 1)
    v.wait_ge(taken, tiles)
    st = c.stats[:, :].rearrange("p (t k) -> p k t", k=6)
    tmp = c.small[:, 0:NT]
    do(v.tensor_tensor(c.mean[:, :], st[:, 1, :], st[:, 4, :], ALU.add))
    do(v.tensor_scalar(c.mean[:, :], c.mean[:, :], 0.5, None, ALU.mult))
    do(v.tensor_tensor(tmp, st[:, 1, :], st[:, 4, :], ALU.subtract))
    do(v.tensor_tensor(tmp, tmp, tmp, ALU.mult))
    do(v.tensor_tensor(c.rstd[:, :], st[:, 2, :], st[:, 5, :], ALU.add))
    do(v.tensor_scalar(tmp, tmp, D / 4.0, None, ALU.mult))
    do(v.tensor_tensor(c.rstd[:, :], c.rstd[:, :], tmp, ALU.add))
    do(v.tensor_scalar(c.rstd[:, :], c.rstd[:, :], 1.0 / D, None, ALU.mult))
    v.sem_inc(var_ready, 1)
    v.wait_ge(rooted, 1)
    do(v.reciprocal(c.rstd[:, :], c.rstd[:, :]))
    with v.Fori(0, tiles // 10) as i:
        for u in range(10):
            at, t = bass.ds(i * 10 * D + u * D, D), bass.ds(i * 10 + u, 1)
            v.tensor_scalar(dst[:, at], src[:, at], c.mean[:, t], c.rstd[:, t], ALU.subtract, ALU.mult).then_inc(taken, 1)
    v.wait_ge(taken, 2 * tiles)



def groups(eng, body):
    with eng.Fori(0, GROUPS2 // 2) as i:
        body(i * 2, 0, False)
        body(i * 2 + 1, 1, False)
    body(GROUPS2 - 1, (GROUPS2 - 1) % 2, True)


def turn(pe, c, staged_rows, parity):
    for k in range(2):
        for u in range(2):
            to = parity * 512 + k * 2 * P + u * P
            mm = pe.transpose(c.ps[:, to:to + P], staged_rows[:, u * D + k * P:u * D + k * P + P], c.ident[:, :])
    return mm


def load_tiles(eng, c, b):
    packed = eng.value_load(c.batch_tiles[0:1, bass.ds(b, 1)], min_val=0, max_val=(1 << TILE_BITS * BATCH) - 1)
    why = "the item table counts node tiles from 0 to NODE_TILES"
    return [c.nc.s_assert_within((packed >> (TILE_BITS * u)) & ((1 << TILE_BITS) - 1), 0, NODE_TILES,
                                 skip_runtime_bounds_check_because=why) for u in range(BATCH)]


class Front:

    def __init__(self, c, s, name, rows, turned_rows, source):
        self.c, self.rows, self.turned_rows, self.source = c, rows, turned_rows, source
        self.staged, self.turned, self.copied, self.used = (
            s.sem(f"{name}_{n}") for n in ("staged", "turned", "copied", "used"))

    def start_pe(self, pe):
        pe.sem_inc(self.turned, 2)
        pe.sem_inc(self.used, 2)

    def start_vector(self, v):
        v.sem_inc(self.copied, 2)

    def stage(self, a, g, parity):
        a.wait_ge(self.turned, g + 1)
        a.activation(self.rows[parity], self.source[:, bass.ds(g * 2 * D, 2 * D)],
                     ACT.Copy).then_inc(self.staged, 1)

    def turn(self, pe, g, parity):
        pe.wait_ge(self.staged, g + 1)
        pe.wait_ge(self.copied, g + 1)
        turn(pe, self.c, self.rows[parity], parity).then_inc(self.turned, 1)

    def copy(self, v, g, parity):
        v.wait_ge(self.used, g + 1)
        v.wait_ge(self.turned, g + 3)
        v.tensor_copy(self.turned_rows[:, parity], self.c.ps[:, parity * 512:parity * 512 + 512]).then_inc(self.copied, 1)


def qkv(c, wq, wk, wv, name):
    nc = c.nc
    w = c.scores[:, 0:2 * 3 * D].rearrange("p (k n) -> p k n", k=2)
    rows = [c.scores[:, 1536 + k * 512:2048 + k * 512] for k in range(2)]
    rows_t = c.scores[:, 2560:3584].rearrange("p (b n) -> p b n", b=2)
    kv = c.scores[:, 3584:3584 + 4 * 2 * D].rearrange("p (b n) -> p b n", b=4)
    scale = float(DK) ** -0.5
    with Semaphores(nc) as s:
        def sem(n):
            return s.sem(f"{name}_{n}")
        loaded, saved, out_done, kv_ready = sem("w_loaded"), sem("h_saved"), sem("out_done"), sem("kv_ready")
        stored, kv_free = [sem(f"stored{u}") for u in range(4)], sem("kv_free")
        f = Front(c, s, name, rows, rows_t, c.rows_a)
        with nc.Block() as block:
            @block.sync
            def _(sp):
                for j, m in enumerate((wq, wk, wv)):
                    sp.dma_start(w[:, :, j * D:(j + 1) * D], m.rearrange("(k p) n -> p k n", p=P)).then_inc(loaded, 16)
                sp.dma_start(c.h_dram.rearrange("(t p) d -> p t d", p=P),
                             c.rows_a[:, :].rearrange("p (t d) -> p t d", d=D)).then_inc(saved, 16)

                def body(g, parity, last):
                    for u in range(2):
                        b = 2 * parity + u
                        sp.wait_ge(kv_ready, g * 2 + u + 1)
                        for to, n in ((c.k_dram, 0), (c.v_dram, D)):
                            sp.dma_start(to[bass.ds(g * 2 * P + u * P, P), :], kv[:, b, n:n + D]).then_inc(stored[b], 16)
                    for u in range(2):
                        sp.wait_ge(stored[2 * parity + u], (g - parity) * 16 + 32)
                        sp.sem_inc(kv_free, 1)
                groups(sp, body)
                sp.wait_ge(saved, 16)

            @block.scalar
            def _(a):
                groups(a, lambda g, parity, last: f.stage(a, g, parity))

            @block.tensor
            def _(pe):
                f.start_pe(pe)
                pe.wait_ge(loaded, 48)
                f.turn(pe, 0, 0)

                def body(g, parity, last):
                    if not last:
                        f.turn(pe, g + 1, 1 - parity)
                    pe.wait_ge(f.copied, g + 3)
                    pe.wait_ge(out_done, g + 1)
                    for u in range(2):
                        for k in range(2):
                            x = rows_t[:, parity, k * 2 * P + u * P:k * 2 * P + u * P + P]
                            q = (2 + parity) * 512 + u * D
                            pe.matmul(c.ps[:, q:q + D], x, w[:, k, 0:D], start=(k == 0), stop=(k == 1))
                        for k in range(2):
                            x = rows_t[:, parity, k * 2 * P + u * P:k * 2 * P + u * P + P]
                            to = (4 + 2 * parity + u) * 512
                            mm = pe.matmul(c.ps[:, to:to + 512], x, w[:, k, D:3 * D], start=(k == 0), stop=(k == 1))
                    mm.then_inc(f.used, 1)
                groups(pe, body)

            @block.vector
            def _(v):
                f.start_vector(v)
                v.sem_inc(out_done, 2)
                v.sem_inc(kv_free, 4)
                f.copy(v, 0, 0)

                def body(g, parity, last):
                    if not last:
                        f.copy(v, g + 1, 1 - parity)
                    v.wait_ge(f.used, g + 3)
                    for u in range(2):
                        b = 2 * parity + u
                        v.wait_ge(kv_free, g * 2 + u + 1)
                        to = (4 + b) * 512
                        v.tensor_copy(kv[:, b, :], c.ps[:, to:to + 512]).then_inc(kv_ready, 1)
                    q = (2 + parity) * 512
                    v.tensor_scalar(c.rows_b[:, bass.ds(g * 2 * D, 2 * D)], c.ps[:, q:q + 512], scale, None,
                                    ALU.mult).then_inc(out_done, 1)
                groups(v, body)
                v.wait_ge(out_done, GROUPS2 + 2)


def one_hot(c, v, s_buf, b, parity):
    return v.tensor_tensor(s_buf[:, parity], bc(c.iota_n[:, :].unsqueeze(1), [P, BATCH, P]),
                           bc(c.rel_dst[:, bass.ds(b * BATCH, BATCH)].unsqueeze(2), [P, BATCH, P]), ALU.is_equal)


def gather_rows(c, pool, table, ring, width, idx, staged, free, gate, landed, extra, per_batch=1):
    half = RING // 2

    def fetch(i, h, n):
        pool.wait_ge(free, (i * (RING // BATCH) + (h + 1) * (half // BATCH)) * per_batch)
        pool.sem_inc(gate, 1)
        pool.tensor_copy(idx[:, h * half:h * half + n], c.src_idx[:, bass.ds(i * RING + h * half, n)]).then_inc(staged, 1)
        pool.wait_ge(staged, i * 2 + h + 1)
        pool.sem_inc(gate, 1)
        for u in range(n):
            slot = h * half + u
            pool.indirect_dma_start(ring[:, slot, 0:width], None, table,
                                    bass.IndirectOffsetOnAxis(ap=idx[:, slot:slot + 1], axis=0)).then_inc(landed[slot], 16)

    with pool.Fori(0, ITEMS // RING) as i:
        fetch(i, 0, half)
        fetch(i, 1, half)
    if extra:
        fetch(ITEMS // RING, 0, half)


def edge_scores(c, name):
    nc = c.nc
    BW = BATCH * D
    ring = c.rows_a[:, 0:RING * D].rearrange("p (s d) -> p s d", d=D)
    s_buf = c.rows_a[:, RING * D:RING * D + 2048].rearrange("p (b i n) -> p b i n", b=4, i=BATCH)
    st_buf = c.rows_a[:, RING * D + 2048:RING * D + 3072].rearrange("p (b i n) -> p b i n", b=2, i=BATCH)
    prod = c.rows_a[:, RING * D + 3072:RING * D + 5120].rearrange("p (b n) -> p b n", b=2)
    QPS = 1024
    with Semaphores(nc) as s:
        def sem(n):
            return s.sem(f"{name}_{n}")
        free, staged, gate, made, turned = sem("slots_free"), sem("idx"), sem("gate"), sem("onehot"), sem("turned")
        copied, expanded, multiplied, reduced = sem("copied"), sem("expanded"), sem("multiplied"), sem("reduced")
        landed = [sem(f"landed{u}") for u in range(RING)]
        idx = s.enter_context(nc.sbuf_tensor(f"{name}_idx", [P, RING], U32))
        with nc.Block() as block:
            @block.gpsimd
            def _(pool):
                gather_rows(c, pool, c.k_dram[:, :], ring, D, idx, staged, free, gate, landed, False)

            @block.vector
            def _(v):
                v.sem_inc(free, RING // BATCH)
                v.sem_inc(multiplied, 2)
                v.sem_inc(reduced, 2)
                one_hot(c, v, s_buf, 0, 0).then_inc(made, 1)
                one_hot(c, v, s_buf, 1, 1).then_inc(made, 1)
                with v.Fori(0, BATCHES // 4) as i:
                    for q in range(4):
                        b, par = i * 4 + q, q % 2
                        v.wait_ge(turned, b + 1)
                        one_hot(c, v, s_buf, b + 2, (q + 2) % 4).then_inc(made, 1)
                        v.wait_ge(expanded, b + 3)
                        for u in range(BATCH):
                            v.wait_ge(landed[q * BATCH + u], i * 16 + 16)
                        v.wait_ge(reduced, b + 1)
                        v.tensor_tensor(prod[:, par], c.ps[:, QPS + par * BW:QPS + (par + 1) * BW],
                                        ring[:, q * BATCH:(q + 1) * BATCH, :].rearrange("p s d -> p (s d)"),
                                        ALU.mult).then_inc(multiplied, 1)
                        v.wait_ge(multiplied, b + 3)
                        v.sem_inc(free, 1)
                        v.tensor_reduce(c.scores[:, bass.ds(b * BATCH * H, BATCH * H)],
                                        prod[:, par].rearrange("p (h k) -> p h k", k=DK), AX.X, ALU.add).then_inc(reduced, 1)
                v.wait_ge(reduced, BATCHES + 2)

            @block.scalar
            def _(a):
                a.sem_inc(copied, 2)
                with a.Fori(0, BATCHES // 2) as i:
                    for par in range(2):
                        b = i * 2 + par
                        a.wait_ge(expanded, b + 1)
                        a.wait_ge(turned, b + 3)
                        a.activation(st_buf[:, par].rearrange("p i n -> p (i n)"), c.ps[:, par * 512:par * 512 + 512],
                                     ACT.Copy).then_inc(copied, 1)

            @block.tensor
            def _(pe):
                pe.sem_inc(turned, 2)
                pe.sem_inc(expanded, 2)

                def flip(b, slot):
                    par = slot % 2
                    pe.wait_ge(made, b + 1)
                    pe.wait_ge(copied, b + 1)
                    for u in range(BATCH):
                        mm = pe.transpose(c.ps[:, par * 512 + u * P:par * 512 + u * P + P], s_buf[:, slot, u, :], c.ident[:, :])
                    mm.then_inc(turned, 1)
                flip(0, 0)
                with pe.Fori(0, BATCHES // 4) as i:
                    for q in range(4):
                        b, par = i * 4 + q, q % 2
                        flip(b + 1, (q + 1) % 4)
                        tiles = load_tiles(pe, c, b)
                        pe.wait_ge(copied, b + 3)
                        pe.wait_ge(multiplied, b + 1)
                        for u in range(BATCH):
                            to = QPS + par * BW + u * D
                            mm = pe.matmul(c.ps[:, to:to + D], st_buf[:, par, u, :], c.rows_b[:, bass.ds(tiles[u] * D, D)],
                                           start=True, stop=True)
                        mm.then_inc(expanded, 1)


def segment_masks(c):
    nc = c.nc
    n = GROUPS * P
    sid = c.rows_b[:, 0:n]
    sid3 = sid.rearrange("p (g e) -> p g e", e=P)
    c.link = c.rows_c[:, 0:n // 2 + 1].bitcast(BF16)
    c.to_first = c.rows_c[:, n // 2 + 1:n + 1].bitcast(BF16)
    c.to_last = c.rows_c[:, n + 1:n + 1 + n // 2].bitcast(BF16)
    o = n + 1 + n // 2
    c.item_link = c.rows_c[0:H, o:o + ITEMS + 1]
    c.item_whole = c.rows_c[0:H, o + ITEMS + 1:o + 2 * ITEMS + 1]
    assert o + 2 * ITEMS + 1 <= 2 * n
    ends = c.rows_b[0:H, n:n + 2 * ITEMS].rearrange("p (k i) -> p k i", k=2)
    with Semaphores(nc) as s:
        loaded, step = s.sem("sid_loaded"), s.sem("mask_step")
        with nc.Block() as block:
            @block.sync
            def _(sp):
                for h in range(H):
                    sp.dma_start(sid3[h * 16:(h + 1) * 16], c.sid_dram[0:ITEMS, :].rearrange("(g i) e -> i g e", i=16)).then_inc(loaded, 16)
                for h in range(H):
                    sp.dma_start(ends[h:h + 1], c.edge_sid_dram[:, 0:ITEMS].rearrange("(a k) i -> a k i", a=1)).then_inc(loaded, 16)

            @block.vector
            def _(v):
                do = Chain(v, step)
                v.wait_ge(loaded, 32 * H)

                def masked(out, a, b):
                    do(v.tensor_tensor(out, a, b, ALU.is_equal))
                    do(v.tensor_scalar(out, out, 1.0, BIG, ALU.subtract, ALU.mult))
                link3 = c.link[:, 0:n].rearrange("p (g e) -> p g e", e=P)
                do(v.memset(c.link, 0.0))
                masked(link3[:, :, 1:], sid3[:, :, 1:], sid3[:, :, :P - 1])
                do(v.memset(link3[:, :, 0:1], -BIG))
                do(v.memset(c.link[:, n:n + 2], -BIG))
                for out, e in ((c.to_first, 0), (c.to_last, P - 1)):
                    masked(out.rearrange("p (g e) -> p g e", e=P), sid3, bc(sid3[:, :, e:e + 1], [P, GROUPS, P]))
                do(v.memset(c.item_link, -BIG))
                masked(c.item_link[:, 1:ITEMS], ends[:, 0, 1:ITEMS], ends[:, 1, 0:ITEMS - 1])
                masked(c.item_whole, ends[:, 0, :], ends[:, 1, :])


def segment_softmax(c, name):
    nc = c.nc
    n = GROUPS * P
    e = c.rows_b[:, 0:n]
    f = c.rows_b[:, n:2 * n]
    m = c.rows_a[:, 0:n]
    ends = c.rows_a[:, n:n + 2 * GROUPS].rearrange("p (k g) -> p k g", k=2)
    t = [n + 2 * GROUPS]

    def take(k):
        a = c.rows_a[0:H, t[0]:t[0] + k]
        t[0] += k
        return a
    ends_t = take(2 * ITEMS).rearrange("p (k i g) -> p k i g", k=2, i=16)
    seq = take(2 * ITEMS).rearrange("p (k i) -> p k i", k=2)
    assert t[0] <= NT * D
    fwd, back = (c.scores[0:H, k * ITEMS:(k + 1) * ITEMS] for k in range(2))
    wl, wr = (c.scores[0:H, (2 + k) * ITEMS:(3 + k) * ITEMS] for k in range(2))
    rounds = GROUPS // 4
    by_group = c.scores[:, 0:ITEMS * H].rearrange("p (g i h) -> p g h i", g=GROUPS, i=16)
    turned_in = c.rows_a
    with Semaphores(nc) as s:
        def sem(x):
            return s.sem(f"{name}_{x}")
        arranged, turned, copied, step, saved = sem("arranged"), sem("turned"), sem("copied"), sem("step"), sem("saved")
        sent, carried, seq_done, ready, exped = sem("sent"), sem("carried"), sem("seq_done"), sem("ready"), sem("exped")
        back_turned, back_copied = sem("back_turned"), sem("back_copied")
        with nc.Block() as block:
            @block.tensor
            def _(pe):
                for r in range(rounds):
                    pe.wait_ge(arranged, r + 1)
                    if r >= 2:
                        pe.wait_ge(copied, r - 1)
                    for u in range(4):
                        to = (r % 2) * 512 + u * P
                        g = r * 4 + u
                        mm = pe.transpose(c.ps[:, to:to + P], f[:, g * P:(g + 1) * P], c.ident[:, :])
                    mm.then_inc(turned, 1)
                for r in range(rounds):
                    if r == 0:
                        pe.wait_ge(exped, 1)
                        pe.wait_ge(copied, rounds)
                    if r >= 2:
                        pe.wait_ge(back_copied, r - 1)
                    for u in range(4):
                        to = (r % 2) * 512 + u * P
                        g = r * 4 + u
                        mm = pe.transpose(c.ps[:, to:to + P], e[:, g * P:(g + 1) * P], c.ident[:, :])
                    mm.then_inc(back_turned, 1)

            @block.scalar
            def _(a):
                for r in range(rounds):
                    a.wait_ge(turned, r + 1)
                    a.activation(e[:, r * 512:(r + 1) * 512], c.ps[:, (r % 2) * 512:(r % 2) * 512 + 512], ACT.Copy).then_inc(copied, 1)
                a.wait_ge(copied, rounds)
                a.wait_ge(ready, 1)
                a.activation(e, e, ACT.Exp).then_inc(exped, 1)

            @block.sync
            def _(sp):
                sp.wait_ge(saved, 1)
                for h in range(H):
                    sp.dma_start(c.ends_dram[:, h, :, :], ends[h * 16:(h + 1) * 16]).then_inc(sent, 16)
                sp.wait_ge(sent, 16 * H)
                for k in range(2):
                    sp.dma_start(ends_t[:, k], c.ends_dram[:, :, k, :].rearrange("i h g -> h i g")).then_inc(carried, 16)
                sp.wait_ge(seq_done, 1)
                for k in range(2):
                    sp.dma_start(c.carry_dram[:, :, k, :].rearrange("i h g -> h i g"), ends_t[:, k]).then_inc(sent, 16)
                sp.wait_ge(sent, 16 * H + 32)
                for h in range(H):
                    sp.dma_start(ends[h * 16:(h + 1) * 16], c.carry_dram[:, h, :, :]).then_inc(carried, 16)
                sp.wait_ge(carried, 32 + 16 * H)

            @block.vector
            def _(v):
                do = Chain(v, step)
                for r in range(rounds):
                    v.tensor_copy(f[:, r * 512:(r + 1) * 512].rearrange("p (g h i) -> p g h i", g=4, h=H),
                                  by_group[:, r * 4:(r + 1) * 4]).then_inc(arranged, 1)
                v.wait_ge(copied, rounds)
                do(v.tensor_tensor_scan(f, c.link[:, 0:n], e, -BIG, ALU.add, ALU.max))
                do(v.tensor_tensor_scan(m[:, ::-1], c.link[:, 1:n + 1][:, ::-1], f[:, ::-1], -BIG, ALU.add, ALU.max))
                m3 = m.rearrange("p (g e) -> p g e", e=P)
                do(v.tensor_copy(ends[:, 0, :], m3[:, :, 0]))
                do(v.tensor_copy(ends[:, 1, :], m3[:, :, P - 1]))
                v.sem_inc(saved, 1)
                do(v.tensor_tensor(wl, c.item_whole, c.item_link[:, 0:ITEMS], ALU.add))
                do(v.tensor_tensor(wr, c.item_whole, c.item_link[:, 1:ITEMS + 1], ALU.add))
                v.wait_ge(carried, 32)
                for k in range(2):
                    do(v.tensor_copy(seq[:, k].rearrange("p (g i) -> p i g", i=16), ends_t[:, k]))
                do(v.tensor_tensor_scan(fwd, wl, seq[:, 1], -BIG, ALU.add, ALU.max))
                do(v.tensor_tensor_scan(back[:, ::-1], wr[:, ::-1], seq[:, 0][:, ::-1], -BIG, ALU.add, ALU.max))
                do(v.memset(seq.rearrange("p k i -> p (k i)"), -BIG))
                do(v.tensor_tensor(seq[:, 0, 1:], fwd[:, 0:ITEMS - 1], c.item_link[:, 1:ITEMS], ALU.add))
                do(v.tensor_tensor(seq[:, 1, 0:ITEMS - 1], back[:, 1:], c.item_link[:, 1:ITEMS], ALU.add))
                for k in range(2):
                    do(v.tensor_copy(ends_t[:, k], seq[:, k].rearrange("p (g i) -> p i g", i=16)))
                v.sem_inc(seq_done, 1)
                v.wait_ge(carried, 32 + 16 * H)
                for k, mask in enumerate((c.to_first, c.to_last)):
                    do(v.tensor_tensor(f.rearrange("p (g e) -> p g e", e=P), mask.rearrange("p (g e) -> p g e", e=P),
                                       bc(ends[:, k, :].unsqueeze(2), [P, GROUPS, P]), ALU.add))
                    do(v.tensor_tensor(m, m, f, ALU.max))
                do(v.tensor_tensor(e, e, m, ALU.subtract))
                v.sem_inc(ready, 1)
                do(v.memset(c.scores[:, ITEMS * H:(ITEMS + 16) * H], 0.0))
                for r in range(rounds):
                    v.wait_ge(back_turned, r + 1)
                    v.tensor_copy(by_group[:, r * 4:(r + 1) * 4],
                                  c.ps[:, (r % 2) * 512:(r % 2) * 512 + 512].rearrange("p (g h i) -> p g h i", g=4, h=H)
                                  ).then_inc(back_copied, 1)
                v.wait_ge(back_copied, rounds)


SUMW = D + H


def edge_sums(c, table, weighted, name):
    nc = c.nc
    width = D if weighted else D + 2
    ring = c.rows_a[:, 0:RING * SUMW].rearrange("p (s d) -> p s d", d=SUMW)
    o = RING * SUMW
    s_buf = c.rows_a[:, o:o + 2048].rearrange("p (b i n) -> p b i n", b=4, i=BATCH)
    msg = c.rows_a[:, o + 2048:o + 2048 + 4 * BATCH * SUMW].rearrange("p (b i n) -> p b i n", b=4, i=BATCH)
    zeros = c.rows_a[:, o + 2048:o + 2048 + D]
    nw = SUMW if weighted else width
    with Semaphores(nc) as s:
        def sem(n):
            return s.sem(f"{name}_{n}")
        staged, gate, made, weights = sem("idx"), sem("gate"), sem("onehot"), sem("weights")
        msgs, summed, added, cleared = sem("messages"), sem("summed"), sem("added"), sem("cleared")
        filled = sem("filled")
        landed = [sem(f"landed{u}") for u in range(RING)]
        idx = s.enter_context(nc.sbuf_tensor(f"{name}_idx", [P, RING], U32))
        with nc.Block() as block:
            @block.gpsimd
            def _(pool):
                if not weighted:
                    pool.wait_ge(cleared, 2)
                    pool.sem_inc(gate, 1)
                gather_rows(c, pool, table, ring, D, idx, staged, msgs if weighted else summed, gate, landed,
                            weighted, 2 if weighted else 1)

            if not weighted:
                @block.sync
                def _(sp):
                    sp.wait_ge(cleared, 3)
                    sp.dma_start(c.slot_in.rearrange("(t p) d -> p t d", p=P),
                                 bc(zeros.unsqueeze(1), [P, SLOT_TILES, D])).then_inc(filled, 16)
                    sp.wait_ge(filled, 16)

            @block.scalar
            def _(a):
                if weighted:
                    with a.Fori(0, BATCHES // 4) as i:
                        for q in range(4):
                            b = i * 4 + q
                            a.wait_ge(summed, b + 1)
                            a.activation(msg[:, q, :, D:SUMW],
                                         c.scores[:, bass.ds(b * BATCH * H, BATCH * H)].rearrange("p (i h) -> p i h", h=H),
                                         ACT.Copy).then_inc(weights, 1)

            @block.vector
            def _(v):
                v.sem_inc(added, 2 * BATCH)
                v.sem_inc(msgs, 2 * (RING // BATCH))
                v.memset(c.rows_b[:, 0:NT * SUMW], 0.0).then_inc(cleared, 1)
                if not weighted:
                    v.memset(ring[:, :, D:SUMW], 1.0).then_inc(cleared, 1)
                    v.memset(zeros, 0.0).then_inc(cleared, 1)
                v.wait_ge(cleared, 1)

                def message(i, q, b, half):
                    lo, hi = half * BATCH // 2, (half + 1) * BATCH // 2
                    for u in range(lo, hi):
                        v.wait_ge(landed[q * BATCH + u], i * 16 + 16)
                    v.tensor_tensor(msg[:, q, lo:hi, 0:D].rearrange("p i (h k) -> p i h k", k=DK),
                                    ring[:, q * BATCH + lo:q * BATCH + hi, 0:D].rearrange("p i (h k) -> p i h k", k=DK),
                                    bc(c.scores[:, bass.ds(b * BATCH * H + lo * H, BATCH // 2 * H)]
                                       .rearrange("p (i h) -> p i h", h=H).unsqueeze(3), [P, BATCH // 2, H, DK]),
                                    ALU.mult).then_inc(msgs, 1)

                for b in range(2):
                    one_hot(c, v, s_buf, b, b).then_inc(made, 1)
                    if weighted:
                        message(0, b, b, 0)
                        message(0, b, b, 1)
                with v.Fori(0, BATCHES // 4) as i:
                    for q in range(4):
                        b, par = i * 4 + q, q % 2
                        one_hot(c, v, s_buf, b + 2, (q + 2) % 4).then_inc(made, 1)
                        tiles = load_tiles(v, c, b)
                        v.wait_ge(summed, b + 5)
                        for u in range(BATCH):
                            ps = c.ps[:, (par * BATCH + u) * 512:(par * BATCH + u) * 512 + nw]
                            to = c.rows_b[:, bass.ds(tiles[u] * SUMW, nw)]
                            v.wait_ge(added, b * BATCH + u + 2 * BATCH)
                            v.tensor_tensor(to, to, ps, ALU.add).then_inc(added, 1)
                            if weighted and u < 2:
                                message(i + (q + 2) // 4, (q + 2) % 4, b + 2, u)
                v.wait_ge(added, ITEMS + 2 * BATCH)

            @block.tensor
            def _(pe):
                pe.sem_inc(summed, 4)
                with pe.Fori(0, BATCHES // 4) as i:
                    for q in range(4):
                        b, par = i * 4 + q, q % 2
                        pe.wait_ge(made, b + 1)
                        pe.wait_ge(added, b * BATCH + BATCH)
                        if weighted:
                            pe.wait_ge(weights, b + 1)
                            pe.wait_ge(msgs, b * 2 + 2 + 2 * (RING // BATCH))
                        else:
                            for u in range(BATCH):
                                pe.wait_ge(landed[q * BATCH + u], i * 16 + 16)
                        for u in range(BATCH):
                            to = (par * BATCH + u) * 512
                            rhs = msg[:, q, u, :] if weighted else ring[:, q * BATCH + u, 0:nw]
                            mm = pe.matmul(c.ps[:, to:to + nw], s_buf[:, q, u, :], rhs, start=True, stop=True)
                        mm.then_inc(summed, 1)


def rows3(ap, tiles=NT):
    return ap[:, 0:tiles * D].rearrange("p (t d) -> p t d", d=D)


def row_bc(ap):
    return ap.rearrange("(a n) -> a n", a=1).broadcast_to([P, ap.shape[0]])


def attention_out(c, wo, name):
    nc = c.nc
    w = c.scores[:, 0:512].rearrange("p (k n) -> p k n", k=2)
    rows = c.scores[:, 512:1536].rearrange("p (b t d) -> p b t d", b=2, t=2)
    rows_t = c.scores[:, 1536:2560].rearrange("p (b n) -> p b n", b=2)
    inv = c.scores[:, 2560:2592].rearrange("p (b t h) -> p b t h", b=2, t=2)
    with Semaphores(nc) as s:
        def sem(n):
            return s.sem(f"{name}_{n}")
        loaded, staged, turned, copied = sem("loaded"), sem("staged"), sem("turned"), sem("copied")
        used, out_done, step = sem("used"), sem("out_done"), sem("step")
        with nc.Block() as block:
            @block.sync
            def _(sp):
                sp.dma_start(w, wo.rearrange("(k p) n -> p k n", p=P)).then_inc(loaded, 16)
                sp.dma_start(rows3(c.rows_a), c.h_dram.rearrange("(t p) d -> p t d", p=P)).then_inc(loaded, 16)

            @block.scalar
            def _(a):
                a.sem_inc(copied, 2)

                def body(g, parity, last):
                    a.wait_ge(turned, g + 3)
                    a.wait_ge(used, g + 1)
                    a.activation(rows_t[:, parity], c.ps[:, parity * 512:parity * 512 + 512], ACT.Copy).then_inc(copied, 1)
                groups(a, body)

            @block.tensor
            def _(pe):
                pe.sem_inc(turned, 2)
                pe.sem_inc(used, 2)
                pe.wait_ge(loaded, 32)

                def flip(g, parity):
                    pe.wait_ge(staged, g + 1)
                    pe.wait_ge(copied, g + 1)
                    turn(pe, c, rows[:, parity].rearrange("p t d -> p (t d)"), parity).then_inc(turned, 1)
                flip(0, 0)

                def body(g, parity, last):
                    if not last:
                        flip(g + 1, 1 - parity)
                    pe.wait_ge(copied, g + 3)
                    pe.wait_ge(out_done, g + 1)
                    for u in range(2):
                        for k in range(2):
                            to = (2 + parity) * 512 + u * D
                            x = rows_t[:, parity, k * 2 * P + u * P:k * 2 * P + u * P + P]
                            mm = pe.matmul(c.ps[:, to:to + D], x, w[:, k, :], start=(k == 0), stop=(k == 1))
                    mm.then_inc(used, 1)
                groups(pe, body)

            @block.vector
            def _(v):
                v.sem_inc(out_done, 2)

                def norm(g, parity):
                    sums = c.rows_b[:, bass.ds(g * 2 * SUMW, 2 * SUMW)].rearrange("p (t n) -> p t n", t=2)
                    v.tensor_scalar(inv[:, parity], sums[:, :, D:SUMW], 1e-9, None, ALU.add).then_inc(step, 1)
                    v.wait_ge(step, g * 2 + 1)
                    v.reciprocal(inv[:, parity], inv[:, parity]).then_inc(step, 1)
                    v.wait_ge(step, g * 2 + 2)
                    v.wait_ge(turned, g + 1)
                    v.tensor_tensor(rows[:, parity].rearrange("p t (h k) -> p t h k", k=DK),
                                    sums[:, :, 0:D].rearrange("p t (h k) -> p t h k", k=DK),
                                    bc(inv[:, parity].unsqueeze(3), [P, 2, H, DK]), ALU.mult).then_inc(staged, 1)
                norm(0, 0)
                v.wait_ge(loaded, 32)

                def body(g, parity, last):
                    if not last:
                        norm(g + 1, 1 - parity)
                    v.wait_ge(used, g + 3)
                    to = c.rows_a[:, bass.ds(g * 2 * D, 2 * D)]
                    v.tensor_tensor(to, to, c.ps[:, (2 + parity) * 512:(2 + parity) * 512 + 512], ALU.add).then_inc(out_done, 1)
                groups(v, body)
                v.wait_ge(out_done, GROUPS2 + 2)


def affine(c, gamma, beta, name, add_to=None):
    nc = c.nc
    gb, bb = c.scores[:, 0:D], c.scores[:, D:2 * D]
    with Semaphores(nc) as s:
        loaded, step = s.sem(f"{name}_loaded"), s.sem(f"{name}_step")
        with nc.Block() as block:
            @block.sync
            def _(sp):
                sp.dma_start(gb, row_bc(gamma)).then_inc(loaded, 16)
                sp.dma_start(bb, row_bc(beta)).then_inc(loaded, 16)

            @block.vector
            def _(v):
                do = Chain(v, step)
                v.wait_ge(loaded, 32)
                r = rows3(c.rows_a)
                do(v.tensor_tensor(r, r, bc(gb.unsqueeze(1), [P, NT, D]), ALU.mult))
                do(v.tensor_tensor(r, r, bc(bb.unsqueeze(1), [P, NT, D]), ALU.add))
                if add_to is not None:
                    do(v.tensor_tensor(rows3(add_to), rows3(add_to), r, ALU.add))


class FfnRoom:

    def __init__(self, c):
        sc = c.scores
        self.w1 = sc[:, 0:2048].rearrange("p (k n) -> p k n", k=2)
        self.w2 = sc[:, 2048:4096].rearrange("p (k n) -> p k n", k=8)
        self.rows = [sc[:, 4096 + k * 512:4608 + k * 512] for k in range(2)]
        self.rows_t = sc[:, 5120:6144].rearrange("p (b n) -> p b n", b=2)
        self.b1 = sc[:, 6144:6152]
        self.b2 = sc[:, 6152:6152 + D]
        self.hid = c.rows_b[:, 0:4096].rearrange("p (b k n) -> p b k n", b=2, k=8)


def ffn(c, room, func, target, name, load=None):
    nc = c.nc
    K2 = HID // P
    with Semaphores(nc) as s:
        def sem(n):
            return s.sem(f"{name}_{n}")
        loaded, chunk, acted, summed, out_done = sem("loaded"), sem("chunk"), sem("acted"), sem("summed"), sem("out_done")
        step, zeroed = sem("step"), sem("zeroed")
        f = Front(c, s, name, room.rows, room.rows_t, c.rows_a)
        with nc.Block() as block:
            if load:
                @block.sync
                def _(sp):
                    load(sp, loaded, zeroed)

            @block.scalar
            def _(a):
                a.sem_inc(acted, 4)
                if load:
                    a.wait_ge(loaded, 96)
                f.stage(a, 0, 0)

                def body(g, parity, last):
                    if not last:
                        f.stage(a, g + 1, 1 - parity)
                    a.wait_ge(summed, g + 1)
                    for k in range(K2):
                        a.wait_ge(chunk, g * K2 + k + 1)
                        at = (2 + k % 4) * 512
                        a.activation(room.hid[:, parity, k, :], c.ps[:, at:at + 2 * P], func,
                                     bias=room.b1[:, k:k + 1]).then_inc(acted, 1)
                groups(a, body)

            @block.tensor
            def _(pe):
                f.start_pe(pe)
                pe.sem_inc(summed, 2)
                if load:
                    pe.wait_ge(loaded, 96)
                f.turn(pe, 0, 0)

                def body(g, parity, last):
                    if not last:
                        f.turn(pe, g + 1, 1 - parity)
                    pe.wait_ge(f.copied, g + 3)
                    for n in range(K2):
                        pe.wait_ge(acted, g * K2 + n + 1)
                        at = (2 + n % 4) * 512
                        for k in range(2):
                            mm = pe.matmul(c.ps[:, at:at + 2 * P], room.w1[:, k, n * P:(n + 1) * P],
                                           room.rows_t[:, parity, k * 2 * P:(k + 1) * 2 * P], start=(k == 0), stop=(k == 1))
                        mm.then_inc(chunk, 1)
                    pe.wait_ge(out_done, g + 1)
                    for u in range(2):
                        at = (6 + parity) * 512 + u * D
                        for n in range(K2):
                            if u == 0:
                                pe.wait_ge(acted, g * K2 + n + 5)
                            mm = pe.matmul(c.ps[:, at:at + D], room.hid[:, parity, n, u * P:(u + 1) * P], room.w2[:, n, :],
                                           start=(n == 0), stop=(n == K2 - 1))
                            if u == 0 and n == 0:
                                mm.then_inc(f.used, 1)
                    mm.then_inc(summed, 1)
                groups(pe, body)

            @block.vector
            def _(v):
                do = Chain(v, step)
                f.start_vector(v)
                v.sem_inc(out_done, 2)
                if load:
                    v.memset(c.rows_c[:, FULL_ROWS // P * D:NT * D], 0.0).then_inc(zeroed, 1)
                    v.wait_ge(loaded, 96)
                f.copy(v, 0, 0)

                def body(g, parity, last):
                    if not last:
                        f.copy(v, g + 1, 1 - parity)
                    v.wait_ge(summed, g + 3)
                    v.wait_ge(f.turned, g + 3)
                    to = target[:, bass.ds(g * 2 * D, 2 * D)]
                    v.tensor_tensor(to, to, c.ps[:, (6 + parity) * 512:(7 + parity) * 512], ALU.add).then_inc(out_done, 1)
                groups(v, body)
                v.wait_ge(out_done, GROUPS2 + 2)
                t = rows3(target)
                do(v.tensor_tensor(t, t, bc(room.b2.unsqueeze(1), [P, NT, D]), ALU.add))


def load_ffn(c, room, x, w1, b1, w2, b2):
    def load(sp, loaded, zeroed):
        nc = c.nc
        sp.dma_start(room.w1, w1.rearrange("(k p) n -> p k n", p=P)).then_inc(loaded, 16)
        sp.dma_start(room.w2, w2.rearrange("(k p) n -> p k n", p=P)).then_inc(loaded, 16)
        with nc.allow_non_contiguous_dma("a bias, one number a partition"):
            sp.dma_start(room.b1, b1.rearrange("(k p) -> p k", p=P)).then_inc(loaded, 16)
        sp.dma_start(room.b2, row_bc(b2)).then_inc(loaded, 16)
        sp.wait_ge(zeroed, 1)
        rows = rows3(c.rows_c)
        sp.dma_start(rows[:, 0:FULL_ROWS // P, :], x[0:FULL_ROWS, :].rearrange("(t p) d -> p t d", p=P)).then_inc(loaded, 16)
        sp.dma_start(rows[0:LAST_ROWS, FULL_ROWS // P, :], x[FULL_ROWS:N, :]).then_inc(loaded, 16)
    return load


def route_all(c, room, wr, br, w1, b1, w2, b2):
    nc = c.nc
    capacity = float(-(-int(N * 1.25) // NE)) if (N * 1.25) == int(N * 1.25) else float(-(-(N * 5) // (NE * 4)))
    o = [0]

    def take(n, dt=F32):
        a = c.rows_b[:, o[0]:o[0] + n]
        o[0] += n
        return a if dt == F32 else a.bitcast(dt)
    total, wr_sb, br_sb, ones = take(D), take(2 * NE).rearrange("p (k n) -> p k n", k=2), take(NE), take(1)
    mean_t, wide = take(2), take(2 * P).rearrange("p (k n) -> p k n", k=2)
    lg, t8, m8, p8, one = take(NE), take(NE), take(NE), take(NE), take(1)
    best, best_i, best_f = take(8), take(8, U32), take(8)
    weight = take(2)
    row_no = take(4)
    idx1 = take(4).rearrange("p (j k) -> p j k", j=2)
    idx2 = take(8).rearrange("p (j k) -> p j k", j=2)
    idx1u, idx2u = take(4, U32).rearrange("p (j k) -> p j k", j=2), take(8, U32).rearrange("p (j k) -> p j k", j=2)
    b2_rows = take(2 * D).rearrange("p (j n) -> p j n", j=2)
    with Semaphores(nc) as s:
        def sem(n):
            return s.sem(f"route_{n}")
        loaded, step, total_ready, mean_ps, wide_ready = sem("loaded"), sem("step"), sem("total"), sem("mean"), sem("wide")
        logits_ps, ask, exped, idx_ready, landed, rowno = sem("logits"), sem("ask"), sem("exped"), sem("idx"), sem("landed"), sem("rowno")
        with nc.Block() as block:
            @block.sync
            def _(sp):
                sp.dma_start(wr_sb, wr.rearrange("(k p) n -> p k n", p=P)).then_inc(loaded, 16)
                sp.dma_start(br_sb, row_bc(br)).then_inc(loaded, 16)

            @block.gpsimd
            def _(pool):
                pool.iota(row_no, [[P, 4]], base=0, channel_multiplier=1, allow_small_or_imprecise_dtypes=True).then_inc(rowno, 1)
                pool.wait_ge(idx_ready, 1)
                w1_rows, w2_rows = w1.rearrange("e d n -> (e d) n"), w2.rearrange("e n d -> (e n) d")
                b1_rows = b1.rearrange("e (n a) -> (e n) a", a=1)

                def fetch(to, table, idx):
                    pool.indirect_dma_start(to, None, table, bass.IndirectOffsetOnAxis(ap=idx, axis=0)).then_inc(landed, 16)
                for j in range(2):
                    for k in range(2):
                        fetch(room.w1[:, k, j * HE:(j + 1) * HE], w1_rows, idx1u[:, j, k:k + 1])
                    for k in range(4):
                        fetch(room.w2[:, j * 4 + k, :], w2_rows, idx2u[:, j, k:k + 1])
                        fetch(room.b1[:, j * 4 + k:j * 4 + k + 1], b1_rows, idx2u[:, j, k:k + 1])
                    fetch(b2_rows[:, j, :], b2, best_i[:, j:j + 1])

            @block.tensor
            def _(pe):
                pe.wait_ge(total_ready, 1)
                for k in range(2):
                    mm = pe.matmul(c.ps[:, k:k + 1], total[:, k * P:(k + 1) * P], ones, start=True, stop=True)
                mm.then_inc(mean_ps, 1)
                pe.wait_ge(wide_ready, 1)
                pe.wait_ge(loaded, 32)
                for k in range(2):
                    mm = pe.matmul(c.ps[:, 512:512 + NE], wide[:, k, :], wr_sb[:, k, :], start=(k == 0), stop=(k == 1))
                mm.then_inc(logits_ps, 1)

            @block.scalar
            def _(a):
                for n, x in enumerate((lg, p8, weight[:, 1:2])):
                    a.wait_ge(ask, n + 1)
                    a.activation(x, x, ACT.Exp).then_inc(exped, 1)

            @block.vector
            def _(v):
                do = Chain(v, step)
                do(v.memset(ones, 1.0))
                do(v.tensor_reduce(total, c.rows_a[:, 0:FULL_ROWS // P * D].rearrange("p (t d) -> p d t", d=D), AX.X, ALU.add))
                last = FULL_ROWS // P * D
                do(v.tensor_tensor(total[0:LAST_ROWS], total[0:LAST_ROWS], c.rows_a[0:LAST_ROWS, last:last + D], ALU.add))
                v.sem_inc(total_ready, 1)
                v.wait_ge(mean_ps, 1)
                do(v.tensor_scalar(mean_t, c.ps[:, 0:2], 1.0 / N, None, ALU.mult))
                do(v.tensor_copy(wide, bc(mean_t.unsqueeze(2), [P, 2, P])))
                v.sem_inc(wide_ready, 1)
                v.wait_ge(logits_ps, 1)
                do(v.tensor_tensor(lg, c.ps[:, 512:512 + NE], br_sb, ALU.add))

                def softmax(x, n):
                    do(v.tensor_reduce(one, x, AX.X, ALU.max))
                    do(v.tensor_scalar(x, x, one, None, ALU.subtract))
                    v.sem_inc(ask, 1)
                    v.wait_ge(exped, n)
                    do(v.tensor_reduce(one, x, AX.X, ALU.add))
                    do(v.reciprocal(one, one))
                    do(v.tensor_scalar(x, x, one, None, ALU.mult))
                softmax(lg, 1)
                do(v.tensor_scalar(t8, lg, float(N), capacity, ALU.mult, ALU.max))
                do(v.reciprocal(t8, t8))
                do(v.tensor_scalar(t8, t8, capacity, None, ALU.mult))
                do(v.tensor_tensor(p8, lg, t8, ALU.mult))
                softmax(p8, 2)
                do(v.max(best, p8))
                do(v.max_index(best_i, best, p8))
                do(v.tensor_copy(best_f, best_i))
                do(v.tensor_tensor(weight[:, 1:2], best[:, 1:2], best[:, 0:1], ALU.subtract))
                v.sem_inc(ask, 1)
                v.wait_ge(rowno, 1)
                for j in range(2):
                    do(v.tensor_scalar(one, best_f[:, j:j + 1], float(D), None, ALU.mult))
                    do(v.tensor_scalar(idx1[:, j], row_no[:, 0:2], one, None, ALU.add))
                    do(v.tensor_scalar(one, best_f[:, j:j + 1], float(HE), None, ALU.mult))
                    do(v.tensor_scalar(idx2[:, j], row_no, one, None, ALU.add))
                do(v.tensor_copy(idx1u, idx1))
                do(v.tensor_copy(idx2u, idx2))
                v.sem_inc(idx_ready, 1)
                v.wait_ge(exped, 3)
                do(v.tensor_scalar(one, weight[:, 1:2], 1.0, None, ALU.add))
                do(v.reciprocal(weight[:, 0:1], one))
                do(v.tensor_tensor(weight[:, 1:2], weight[:, 1:2], weight[:, 0:1], ALU.mult))
                v.wait_ge(landed, 22 * 16)
                for j in range(2):
                    r = room.w2[:, j * 4:j * 4 + 4, :]
                    do(v.tensor_scalar(r, r, weight[:, j:j + 1], None, ALU.mult))
                    do(v.tensor_scalar(b2_rows[:, j], b2_rows[:, j], weight[:, j:j + 1], None, ALU.mult))
                do(v.tensor_tensor(room.b2, b2_rows[:, 0], b2_rows[:, 1], ALU.add))


def sage_products(c, w_self, w_neigh):
    nc = c.nc
    w = c.scores[:, 0:1024].rearrange("p (k n) -> p k n", k=2)
    rows = [c.scores[:, 1024 + k * 512:1536 + k * 512] for k in range(2)]
    rows_t = c.scores[:, 2048:3072].rearrange("p (b n) -> p b n", b=2)
    neigh = c.scores[:, 3072:4096].rearrange("p (b n) -> p b n", b=4)
    left = c.scores[:, 4096:5120].rearrange("p (b n) -> p b n", b=4)
    top = c.scores[:, 5120:5128]
    NEG = -3.0e38
    with Semaphores(nc) as s:
        def sem(n):
            return s.sem(f"sage_{n}")
        loaded, out_done, ready, step, neigh_out = sem("loaded"), sem("out_done"), sem("ready"), sem("step"), sem("neigh_out")
        stored, buf_free, gate = [sem(f"stored{u}") for u in range(4)], sem("buf_free"), sem("gate")
        f = Front(c, s, "sage", rows, rows_t, c.rows_a)
        with nc.Block() as block:
            @block.sync
            def _(sp):
                sp.dma_start(w[:, :, 0:D], w_self.rearrange("(k p) n -> p k n", p=P)).then_inc(loaded, 16)
                sp.dma_start(w[:, :, D:2 * D], w_neigh.rearrange("(k p) n -> p k n", p=P)).then_inc(loaded, 16)

                def body(g, parity, last):
                    for u in range(2):
                        b = 2 * parity + u
                        sp.wait_ge(ready, g * 2 + u + 1)
                        sp.dma_start(c.k_dram[bass.ds(g * 2 * P + u * P, P), :], left[:, b, :]).then_inc(stored[b], 16)
                    for u in range(2):
                        sp.wait_ge(stored[2 * parity + u], (g - parity) * 8 + 16)
                        sp.sem_inc(buf_free, 1)
                groups(sp, body)

            @block.scalar
            def _(a):
                a.sem_inc(neigh_out, 4)
                f.stage(a, 0, 0)

                def body(g, parity, last):
                    if not last:
                        f.stage(a, g + 1, 1 - parity)
                    a.wait_ge(f.used, g + 3)
                    for u in range(2):
                        b = 2 * parity + u
                        a.wait_ge(buf_free, g * 2 + u + 1)
                        at = (4 + parity) * 512 + u * D
                        a.activation(neigh[:, b, :], c.ps[:, at:at + D], ACT.Copy).then_inc(neigh_out, 1)
                groups(a, body)

            @block.tensor
            def _(pe):
                f.start_pe(pe)
                pe.wait_ge(loaded, 32)
                f.turn(pe, 0, 0)

                def body(g, parity, last):
                    if not last:
                        f.turn(pe, g + 1, 1 - parity)
                    pe.wait_ge(f.copied, g + 3)
                    pe.wait_ge(out_done, g + 1)
                    pe.wait_ge(neigh_out, g * 2 + 2)
                    for u in range(2):
                        for half in range(2):
                            at = (2 + 2 * half + parity) * 512 + u * D
                            for k in range(2):
                                x = rows_t[:, parity, k * 2 * P + u * P:k * 2 * P + u * P + P]
                                mm = pe.matmul(c.ps[:, at:at + D], x, w[:, k, half * D:(half + 1) * D],
                                               start=(k == 0), stop=(k == 1))
                    mm.then_inc(f.used, 1)
                groups(pe, body)

            @block.vector
            def _(v):
                f.start_vector(v)
                v.sem_inc(out_done, 2)
                v.sem_inc(buf_free, 4)
                f.copy(v, 0, 0)
                STEPS = 8

                def body(g, parity, last):
                    if not last:
                        f.copy(v, g + 1, 1 - parity)
                    v.wait_ge(f.used, g + 3)
                    to = c.rows_c[:, bass.ds(g * 2 * D, 2 * D)]
                    v.tensor_tensor(to, to, c.ps[:, (2 + parity) * 512:(3 + parity) * 512], ALU.add).then_inc(out_done, 1)
                    for u in range(2):
                        b = 2 * parity + u
                        v.wait_ge(neigh_out, g * 2 + u + 5)
                        for r in range(4):
                            n = g * 2 * STEPS + u * STEPS + 2 * r
                            src = neigh[:, b, :] if r == 0 else left[:, b, :]
                            v.sem_inc(gate, 1)
                            v.max(top, src).then_inc(step, 1)
                            v.wait_ge(step, n + 1)
                            v.sem_inc(gate, 1)
                            v.match_replace(left[:, b, :], top, src, NEG).then_inc(step, 1)
                            v.wait_ge(step, n + 2)
                        v.scalar_tensor_tensor(left[:, b, :], left[:, b, :], NEG, neigh[:, b, :], ALU.is_equal,
                                               ALU.mult).then_inc(ready, 1)
                groups(v, body)
                v.wait_ge(ready, NT)


def add_neighbours(c):
    nc = c.nc
    sums = c.rows_b[:, 0:NT * SUMW].rearrange("p (t n) -> p t n", t=NT)
    inv = c.small[:, 0:NT]
    with Semaphores(nc) as s:
        step = s.sem("neigh_step")
        with nc.Block() as block:
            @block.vector
            def _(v):
                do = Chain(v, step)
                do(v.tensor_scalar(inv, sums[:, :, D], 1.0, None, ALU.max))
                do(v.reciprocal(inv, inv))
                do(v.tensor_tensor(sums[:, :, 0:D], sums[:, :, 0:D], bc(inv.unsqueeze(2), [P, NT, D]), ALU.mult))
                do(v.tensor_tensor(rows3(c.rows_c), rows3(c.rows_c), sums[:, :, 0:D], ALU.add))


def token_routes(c, gates, wr, br, b2, w1):
    nc = c.nc
    wr_sb = c.scores[:, 0:16].rearrange("p (k n) -> p k n", k=2)
    br_sb = c.scores[:, 16:24]
    lg = c.scores[:, 24:56].rearrange("p (b t n) -> p b t n", b=2, t=2)
    mx = c.scores[:, 56:88].rearrange("p (b t n) -> p b t n", b=2, t=2)
    mi = c.scores[:, 88:120].bitcast(U32).rearrange("p (b t n) -> p b t n", b=2, t=2)
    rows = [c.scores[:, 128 + k * 512:640 + k * 512] for k in range(2)]
    rows_t = c.scores[:, 1152:2176].rearrange("p (b n) -> p b n", b=2)
    iota8 = c.scores[:, 2176:2184]
    val = c.scores[:, 2184:2184 + 2 * NT].rearrange("p (t n) -> p t n", n=2)
    sel = c.scores[:, 2284:2284 + 2 * NT].rearrange("p (t n) -> p t n", n=2)
    w0, w1_ = c.small[:, 0:NT], c.small[:, NT:2 * NT]
    pick = c.scores[:, 2384:2384 + NT * NE].rearrange("p (t n) -> p t n", n=NE)
    b2_sb = c.scores[0:NE, 2784:2784 + D]
    g_buf = c.scores[:, 3040:3072].rearrange("p (b t n) -> p b t n", b=2, t=2)
    g_t = c.scores[0:NE, 3072:3072 + 512].rearrange("p (b n) -> p b n", b=2)
    g3 = gates.rearrange("p (t n) -> p t n", n=NE)
    at = [3584]

    def take(size, shape=None, **k):
        a = c.scores[:, at[0]:at[0] + size]
        at[0] += size
        return a.rearrange(shape, **k) if shape else a
    hot = [take(NT * NE, "p (t n) -> p t n", n=NE) for _ in range(2)]
    chosen = take(NT * NE)
    before = take(P)
    ones = take(P)
    real = take(NT)
    per_tile = take(NT * NE, "p (n t) -> p n t", n=NE)
    upto = take(NT * NE, "p (n t) -> p n t", n=NE)
    n_rows, n_tiles, start, tiles_to = (take(NE) for _ in range(4))
    limit = c.small[:, 3 * NT:4 * NT]
    slot_no = c.stats[:, 0:SLOT_TILES]
    ended = c.rows_b[:, 8192:8192 + SLOT_TILES * NE].rearrange("p (s n) -> p s n", n=NE)
    wider = c.rows_b[:, 9216:9216 + NT * NE].rearrange("p (n t) -> p n t", n=NE)
    expert_f = c.rows_b[:, 9728:9728 + SLOT_TILES]
    place_f = c.rows_b[:, 9856:9856 + NT]
    assert at[0] <= (ITEMS + 16) * H
    with Semaphores(nc) as s:
        def sem(n):
            return s.sem(f"tok_{n}")
        loaded, iotas, lg_done, step, kept = sem("loaded"), sem("iotas"), sem("lg_done"), sem("step"), sem("kept")
        gate = sem("gate")
        ranked, marked, w_loaded = sem("ranked"), sem("marked"), sem("w_loaded")
        s1, ask, exped = sem("s1"), sem("ask"), sem("exped")
        gated, g_staged, g_turned, g_copied, b_summed, b_added = (sem(n) for n in ("gated", "gs", "gt", "gc", "bs", "ba"))
        f = Front(c, s, "tok", rows, rows_t, c.rows_a)
        with nc.Block() as block:
            @block.sync
            def _(sp):
                sp.dma_start(wr_sb, wr.rearrange("(k p) n -> p k n", p=P)).then_inc(loaded, 16)
                sp.dma_start(br_sb, row_bc(br)).then_inc(loaded, 16)
                sp.dma_start(b2_sb, b2).then_inc(loaded, 16)
                sp.dma_start(c.rows_b[:, 0:NE * 2 * HE].rearrange("p (e k n) -> p e k n", e=NE, k=2),
                             w1.rearrange("e (k p) n -> p e k n", p=P)).then_inc(w_loaded, 16)
                sp.wait_ge(w_loaded, 16)

            @block.gpsimd
            def _(pool):
                pool.iota(real, [[P, NT]], base=0, channel_multiplier=1, allow_small_or_imprecise_dtypes=True).then_inc(iotas, 1)
                pool.iota(limit, [[P, NT]], base=0, channel_multiplier=0, allow_small_or_imprecise_dtypes=True).then_inc(iotas, 1)
                pool.iota(slot_no, [[1, SLOT_TILES]], base=0, channel_multiplier=0,
                          allow_small_or_imprecise_dtypes=True).then_inc(iotas, 1)
                pool.iota(iota8, [[1, NE]], base=0, channel_multiplier=0, allow_small_or_imprecise_dtypes=True).then_inc(iotas, 1)

            @block.scalar
            def _(a):
                groups(a, lambda g, parity, last: f.stage(a, g, parity))
                a.wait_ge(ask, 1)
                a.activation(w1_, w1_, ACT.Exp).then_inc(exped, 1)
                a.wait_ge(gated, 1)

                def stage(g, parity, last):
                    a.wait_ge(g_turned, g + 1)
                    a.activation(g_buf[:, parity], gates[:, bass.ds(g * 2 * NE, 2 * NE)].rearrange("p (t n) -> p t n", n=NE),
                                 ACT.Copy).then_inc(g_staged, 1)
                groups(a, stage)

            @block.tensor
            def _(pe):
                f.start_pe(pe)
                pe.sem_inc(g_turned, 2)
                pe.sem_inc(b_summed, 2)
                pe.wait_ge(loaded, 48)
                f.turn(pe, 0, 0)

                def body(g, parity, last):
                    if not last:
                        f.turn(pe, g + 1, 1 - parity)
                    pe.wait_ge(f.copied, g + 3)
                    pe.wait_ge(lg_done, g + 1)
                    for u in range(2):
                        at = (2 + parity) * 512 + u * NE
                        for k in range(2):
                            x = rows_t[:, parity, k * 2 * P + u * P:k * 2 * P + u * P + P]
                            mm = pe.matmul(c.ps[:, at:at + NE], x, wr_sb[:, k, :], start=(k == 0), stop=(k == 1))
                    mm.then_inc(f.used, 1)
                groups(pe, body)

                pe.wait_ge(marked, 1)
                pe.matmul(c.ps[:, 1024:1024 + NT * NE], before, chosen, start=True, stop=True)
                pe.matmul(c.ps[:, 1536:1536 + NT * NE], ones, chosen, start=True, stop=True).then_inc(ranked, 1)

                def bias(g, parity, last):
                    pe.wait_ge(g_staged, g + 1)
                    pe.wait_ge(g_copied, g + 1)
                    for u in range(2):
                        at = (4 + parity) * 512 + u * P
                        mm = pe.transpose(c.ps[0:NE, at:at + P], g_buf[:, parity, u, :], c.ident[:, :])
                    mm.then_inc(g_turned, 1)
                    pe.wait_ge(g_copied, g + 3)
                    pe.wait_ge(b_added, g + 1)
                    for u in range(2):
                        at = (6 + parity) * 512 + u * D
                        mm = pe.matmul(c.ps[:, at:at + D], g_t[:, parity, u * P:(u + 1) * P], b2_sb, start=True, stop=True)
                    mm.then_inc(b_summed, 1)
                groups(pe, bias)

            @block.vector
            def _(v):
                do = Chain(v, step)
                f.start_vector(v)
                v.sem_inc(lg_done, 2)
                v.sem_inc(g_copied, 2)
                v.sem_inc(b_added, 2)
                v.wait_ge(loaded, 48)
                v.wait_ge(iotas, 4)
                f.copy(v, 0, 0)
                S1 = 6

                def body(g, parity, last):
                    if not last:
                        f.copy(v, g + 1, 1 - parity)
                    v.wait_ge(f.used, g + 3)
                    at = (2 + parity) * 512
                    v.tensor_tensor(lg[:, parity], c.ps[:, at:at + 2 * NE].rearrange("p (t n) -> p t n", t=2),
                                    bc(br_sb.unsqueeze(1), [P, 2, NE]), ALU.add).then_inc(lg_done, 1)
                    v.wait_ge(lg_done, g + 3)
                    v.sem_inc(gate, 1)
                    for u in range(2):
                        v.max(mx[:, parity, u, :], lg[:, parity, u, :]).then_inc(s1, 1)
                    v.wait_ge(s1, g * S1 + 2)
                    v.sem_inc(gate, 1)
                    for u in range(2):
                        v.max_index(mi[:, parity, u, :], mx[:, parity, u, :], lg[:, parity, u, :]).then_inc(s1, 1)
                    v.wait_ge(s1, g * S1 + 4)
                    v.tensor_copy(val[:, bass.ds(g * 2, 2), :], mx[:, parity, :, 0:2]).then_inc(s1, 1)
                    v.tensor_copy(sel[:, bass.ds(g * 2, 2), :], mi[:, parity, :, 0:2]).then_inc(s1, 1)
                groups(v, body)
                v.wait_ge(s1, GROUPS2 * S1)
                do(v.tensor_tensor(w1_, val[:, :, 1], val[:, :, 0], ALU.subtract))
                v.sem_inc(ask, 1)
                v.wait_ge(exped, 1)
                do(v.tensor_scalar(w0, w1_, 1.0, None, ALU.add))
                do(v.reciprocal(w0, w0))
                do(v.tensor_tensor(w1_, w1_, w0, ALU.mult))
                wide8 = bc(iota8.unsqueeze(1), [P, NT, NE])
                for j in range(2):
                    do(v.tensor_tensor(hot[j], wide8, bc(sel[:, :, j:j + 1], [P, NT, NE]), ALU.is_equal))
                do(v.tensor_scalar(real, real, float(N), None, ALU.is_lt))
                chosen3 = chosen.rearrange("p (t n) -> p t n", n=NE)
                do(v.tensor_tensor(chosen3, hot[0], hot[1], ALU.add))
                do(v.tensor_tensor(chosen3, chosen3, bc(real.unsqueeze(2), [P, NT, NE]), ALU.mult))
                do(v.tensor_scalar(before, c.iota_n[:, :], c.iota_p[:, 0:1], None, ALU.is_gt))
                do(v.memset(ones, 1.0))
                v.sem_inc(marked, 1)
                do(v.tensor_tensor(g3, hot[0], bc(w0.unsqueeze(2), [P, NT, NE]), ALU.mult))
                do(v.tensor_tensor(pick, hot[1], bc(w1_.unsqueeze(2), [P, NT, NE]), ALU.mult))
                do(v.tensor_tensor(g3, g3, pick, ALU.add))
                v.sem_inc(gated, 1)

                def bias(g, parity, last):
                    v.wait_ge(g_turned, g + 3)
                    v.wait_ge(b_summed, g + 1)
                    at = (4 + parity) * 512
                    v.tensor_copy(g_t[:, parity, :], c.ps[0:NE, at:at + 2 * P]).then_inc(g_copied, 1)
                    v.wait_ge(b_summed, g + 3)
                    to = c.rows_c[:, bass.ds(g * 2 * D, 2 * D)]
                    v.tensor_tensor(to, to, c.ps[:, (6 + parity) * 512:(7 + parity) * 512], ALU.add).then_inc(b_added, 1)
                groups(v, bias)
                v.wait_ge(b_added, GROUPS2 + 2)

                v.wait_ge(ranked, 1)
                flat = upto.rearrange("p n t -> p (n t)")
                do(v.tensor_copy(per_tile, c.ps[:, 1536:1536 + NT * NE].rearrange("p (t n) -> p n t", n=NE)))
                do(v.memset(wider, 1.0))
                do(v.tensor_tensor_scan(flat, wider.rearrange("p n t -> p (n t)"), per_tile.rearrange("p n t -> p (n t)"),
                                        0.0, ALU.mult, ALU.add))
                do(v.tensor_copy(n_rows, upto[:, :, NT - 1]))
                do(v.tensor_tensor(upto, upto, per_tile, ALU.subtract))
                do(v.memset(start, 0.0))
                do(v.tensor_copy(start[:, 1:], n_rows[:, :NE - 1]))
                do(v.tensor_tensor(n_rows, n_rows, start, ALU.subtract))
                do(v.tensor_tensor(upto, upto, bc(start.unsqueeze(2), [P, NE, NT]), ALU.subtract))
                do(v.tensor_tensor(wider, bc(n_rows.unsqueeze(2), [P, NE, NT]), bc(limit.unsqueeze(1), [P, NE, NT]), ALU.is_gt))
                do(v.tensor_reduce(n_tiles, wider, AX.X, ALU.add))
                do(v.tensor_tensor_scan(tiles_to, ones[:, 0:NE], n_tiles, 0.0, ALU.mult, ALU.add))
                do(v.tensor_tensor(start, tiles_to, n_tiles, ALU.subtract))
                do(v.tensor_scalar(start, start, float(P), None, ALU.mult))
                do(v.tensor_tensor(upto, upto, bc(start.unsqueeze(2), [P, NE, NT]), ALU.add))
                do(v.tensor_tensor(chosen3, c.ps[:, 1024:1024 + NT * NE].rearrange("p (t n) -> p t n", n=NE),
                                   upto.rearrange("p n t -> p t n"), ALU.add))
                place = c.slots[:, :].rearrange("p (t j) -> p t j", j=2)
                for j in range(2):
                    do(v.tensor_tensor(hot[j], hot[j], chosen3, ALU.mult))
                    do(v.tensor_reduce(place_f, hot[j], AX.X, ALU.add))
                    do(v.tensor_copy(place[:, :, j], place_f))
                do(v.tensor_tensor(ended, bc(tiles_to.unsqueeze(1), [P, SLOT_TILES, NE]),
                                   bc(slot_no.unsqueeze(2), [P, SLOT_TILES, NE]), ALU.is_le))
                do(v.tensor_reduce(expert_f, ended, AX.X, ALU.add))
                do(v.tensor_scalar(expert_f, expert_f, float(NE - 1), None, ALU.min))
                do(v.tensor_copy(c.slot_expert[:, :], expert_f[0:1]))


def dispatch(c):
    nc = c.nc
    rows = [c.scores[:, k * 512:(k + 1) * 512] for k in range(2)]
    with Semaphores(nc) as s:
        staged, idx_ready, gate, sent = s.sem("disp_staged"), s.sem("disp_idx"), s.sem("disp_gate"), s.sem("disp_free")
        landed = [s.sem(f"disp_landed{u}") for u in range(2)]
        idx = s.enter_context(nc.sbuf_tensor("disp_idx_buf", [P, 8], U32))
        with nc.Block() as block:
            @block.scalar
            def _(a):
                def body(g, parity, last):
                    a.wait_ge(sent, g + 1)
                    a.activation(rows[parity], c.rows_a[:, bass.ds(g * 2 * D, 2 * D)], ACT.Copy).then_inc(staged, 1)
                groups(a, body)

            @block.gpsimd
            def _(pool):
                def body(g, parity, last):
                    pool.wait_ge(sent, g + 1)
                    pool.sem_inc(gate, 1)
                    pool.tensor_copy(idx[:, parity * 4:parity * 4 + 4], c.slots[:, bass.ds(g * 4, 4)]).then_inc(idx_ready, 1)
                    pool.wait_ge(idx_ready, g + 1)
                    pool.wait_ge(staged, g + 1)
                    pool.sem_inc(gate, 1)
                    n = LAST_ROWS if last else P
                    for u in range(1 if last else 2):
                        for j in range(2):
                            k = parity * 4 + u * 2 + j
                            pool.indirect_dma_start(c.slot_in[:, :], bass.IndirectOffsetOnAxis(ap=idx[0:n, k:k + 1], axis=0),
                                                    rows[parity][0:n, u * D:(u + 1) * D], None).then_inc(landed[parity], 16)
                groups(pool, body)

            @block.sync
            def _(sp):
                sp.sem_inc(sent, 2)

                def body(g, parity, last):
                    if last:
                        sp.wait_ge(landed[parity], (g - parity) * 32 + 32)
                    else:
                        sp.wait_ge(landed[parity], (g - parity) * 32 + 64)
                    sp.sem_inc(sent, 1)
                groups(sp, body)


def expert_rows(c, b1, w2):
    nc = c.nc
    K2 = HE // P
    TB = NE * 2 * HE
    w1_sb, b1_sb = c.rows_b[:, 0:TB], c.rows_b[:, TB:TB + NE * HE]
    w2_sb = c.rows_a[:, 0:NE * K2 * D]
    o = NE * K2 * D
    x_in = c.rows_a[:, o:o + 4 * D].rearrange("p (b n) -> p b n", b=4)
    x_t = c.rows_a[:, o + 1024:o + 1536].rearrange("p (b n) -> p b n", b=2)
    y_out = c.rows_a[:, o + 1536:o + 2560].rearrange("p (b n) -> p b n", b=4)
    hid = c.scores[:, 0:1024].rearrange("p (b n) -> p b n", b=2)
    act = c.scores[:, 1024:2048].rearrange("p (b n) -> p b n", b=2)
    act_t = c.scores[:, 2048:3072].rearrange("p (b n) -> p b n", b=2)
    S = SLOT_TILES
    with Semaphores(nc) as s:
        def sem(n):
            return s.sem(f"exp_{n}")
        w_loaded, in_free = sem("w_loaded"), sem("in_free")
        arrived = [sem(f"arrived{u}") for u in range(4)]
        turned, copied, up, biased, acted, act_turned, act_copied, down, out_ready, out_free = (
            sem(n) for n in ("turned", "copied", "up", "biased", "acted", "act_turned", "act_copied", "down", "out_ready", "out_free"))
        stored = [sem(f"stored{u}") for u in range(4)]

        def expert(eng, t):
            return eng.value_load(c.slot_expert[0:1, bass.ds(t, 1)], min_val=0, max_val=NE - 1)

        def tiles(eng, n, body):
            with eng.Fori(0, S // n) as i:
                for u in range(n):
                    body(i * n + u, u)
            for t in range(S // n * n, S):
                body(t, t % n)
        with nc.Block() as block:
            @block.sync
            def _(sp):
                def body(t, u):
                    sp.wait_ge(turned, t + 1)
                    sp.dma_start(x_in[:, u, :], c.slot_in[bass.ds(t * P, P), :]).then_inc(arrived[u], 16)
                sp.dma_start(w2_sb.rearrange("p (e k n) -> p e k n", e=NE, k=K2),
                             w2.rearrange("e (k p) n -> p e k n", p=P)).then_inc(w_loaded, 16)
                sp.dma_start(b1_sb.rearrange("p (e n) -> p e n", e=NE),
                             b1.rearrange("(a e) n -> a e n", a=1).broadcast_to([P, NE, HE])).then_inc(w_loaded, 16)
                tiles(sp, 4, body)

            @block.scalar
            def _(a):
                a.sem_inc(act_copied, 2)
                a.sem_inc(acted, 2)

                def gelu(t, u):
                    a.wait_ge(act_turned, t + 1)
                    a.wait_ge(biased, t + 3)
                    a.activation(act[:, u, :], hid[:, u, :], ACT.Gelu).then_inc(acted, 1)

                def body(t, u):
                    gelu(t, u)
                    a.wait_ge(down, t + 1)
                    a.wait_ge(act_turned, t + 3)
                    a.activation(act_t[:, u, :], c.ps[:, (4 + u) * 512:(5 + u) * 512], ACT.Copy).then_inc(act_copied, 1)
                tiles(a, 2, body)

            @block.tensor
            def _(pe):
                for x, n in ((turned, 4), (up, 2), (act_turned, 2), (down, 2)):
                    pe.sem_inc(x, n)

                def flip(t, u, slot):
                    pe.wait_ge(arrived[slot], (t - slot) * 4 + 16)
                    pe.wait_ge(copied, t + 1)
                    for k in range(2):
                        mm = pe.transpose(c.ps[:, u * 512 + k * P:u * 512 + (k + 1) * P], x_in[:, slot, k * P:(k + 1) * P], c.ident[:, :])
                    mm.then_inc(turned, 1)

                def first(t, u):
                    e = expert(pe, t)
                    pe.wait_ge(copied, t + 3)
                    pe.wait_ge(biased, t + 1)
                    for k in range(2):
                        mm = pe.matmul(c.ps[:, (2 + u) * 512:(3 + u) * 512], x_t[:, u, k * P:(k + 1) * P],
                                       w1_sb[:, bass.ds(e * 2 * HE + k * HE, HE)], start=(k == 0), stop=(k == 1))
                    mm.then_inc(up, 1)
                    return e

                def second(t, u):
                    pe.wait_ge(acted, t + 3)
                    pe.wait_ge(act_copied, t + 1)
                    for k in range(K2):
                        mm = pe.transpose(c.ps[:, (4 + u) * 512 + k * P:(4 + u) * 512 + (k + 1) * P], act[:, u, k * P:(k + 1) * P], c.ident[:, :])
                    mm.then_inc(act_turned, 1)

                def third(t, u):
                    e = expert(pe, t)
                    pe.wait_ge(act_copied, t + 3)
                    pe.wait_ge(out_ready, t + 1)
                    for k in range(K2):
                        mm = pe.matmul(c.ps[:, (6 + u) * 512:(6 + u) * 512 + D], act_t[:, u, k * P:(k + 1) * P],
                                       w2_sb[:, bass.ds(e * K2 * D + k * D, D)], start=(k == 0), stop=(k == K2 - 1))
                    mm.then_inc(down, 1)
                flip(0, 0, 0)
                first(0, 0)
                flip(1, 1, 1)
                pe.wait_ge(w_loaded, 32)

                def body(t, q, ahead=2):
                    u = q % 2
                    if ahead > 0:
                        first(t + 1, 1 - u)
                    second(t, u)
                    if ahead > 1:
                        flip(t + 2, u, (q + 2) % 4)
                    third(t, u)
                with pe.Fori(0, (S - 2) // 4) as i:
                    for q in range(4):
                        body(i * 4 + q, q)
                for t in range((S - 2) // 4 * 4, S):
                    body(t, t % 4, min(2, S - 1 - t))

            @block.vector
            def _(v):
                for x, n in ((copied, 2), (biased, 2), (out_ready, 2)):
                    v.sem_inc(x, n)

                def copy(t, u):
                    v.wait_ge(up, t + 1)
                    v.wait_ge(turned, t + 5)
                    v.tensor_copy(x_t[:, u, :], c.ps[:, u * 512:u * 512 + D]).then_inc(copied, 1)

                def bias(t, u):
                    e = expert(v, t)
                    v.wait_ge(acted, t + 1)
                    v.wait_ge(up, t + 3)
                    v.tensor_tensor(hid[:, u, :], c.ps[:, (2 + u) * 512:(3 + u) * 512], b1_sb[:, bass.ds(e * HE, HE)],
                                    ALU.add).then_inc(biased, 1)

                def result(t, u, slot):
                    v.wait_ge(out_free, t + 1)
                    v.wait_ge(down, t + 3)
                    v.tensor_copy(y_out[:, slot, :], c.ps[:, (6 + u) * 512:(6 + u) * 512 + D]).then_inc(out_ready, 1)
                v.wait_ge(w_loaded, 32)
                copy(0, 0)
                bias(0, 0)
                copy(1, 1)

                def body(t, q, ahead=2):
                    u = q % 2
                    if ahead > 0:
                        bias(t + 1, 1 - u)
                    if ahead > 1:
                        copy(t + 2, u)
                    result(t, u, q)
                with v.Fori(0, (S - 2) // 4) as i:
                    for q in range(4):
                        body(i * 4 + q, q)
                for t in range((S - 2) // 4 * 4, S):
                    body(t, t % 4, min(2, S - 1 - t))

            @block.gpsimd
            def _(pool):
                pool.sem_inc(out_free, 4)

                def body(t, slot):
                    pool.wait_ge(out_ready, t + 3)
                    pool.sem_inc(in_free, 1)
                    pool.dma_start(c.slot_out[bass.ds(t * P, P), :], y_out[:, slot, :]).then_inc(stored[slot], 16)
                    pool.wait_ge(stored[slot], (t - slot) * 4 + 16)
                    pool.sem_inc(out_free, 1)
                tiles(pool, 4, body)


def combine(c, out):
    nc = c.nc
    RG = 8
    ring = c.scores[:, 0:RG * D].rearrange("p (s d) -> p s d", d=D)
    w0, w1 = c.small[:, 0:NT], c.small[:, NT:2 * NT]
    with Semaphores(nc) as s:
        def sem(n):
            return s.sem(f"comb_{n}")
        idx_ready, gate, added, written = sem("idx"), sem("gate"), sem("added"), sem("written")
        landed = [sem(f"landed{u}") for u in range(RG)]
        idx = s.enter_context(nc.sbuf_tensor("comb_idx_buf", [P, RG], U32))
        with nc.Block() as block:
            @block.gpsimd
            def _(pool):
                def body(g, parity, last):
                    pool.wait_ge(added, g * 4 + 4)
                    pool.sem_inc(gate, 1)
                    pool.tensor_copy(idx[:, parity * 4:parity * 4 + 4], c.slots[:, bass.ds(g * 4, 4)]).then_inc(idx_ready, 1)
                    pool.wait_ge(idx_ready, g + 1)
                    pool.sem_inc(gate, 1)
                    n = LAST_ROWS if last else P
                    for k in range(2 if last else 4):
                        slot = parity * 4 + k
                        pool.indirect_dma_start(ring[0:n, slot, :], None, c.slot_out[:, :],
                                                bass.IndirectOffsetOnAxis(ap=idx[0:n, slot:slot + 1], axis=0)).then_inc(landed[slot], 16)
                groups(pool, body)

            @block.vector
            def _(v):
                v.sem_inc(added, 8)

                def body(g, parity, last):
                    n = LAST_ROWS if last else P
                    for u in range(1 if last else 2):
                        to = c.rows_c[0:n, bass.ds(g * 2 * D + u * D, D)]
                        for j, w in enumerate((w0, w1)):
                            slot = parity * 4 + u * 2 + j
                            v.wait_ge(landed[slot], (g - parity) * 8 + 16)
                            v.wait_ge(added, g * 4 + u * 2 + j + 8)
                            v.scalar_tensor_tensor(to, ring[0:n, slot, :], w[0:n, bass.ds(g * 2 + u, 1)], to,
                                                   ALU.mult, ALU.add).then_inc(added, 1)
                groups(v, body)

            @block.sync
            def _(sp):
                def body(g, parity, last):
                    for u in range(1 if last else 2):
                        sp.wait_ge(added, g * 4 + u * 2 + 10)
                        n = LAST_ROWS if last else P
                        sp.dma_start(out[bass.ds(g * 2 * P + u * P, n), :],
                                     c.rows_c[0:n, bass.ds(g * 2 * D + u * D, D)]).then_inc(written, 16)
                groups(sp, body)
                sp.wait_ge(written, 16 * NODE_TILES)


def build(nc, x, src, dst, L0_gnn_Wq, L0_gnn_Wk, L0_gnn_Wv, L0_gnn_Wo, L0_gnn_ln_g, L0_gnn_ln_b, L0_gnn_w1, L0_gnn_b1,
          L0_gnn_w2, L0_gnn_b2, L0_ffn_Wr, L0_ffn_br, L0_ffn_W1, L0_ffn_b1, L0_ffn_W2, L0_ffn_b2, L0_ffn_gamma,
          L0_ffn_beta, L1_gnn_W_self, L1_gnn_W_neigh, L1_ffn_gamma, L1_ffn_beta, L1_ffn_Wr, L1_ffn_br, L1_ffn_W1,
          L1_ffn_b1, L1_ffn_W2, L1_ffn_b2, out, probe=None):
    with ExitStack() as ctx:
        c = Core(nc, ctx)
        say = probe or (lambda c, what: None)
        load_and_constants(c, x)
        item_tables(c, src, dst)
        say(c, "tables")
        layer_norm(c, c.rows_a, c.rows_a, "ln_in")
        say(c, "ln_in")
        segment_masks(c)
        for l in range(L0_gnn_Wq.shape[0]):
            qkv(c, L0_gnn_Wq[l], L0_gnn_Wk[l], L0_gnn_Wv[l], f"qkv{l}")
            say(c, f"qkv{l}")
            edge_scores(c, f"score{l}")
            say(c, f"score{l}")
            segment_softmax(c, f"soft{l}")
            say(c, f"soft{l}")
            edge_sums(c, c.v_dram[:, :], True, f"sum{l}")
            say(c, f"sum{l}")
            attention_out(c, L0_gnn_Wo[l], f"out{l}")
            layer_norm(c, c.rows_a, c.rows_a, f"ln_l{l}")
            affine(c, L0_gnn_ln_g[l], L0_gnn_ln_b[l], f"aff{l}")
            say(c, f"layer{l}")
        room = FfnRoom(c)
        ffn(c, room, ACT.Relu, c.rows_c, "mlp", load_ffn(c, room, x, L0_gnn_w1, L0_gnn_b1, L0_gnn_w2, L0_gnn_b2))
        say(c, "x1")
        layer_norm(c, c.rows_c, c.rows_a, "ln_x1")
        route_all(c, room, L0_ffn_Wr, L0_ffn_br, L0_ffn_W1, L0_ffn_b1, L0_ffn_W2, L0_ffn_b2)
        say(c, "route")
        ffn(c, room, ACT.Gelu, c.rows_a, "moe_all")
        layer_norm(c, c.rows_a, c.rows_a, "ln_ffn")
        affine(c, L0_ffn_gamma, L0_ffn_beta, "aff_ffn", c.rows_c)
        say(c, "x2")
        layer_norm(c, c.rows_c, c.rows_a, "ln_x2")
        sage_products(c, L1_gnn_W_self, L1_gnn_W_neigh)
        edge_sums(c, c.k_dram[:, :], False, "sage_sum")
        add_neighbours(c)
        say(c, "x3")
        layer_norm(c, c.rows_c, c.rows_a, "ln_x3")
        layer_norm(c, c.rows_a, c.rows_a, "ln_tok")
        affine(c, L1_ffn_gamma, L1_ffn_beta, "aff_tok")
        gates = ctx.enter_context(nc.sbuf_tensor("gates", [P, NT * 8], F32))
        token_routes(c, gates[:, :], L1_ffn_Wr, L1_ffn_br, L1_ffn_b2, L1_ffn_W1)
        dispatch(c)
        expert_rows(c, L1_ffn_b1, L1_ffn_W2)
        combine(c, out)


_INS = ['x', 'src', 'dst', 'L0_gnn_Wq', 'L0_gnn_Wk', 'L0_gnn_Wv', 'L0_gnn_Wo', 'L0_gnn_ln_g', 'L0_gnn_ln_b',
        'L0_gnn_w1', 'L0_gnn_b1', 'L0_gnn_w2', 'L0_gnn_b2', 'L0_ffn_Wr', 'L0_ffn_br', 'L0_ffn_W1', 'L0_ffn_b1',
        'L0_ffn_W2', 'L0_ffn_b2', 'L0_ffn_gamma', 'L0_ffn_beta', 'L1_gnn_W_self', 'L1_gnn_W_neigh', 'L1_ffn_gamma',
        'L1_ffn_beta', 'L1_ffn_Wr', 'L1_ffn_br', 'L1_ffn_W1', 'L1_ffn_b1', 'L1_ffn_W2', 'L1_ffn_b2']
_OUTS = [((N, D), 'float32')]


def kernel(**inputs):
    import numpy as _np
    import concourse.bacc as _bacc
    from concourse import mybir as _mybir
    from concourse.bass_utils import run_bass_kernel_spmd as _run

    nc = _bacc.Bacc("TRN2", target_bir_lowering=False, num_devices=1)
    arrays, args = {}, []
    for name in _INS:
        a = _np.ascontiguousarray(inputs[name])
        arrays[f"in_{name}_dram"] = a
        args.append(nc.dram_tensor(f"in_{name}_dram", a.shape, _mybir.dt.from_np(a.dtype), kind="ExternalInput").ap())
    for i, (shape, dtype) in enumerate(_OUTS):
        dt = _mybir.dt.from_np(_np.dtype(dtype))
        args.append(nc.dram_tensor(f"out_{i}_dram", shape, dt, kind="ExternalOutput").ap())
    build(nc, *args)
    r = _run(nc, [arrays], core_ids=[0])
    return r.results[0]["out_0_dram"]
```

```python
import concourse.bass as bass
from concourse import mybir
from contextlib import ExitStack

F32 = mybir.dt.float32
F32R = mybir.dt.float32r
BF16 = mybir.dt.bfloat16
I32 = mybir.dt.int32
U32 = mybir.dt.uint32
ALU = mybir.AluOpType
ACT = mybir.ActivationFunctionType
AX = mybir.AxisListType

P = 128
N, D, E = 6250, 256, 100000
H, DK = 8, 32
NODE_TILES = -(-N // P)
NT = NODE_TILES + 1
FULL_ROWS = (N // P) * P
LAST_ROWS = N - FULL_ROWS
EDGE_TILES = -(-E // P)
EC = -(-EDGE_TILES // P)
ITEMS = -(-(EDGE_TILES + NODE_TILES - 1) // 16) * 16
IC = -(-(ITEMS + 16) // P)
BATCH = 4
BATCHES = ITEMS // BATCH
RING = 16
GROUPS = ITEMS // 16
GROUPS2 = NT // 2
BIG = 1e30
TILE_BITS = 6
PAD_DST = 60000
HID = 1024
LN_EPS = 1e-5
NE, HE = 8, 512
SLOT_TILES = (2 * N + NE * (P - 1)) // P
SLOT_TILES += -SLOT_TILES % 2
SLOT_ROUNDS = -(-SLOT_TILES // 4)
EXPERT_BITS = 3


def bc(ap, shape):
    return ap.broadcast_to(shape)


class Core:

    def __init__(self, nc, ctx):
        def sb(name, shape, dt=F32):
            return ctx.enter_context(nc.sbuf_tensor(name, shape, dt))

        self.nc = nc
        self.rows_a = sb("rows_a", [P, NT * D])
        self.rows_c = sb("rows_c", [P, GROUPS * P * 2])
        self.ident = sb("ident", [P, P])
        self.iota_n = sb("iota_n", [P, P])
        self.rel_dst = sb("rel_dst", [P, IC * P])
        self.src_idx = sb("src_idx", [P, IC * P], U32)
        self.item_tile = sb("item_tile", [1, IC * P], I32)
        self.batch_tiles = sb("batch_tiles", [1, IC * P // BATCH], I32)
        self.stats = sb("stats", [P, NT * 6])
        self.mean = sb("mean", [P, NT])
        self.rstd = sb("rstd", [P, NT])
        self.nbias = sb("nbias", [P, NT])
        self.small = sb("small", [P, 4 * NT])
        self.eps_col = sb("eps_col", [P, 1])
        self.iota_p = sb("iota_p", [P, 1])
        self.slots = sb("slots", [P, 2 * NT], U32)
        self.slot_experts = sb("slot_experts", [1, SLOT_ROUNDS], I32)
        self.ps = ctx.enter_context(nc.psum_tensor("ps", [P, 8 * 512], F32))
        self.h_dram = nc.dram_tensor("h_scratch", [NT * P, D], F32, kind="Internal").ap()
        self.k_dram = nc.dram_tensor("k_scratch", [NT * P, D], F32, kind="Internal").ap()
        self.v_dram = nc.dram_tensor("v_scratch", [NT * P, D], F32, kind="Internal").ap()
        self.sid_dram = nc.dram_tensor("sid_scratch", [IC * P, P], F32, kind="Internal").ap()
        self.dstp_dram = nc.dram_tensor("dst_scratch", [EDGE_TILES, P], I32, kind="Internal").ap()
        self.srcp_dram = nc.dram_tensor("src_scratch", [EDGE_TILES, P], I32, kind="Internal").ap()
        self.tile_dram = nc.dram_tensor("tile_scratch", [IC * P], I32, kind="Internal").ap()
        self.edge_sid_dram = nc.dram_tensor("edge_sid_scratch", [2, IC * P], F32, kind="Internal").ap()
        self.ends_dram = nc.dram_tensor("ends_scratch", [16, H, 2, GROUPS], F32, kind="Internal").ap()
        self.slot_in = nc.dram_tensor("slot_in", [SLOT_TILES * P, D], F32, kind="Internal").ap()
        self.slot_out = nc.dram_tensor("slot_out", [SLOT_TILES * P, D], F32, kind="Internal").ap()
        self.carry_dram = nc.dram_tensor("carry_scratch", [16, H, 2, GROUPS], F32, kind="Internal").ap()

    def rows_room(self, ctx, name):
        self.rows_b = ctx.enter_context(self.nc.sbuf_tensor(f"{name}_rows_b", [P, GROUPS * P * 2], F32))

    def scores_room(self, ctx, name):
        self.scores = ctx.enter_context(self.nc.sbuf_tensor(f"{name}_scores", [P, (ITEMS + 16) * H], F32))


class Semaphores(ExitStack):

    def __init__(self, nc):
        super().__init__()
        self.nc, self.all = nc, []

    def sem(self, name):
        one = self.nc.alloc_semaphore(name)
        self.all.append(one)
        return one

    def __exit__(self, *error):
        if not error[0]:
            self.nc.clear_and_free_semaphores(self.all)
            self.nc.all_engine_barrier()
        return super().__exit__(*error)


class Chain:

    def __init__(self, eng, sem):
        self.eng, self.sem, self.n = eng, sem, 0

    def __call__(self, ins):
        self.n += 1
        ins.then_inc(self.sem, 1)
        self.eng.wait_ge(self.sem, self.n)


def constants(c):
    nc = c.nc
    with Semaphores(nc) as s:
        iotas, ready = s.sem("const_iotas"), s.sem("ident_ready")
        with nc.Block() as block:
            @block.gpsimd
            def _(pool):
                pool.iota(c.iota_n[:, :], [[1, P]], base=0, channel_multiplier=0,
                          allow_small_or_imprecise_dtypes=True).then_inc(iotas, 1)
                pool.iota(c.iota_p[:, :], [[1, 1]], base=0, channel_multiplier=1,
                          allow_small_or_imprecise_dtypes=True).then_inc(iotas, 1)

            @block.vector
            def _(v):
                v.memset(c.eps_col[:, :], LN_EPS)
                v.wait_ge(iotas, 2)
                v.tensor_scalar(c.ident[:, :], c.iota_n[:, :], c.iota_p[:, 0:1], None, ALU.is_equal).then_inc(ready, 1)
                v.wait_ge(ready, 1)


def item_tables(c, src, dst):
    nc = c.nc
    whole = EDGE_TILES - 1
    tail = E - whole * P
    cols, rest = whole // P, whole % P
    b = c.rows_b
    at = [0]

    def take(n, dt=F32):
        a = b[:, at[0]:at[0] + n]
        at[0] += n
        return a if dt == F32 else a.bitcast(dt)

    dt_i = take(EC * P, I32).rearrange("p (c e) -> p c e", e=P)
    st_i = take(EC * P, I32).rearrange("p (c e) -> p c e", e=P)
    d_i = take(IC * P, I32).rearrange("p (c e) -> p c e", e=P)
    s_i = take(IC * P, I32).rearrange("p (c e) -> p c e", e=P)
    ends = take(2 * EC).rearrange("p (k c) -> p k c", k=2)
    limits = take(2 * NODE_TILES).rearrange("p (k j) -> p k j", k=2)
    below = take(2 * EC * NODE_TILES).rearrange("p (k c j) -> p k c j", k=2, c=EC)
    ones = take(P)
    counts = take(2 * NODE_TILES).rearrange("p (k j) -> p k j", k=2)
    size, upto, first, shift = (take(NODE_TILES) for _ in range(4))
    item_no = take(IC)
    past = take(IC * NODE_TILES).rearrange("p (c j) -> p c j", c=IC)
    moved = take(IC * NODE_TILES).rearrange("p (c j) -> p c j", c=IC)
    tile_no = take(IC)
    edge_tile = take(IC)
    edge_tile_u = take(IC, U32)
    tile_i = take(IC, I32)
    dst_f = take(IC * P).rearrange("p (c e) -> p c e", e=P)
    src_f = take(IC * P).rearrange("p (c e) -> p c e", e=P)
    rel = take(IC * P).rearrange("p (c e) -> p c e", e=P)
    valid = take(IC * P).rearrange("p (c e) -> p c e", e=P)
    sid = take(IC * P).rearrange("p (c e) -> p c e", e=P)
    row_f = take(IC * P)[0:1]
    with Semaphores(nc) as s:
        def sem(n):
            return s.sem(n)
        padded, loaded, saved, iotas = sem("padded"), sem("edges_loaded"), sem("edges_saved"), sem("iotas")
        step, summed, rows_at, gathered = sem("table_step"), sem("ends_summed"), sem("edge_tile_ready"), sem("rows_gathered")
        turned, copied, sid_ready, written = sem("turned"), sem("turned_copied"), sem("sid_ready"), sem("tables_written")
        rel_ready, tiles_back = sem("rel_ready"), sem("tiles_back")
        with nc.Block() as block:
            @block.sync
            def _(sp):
                sp.wait_ge(padded, 2)
                for flat, to in ((dst, dt_i), (src, st_i)):
                    rows = flat[0:whole * P].rearrange("(k e) -> k e", e=P)
                    sp.dma_start(to[:, 0:cols, :], rows[0:cols * P, :].rearrange("(c p) e -> p c e", p=P)).then_inc(loaded, 16)
                    sp.dma_start(to[0:rest, cols, :], rows[cols * P:whole, :]).then_inc(loaded, 16)
                    sp.dma_start(to[rest:rest + 1, cols, 0:tail], flat[whole * P:E].rearrange("(a e) -> a e", a=1)).then_inc(loaded, 16)
                sp.wait_ge(loaded, 96)
                for ap, to in ((dt_i, c.dstp_dram), (st_i, c.srcp_dram)):
                    sp.dma_start(to[0:cols * P, :].rearrange("(c p) e -> p c e", p=P), ap[:, 0:cols, :]).then_inc(saved, 16)
                    sp.dma_start(to[cols * P:EDGE_TILES, :], ap[0:rest + 1, cols, :]).then_inc(saved, 16)
                sp.wait_ge(sid_ready, 1)
                sp.dma_start(c.sid_dram[:, :].rearrange("(c p) e -> p c e", p=P), sid).then_inc(written, 16)
                with nc.allow_non_contiguous_dma("one number an item"):
                    sp.dma_start(c.tile_dram.rearrange("(c p) -> p c", p=P), tile_i).then_inc(written, 16)
                    sp.dma_start(c.edge_sid_dram[0].rearrange("(c p) -> p c", p=P), sid[:, :, 0]).then_inc(written, 16)
                    sp.dma_start(c.edge_sid_dram[1].rearrange("(c p) -> p c", p=P), sid[:, :, P - 1]).then_inc(written, 16)
                sp.wait_ge(written, 64)
                sp.dma_start(c.item_tile[:, :], c.tile_dram.rearrange("(a i) -> a i", a=1)).then_inc(tiles_back, 16)

            @block.gpsimd
            def _(pool):
                pool.iota(limits[:, 0, :], [[P, NODE_TILES]], base=0, channel_multiplier=0,
                          allow_small_or_imprecise_dtypes=True).then_inc(iotas, 1)
                pool.iota(limits[:, 1, :], [[P, NODE_TILES]], base=P, channel_multiplier=0,
                          allow_small_or_imprecise_dtypes=True).then_inc(iotas, 1)
                pool.iota(item_no, [[P, IC]], base=0, channel_multiplier=1,
                          allow_small_or_imprecise_dtypes=True).then_inc(iotas, 1)
                pool.wait_ge(saved, 64)
                pool.wait_ge(rows_at, 1)
                for i in range(IC):
                    at_row = bass.IndirectOffsetOnAxis(ap=edge_tile_u[:, i:i + 1], axis=0)
                    pool.indirect_dma_start(d_i[:, i, :], None, c.dstp_dram[:, :], at_row).then_inc(gathered, 16)
                    pool.indirect_dma_start(s_i[:, i, :], None, c.srcp_dram[:, :], at_row).then_inc(gathered, 16)

            @block.vector
            def _(v):
                do = Chain(v, step)
                v.memset(dt_i, PAD_DST).then_inc(padded, 1)
                v.memset(st_i, 0).then_inc(padded, 1)
                do(v.memset(ones, 1.0))
                v.wait_ge(loaded, 96)
                do(v.tensor_copy(ends[:, 0, :], dt_i[:, :, P - 1]))
                do(v.tensor_copy(ends[:, 1, :], dt_i[:, :, 0]))
                v.wait_ge(iotas, 3)
                for k in range(2):
                    do(v.tensor_tensor(below[:, k], bc(ends[:, k].unsqueeze(2), [P, EC, NODE_TILES]),
                                       bc(limits[:, k].unsqueeze(1), [P, EC, NODE_TILES]), ALU.is_lt))
                v.wait_ge(summed, 1)
                do(v.tensor_copy(counts.rearrange("p k j -> p (k j)"), c.ps[:, 0:2 * NODE_TILES]))
                do(v.tensor_tensor(size, counts[:, 1], counts[:, 0], ALU.subtract))
                do(v.tensor_tensor_scan(upto, ones[:, 0:NODE_TILES], size, 0.0, ALU.mult, ALU.add))
                do(v.tensor_tensor(first, upto, size, ALU.subtract))
                do(v.tensor_tensor(first, counts[:, 0], first, ALU.subtract))
                do(v.memset(shift, 0.0))
                do(v.tensor_tensor(shift[:, 0:NODE_TILES - 1], first[:, 1:], first[:, :NODE_TILES - 1], ALU.subtract))
                do(v.tensor_tensor(past, bc(upto.unsqueeze(1), [P, IC, NODE_TILES]),
                                   bc(item_no.unsqueeze(2), [P, IC, NODE_TILES]), ALU.is_le))
                do(v.tensor_reduce(tile_no, past, AX.X, ALU.add))
                do(v.tensor_tensor(moved, past, bc(shift.unsqueeze(1), [P, IC, NODE_TILES]), ALU.mult))
                do(v.tensor_reduce(edge_tile, moved, AX.X, ALU.add))
                do(v.tensor_tensor(edge_tile, edge_tile, item_no, ALU.add))
                do(v.tensor_scalar(edge_tile, edge_tile, 0.0, float(EDGE_TILES - 1), ALU.max, ALU.min))
                v.tensor_copy(edge_tile_u, edge_tile).then_inc(rows_at, 1)
                do(v.tensor_copy(tile_i, tile_no))
                do(v.tensor_scalar(tile_no, tile_no, float(P), None, ALU.mult))
                v.wait_ge(gathered, 32 * IC)
                do(v.tensor_copy(dst_f, d_i))
                do(v.tensor_copy(src_f, s_i))
                do(v.tensor_tensor(rel, dst_f, bc(tile_no.unsqueeze(2), [P, IC, P]), ALU.subtract))
                v.sem_inc(rel_ready, 1)
                do(v.tensor_scalar(valid, rel, 0.0, None, ALU.is_ge))
                do(v.tensor_scalar(sid, rel, float(P), None, ALU.is_lt))
                do(v.tensor_tensor(valid, valid, sid, ALU.mult))
                do(v.tensor_scalar(dst_f, dst_f, 1.0, None, ALU.add))
                do(v.tensor_tensor(valid, valid, dst_f, ALU.mult))
                do(v.tensor_scalar(sid, valid, 1.0, None, ALU.subtract))
                v.sem_inc(sid_ready, 1)
                v.wait_ge(turned, 1)
                v.tensor_copy(c.rel_dst[:, :], c.ps[:, 1024:1024 + IC * P]).then_inc(copied, 1)
                v.tensor_copy(c.src_idx[:, :], c.ps[:, 2048:2048 + IC * P]).then_inc(copied, 1)
                v.wait_ge(copied, 2)
                v.wait_ge(tiles_back, 16)
                do(v.tensor_copy(row_f, c.item_tile[:, :]))
                each = row_f.rearrange("p (b u) -> p u b", u=BATCH)
                for u in range(1, BATCH):
                    do(v.scalar_tensor_tensor(each[:, 0], each[:, u], float(1 << (TILE_BITS * u)), each[:, 0],
                                              ALU.mult, ALU.add))
                do(v.tensor_copy(c.batch_tiles[:, :], each[:, 0]))

            @block.tensor
            def _(pe):
                pe.wait_ge(step, 5)
                for k in range(2):
                    for i in range(EC):
                        mm = pe.matmul(c.ps[:, k * NODE_TILES:(k + 1) * NODE_TILES], ones, below[:, k, i, :],
                                       start=(i == 0), stop=(i == EC - 1))
                mm.then_inc(summed, 1)
                pe.wait_ge(rel_ready, 1)
                for k, tab in ((0, rel), (1, src_f)):
                    for i in range(IC):
                        to = 1024 * (1 + k) + i * P
                        mm = pe.transpose(c.ps[:, to:to + P], tab[:, i, :], c.ident[:, :])
                mm.then_inc(turned, 1)


def row_stats(v, c, src, t, taken):
    v.bn_stats(c.stats[:, bass.ds(t * 6, 6)], src[:, bass.ds(t * D, D)]).then_inc(taken, 1)


def tiles_of_ten(eng, first, count, body):
    with eng.Fori(first // 10, (first + count) // 10) as i:
        for u in range(10):
            body(i * 10 + u)


def layer_norm(c, src, dst, name, have_stats=False, gamma=None, beta=None, add_to=None):
    nc = c.nc
    by_vector = 0 if gamma is not None else NT // 5 * 3
    if gamma is not None:
        gb, bb = c.scores[:, 0:D], c.scores[:, D:2 * D]
    CH = 5
    with Semaphores(nc) as s:
        taken, step, rooted, var_ready, ready, applied, normed, loaded = (
            s.sem(f"{name}_{n}") for n in ("stats", "step", "root", "var", "ready", "applied", "normed", "loaded"))
        with nc.Block() as block:
            if gamma is not None:
                @block.sync
                def _(sp):
                    sp.dma_start(gb, row_bc(gamma)).then_inc(loaded, 16)
                    sp.dma_start(bb, row_bc(beta)).then_inc(loaded, 16)

            @block.vector
            def _(v):
                do = Chain(v, step)
                if not have_stats:
                    tiles_of_ten(v, 0, NT, lambda t: row_stats(v, c, src, t, taken))
                    v.wait_ge(taken, NT)
                st = c.stats[:, :].rearrange("p (t k) -> p k t", k=6)
                tmp = c.small[:, 0:NT]
                do(v.tensor_tensor(c.mean[:, :], st[:, 1, :], st[:, 4, :], ALU.add))
                do(v.tensor_scalar(c.mean[:, :], c.mean[:, :], 0.5, None, ALU.mult))
                do(v.tensor_tensor(tmp, st[:, 1, :], st[:, 4, :], ALU.subtract))
                do(v.tensor_tensor(tmp, tmp, tmp, ALU.mult))
                do(v.tensor_tensor(c.rstd[:, :], st[:, 2, :], st[:, 5, :], ALU.add))
                do(v.scalar_tensor_tensor(c.rstd[:, :], tmp, D / 4.0, c.rstd[:, :], ALU.mult, ALU.add))
                do(v.tensor_scalar(c.rstd[:, :], c.rstd[:, :], 1.0 / D, None, ALU.mult))
                v.sem_inc(var_ready, 1)
                v.wait_ge(rooted, 1)
                do(v.reciprocal(c.rstd[:, :], c.rstd[:, :]))
                do(v.scalar_tensor_tensor(c.nbias[:, :], c.mean[:, :], -1.0, c.rstd[:, :], ALU.mult, ALU.mult))
                v.sem_inc(ready, 1)

                def apply(t):
                    at, col = bass.ds(t * D, D), bass.ds(t, 1)
                    v.tensor_scalar(dst[:, at], src[:, at], c.mean[:, col], c.rstd[:, col], ALU.subtract,
                                    ALU.mult).then_inc(applied, 1)
                if gamma is None:
                    tiles_of_ten(v, 0, by_vector, apply)
                    v.wait_ge(applied, by_vector)
                    return
                v.wait_ge(loaded, 32)
                for t in range(0, NT, CH):
                    v.wait_ge(normed, t + CH)
                    rows, shape = rows3(dst)[:, t:t + CH, :], [P, CH, D]
                    do(v.tensor_tensor(rows, rows, bc(gb.unsqueeze(1), shape), ALU.mult))
                    do(v.tensor_tensor(rows, rows, bc(bb.unsqueeze(1), shape), ALU.add))
                    if add_to is not None:
                        to = rows3(add_to)[:, t:t + CH, :]
                        do(v.tensor_tensor(to, to, rows, ALU.add))

            @block.scalar
            def _(a):
                a.wait_ge(var_ready, 1)
                a.activation(c.rstd[:, :], c.rstd[:, :], ACT.Sqrt, bias=c.eps_col[:, 0:1]).then_inc(rooted, 1)
                a.wait_ge(ready, 1)

                def apply(t):
                    at, col = bass.ds(t * D, D), bass.ds(t, 1)
                    a.activation(dst[:, at], src[:, at], ACT.Identity, bias=c.nbias[:, col],
                                 scale=c.rstd[:, col]).then_inc(normed, 1)
                tiles_of_ten(a, by_vector, NT - by_vector, apply)
                a.wait_ge(normed, NT - by_vector)


def groups(eng, body):
    with eng.Fori(0, GROUPS2 // 2) as i:
        body(i * 2, 0, False)
        body(i * 2 + 1, 1, False)
    body(GROUPS2 - 1, (GROUPS2 - 1) % 2, True)


def turn(pe, c, staged_rows, parity):
    for k in range(2):
        for u in range(2):
            to = parity * 512 + k * 2 * P + u * P
            mm = pe.transpose(c.ps[:, to:to + P], staged_rows[:, u * D + k * P:u * D + k * P + P], c.ident[:, :])
    return mm


def load_tiles(eng, c, b):
    packed = eng.value_load(c.batch_tiles[0:1, bass.ds(b, 1)], min_val=0, max_val=(1 << TILE_BITS * BATCH) - 1)
    why = "the item table counts node tiles from 0 to NODE_TILES"
    return [c.nc.s_assert_within((packed >> (TILE_BITS * u)) & ((1 << TILE_BITS) - 1), 0, NODE_TILES,
                                 skip_runtime_bounds_check_because=why) for u in range(BATCH)]


class Front:

    def __init__(self, c, s, name, rows, turned_rows, source):
        self.c, self.rows, self.turned_rows, self.source = c, rows, turned_rows, source
        self.staged, self.turned, self.copied, self.used = (
            s.sem(f"{name}_{n}") for n in ("staged", "turned", "copied", "used"))

    def start_pe(self, pe):
        pe.sem_inc(self.turned, 2)
        pe.sem_inc(self.used, 2)

    def start_copies(self, eng):
        eng.sem_inc(self.copied, 2)

    def stage(self, a, g, parity):
        a.wait_ge(self.turned, g + 1)
        a.activation(self.rows[parity], self.source[:, bass.ds(g * 2 * D, 2 * D)],
                     ACT.Copy).then_inc(self.staged, 1)

    def turn(self, pe, g, parity):
        pe.wait_ge(self.staged, g + 1)
        pe.wait_ge(self.copied, g + 1)
        turn(pe, self.c, self.rows[parity], parity).then_inc(self.turned, 1)

    def copy(self, eng, g, parity):
        eng.wait_ge(self.used, g + 1)
        eng.wait_ge(self.turned, g + 3)
        to, ps = self.turned_rows[:, parity], self.c.ps[:, parity * 512:parity * 512 + 512]
        by_scalar = eng.engine == self.c.nc.scalar.engine
        (eng.activation(to, ps, ACT.Copy) if by_scalar else eng.tensor_copy(to, ps)).then_inc(self.copied, 1)


def groups_ahead(eng, body):
    looped = (GROUPS2 - 2) // 2
    with eng.Fori(0, looped) as i:
        body(i * 2, 0, 2)
        body(i * 2 + 1, 1, 2)
    for g in range(2 * looped, GROUPS2):
        body(g, g % 2, min(2, GROUPS2 - 1 - g))


def take_high(eng, high, x):
    return eng.tensor_copy(high.bitcast(F32R), x)


def take_low(eng, low, x, high):
    return eng.tensor_tensor(low.bitcast(F32R), x, high, ALU.subtract)


def split_matmul(pe, out, lhs, rhs, first, last):
    pairs = ((0, 0), (0, 1), (1, 0))
    for n, (i, j) in enumerate(pairs):
        mm = pe.matmul(out, lhs[i].bitcast(F32R), rhs[j].bitcast(F32R), start=first and n == 0,
                       stop=last and n == len(pairs) - 1)
    return mm


def split(do, v, parts, x):
    do(take_high(v, parts[0], x))
    do(take_low(v, parts[1], x, parts[0]))


def qkv(c, wq, wk, wv, name):
    nc = c.nc
    scale = float(DK) ** -0.5
    with ExitStack() as memory, Semaphores(nc) as s:
        def sb(what, n, pattern, **sizes):
            return memory.enter_context(nc.sbuf_tensor(f"{name}_{what}", [P, n], F32))[:, :].rearrange(pattern, **sizes)

        def sem(n):
            return s.sem(f"{name}_{n}")
        rows = [sb(f"rows{u}", 512, "p (t d) -> p t d", t=2).rearrange("p t d -> p (t d)") for u in range(2)]
        kv = sb("kv", 4 * 2 * D, "p (b n) -> p b n", b=4)
        w_raw = kv.rearrange("p b n -> p (b n)")[:, 0:6 * D].rearrange("p (k n) -> p k n", k=2)
        w = [sb(f"w_{x}", 6 * D, "p (k n) -> p k n", k=2) for x in ("high", "low")]
        rows_t = [sb(f"rows_t_{x}", 1024, "p (b n) -> p b n", b=2) for x in ("high", "low")]
        loaded, saved, out_done, kv_ready, step = (
            sem(n) for n in ("w_loaded", "h_saved", "out_done", "kv_ready", "step"))
        staged, turned, row_high, rows_split, used, w_split = (
            sem(n) for n in ("staged", "turned", "row_high", "rows_split", "used", "w_split"))
        stored, kv_free = [sem(f"stored{u}") for u in range(4)], sem("kv_free")
        with nc.Block() as block:
            @block.sync
            def _(sp):
                for j, m in enumerate((wq, wk, wv)):
                    sp.dma_start(w_raw[:, :, j * D:(j + 1) * D], m.rearrange("(k p) n -> p k n", p=P)).then_inc(loaded, 16)
                sp.dma_start(c.h_dram.rearrange("(t p) d -> p t d", p=P),
                             c.rows_a[:, :].rearrange("p (t d) -> p t d", d=D)).then_inc(saved, 16)

                def body(g, parity, last):
                    for u in range(2):
                        b = 2 * parity + u
                        sp.wait_ge(kv_ready, g * 2 + u + 1)
                        for to, n in ((c.k_dram, 0), (c.v_dram, D)):
                            sp.dma_start(to[bass.ds(g * 2 * P + u * P, P), :], kv[:, b, n:n + D]).then_inc(stored[b], 16)
                    for u in range(2):
                        sp.wait_ge(stored[2 * parity + u], (g - parity) * 16 + 32)
                        sp.sem_inc(kv_free, 1)
                groups(sp, body)
                sp.wait_ge(saved, 16)

            @block.scalar
            def _(a):
                def stage(g, parity, last):
                    a.wait_ge(turned, g + 1)
                    a.activation(rows[parity], c.rows_a[:, bass.ds(g * 2 * D, 2 * D)], ACT.Copy).then_inc(staged, 1)
                groups(a, stage)

            @block.tensor
            def _(pe):
                pe.sem_inc(turned, 2)
                pe.sem_inc(used, 2)

                def flip(g, parity):
                    pe.wait_ge(staged, g + 1)
                    pe.wait_ge(rows_split, g + 1)
                    turn(pe, c, rows[parity], parity).then_inc(turned, 1)
                flip(0, 0)
                flip(1, 1)
                pe.wait_ge(w_split, 1)

                def body(g, parity, ahead):
                    pe.wait_ge(rows_split, g + 3)
                    pe.wait_ge(out_done, g + 1)
                    for u in range(2):
                        x = [[m[:, parity, k * 2 * P + u * P:k * 2 * P + u * P + P] for m in rows_t] for k in range(2)]
                        q, kv_at = (2 + parity) * 512 + u * D, (4 + 2 * parity + u) * 512
                        for to, cols in ((c.ps[:, q:q + D], slice(0, D)), (c.ps[:, kv_at:kv_at + 2 * D], slice(D, 3 * D))):
                            for k in range(2):
                                mm = split_matmul(pe, to, x[k], [m[:, k, cols] for m in w], k == 0, k == 1)
                    mm.then_inc(used, 1)
                    if ahead > 1:
                        flip(g + 2, parity)
                groups_ahead(pe, body)

            @block.vector
            def _(v):
                do = Chain(v, step)
                v.sem_inc(rows_split, 2)
                v.sem_inc(out_done, 2)
                v.sem_inc(kv_free, 4)

                def split_rows(g, parity):
                    v.wait_ge(used, g + 1)
                    v.wait_ge(turned, g + 3)
                    ps = c.ps[:, parity * 512:(parity + 1) * 512]
                    take_high(v, rows_t[0][:, parity], ps).then_inc(row_high, 1)
                    v.wait_ge(row_high, g + 1)
                    take_low(v, rows_t[1][:, parity], ps, rows_t[0][:, parity]).then_inc(rows_split, 1)
                split_rows(0, 0)
                v.wait_ge(loaded, 48)
                split(do, v, w, w_raw)
                v.sem_inc(w_split, 1)
                split_rows(1, 1)

                def body(g, parity, ahead):
                    v.wait_ge(used, g + 3)
                    for u in range(2):
                        b = 2 * parity + u
                        v.wait_ge(kv_free, g * 2 + u + 1)
                        to = (4 + b) * 512
                        v.tensor_copy(kv[:, b, :], c.ps[:, to:to + 512]).then_inc(kv_ready, 1)
                    q = (2 + parity) * 512
                    v.tensor_scalar(c.rows_b[:, bass.ds(g * 2 * D, 2 * D)], c.ps[:, q:q + 512], scale, None,
                                    ALU.mult).then_inc(out_done, 1)
                    if ahead > 1:
                        split_rows(g + 2, parity)
                groups_ahead(v, body)
                v.wait_ge(out_done, GROUPS2 + 2)


def one_hot(c, v, s_buf, b, parity):
    return v.tensor_tensor(s_buf[:, parity], bc(c.iota_n[:, :].unsqueeze(1), [P, BATCH, P]),
                           bc(c.rel_dst[:, bass.ds(b * BATCH, BATCH)].unsqueeze(2), [P, BATCH, P]), ALU.is_equal)


def stage_indices(c, a, idx, staged, free, i, h, per_batch=1):
    half = RING // 2
    a.wait_ge(free, (i * (RING // BATCH) + (h + 1) * (half // BATCH)) * per_batch)
    a.activation(idx[:, h * half:(h + 1) * half], c.src_idx[:, bass.ds(i * RING + h * half, half)],
                 ACT.Copy).then_inc(staged, 1)


def gather_rows(pool, table, ring, idx, staged, gate, landed, extra):
    half = RING // 2

    def fetch(i, h):
        pool.wait_ge(staged, i * 2 + h + 1)
        pool.sem_inc(gate, 1)
        for u in range(half):
            slot = h * half + u
            pool.indirect_dma_start(ring[:, slot, 0:D], None, table,
                                    bass.IndirectOffsetOnAxis(ap=idx[:, slot:slot + 1], axis=0)).then_inc(landed[slot], 16)

    with pool.Fori(0, ITEMS // RING) as i:
        fetch(i, 0)
        fetch(i, 1)
    if extra:
        fetch(ITEMS // RING, 0)


def edge_scores(c, name):
    nc = c.nc
    BW = BATCH * D
    ring = c.rows_a[:, 0:RING * D].rearrange("p (s d) -> p s d", d=D)
    s_buf = c.rows_a[:, RING * D:RING * D + 2048].rearrange("p (b i n) -> p b i n", b=4, i=BATCH)
    st_buf = c.rows_a[:, RING * D + 2048:RING * D + 3072].rearrange("p (b i n) -> p b i n", b=2, i=BATCH)
    prod = c.rows_a[:, RING * D + 3072:RING * D + 5120].rearrange("p (b n) -> p b n", b=2)
    QPS = 1024
    with Semaphores(nc) as s:
        def sem(n):
            return s.sem(f"{name}_{n}")
        free, staged, gate, made, turned = sem("slots_free"), sem("idx"), sem("gate"), sem("onehot"), sem("turned")
        copied, expanded, multiplied, reduced = sem("copied"), sem("expanded"), sem("multiplied"), sem("reduced")
        landed = [sem(f"landed{u}") for u in range(RING)]
        idx = s.enter_context(nc.sbuf_tensor(f"{name}_idx", [P, RING], U32))
        with nc.Block() as block:
            @block.gpsimd
            def _(pool):
                gather_rows(pool, c.k_dram[:, :], ring, idx, staged, gate, landed, False)

            @block.vector
            def _(v):
                v.sem_inc(free, RING // BATCH)
                v.sem_inc(multiplied, 2)
                v.sem_inc(reduced, 2)
                one_hot(c, v, s_buf, 0, 0).then_inc(made, 1)
                one_hot(c, v, s_buf, 1, 1).then_inc(made, 1)
                with v.Fori(0, BATCHES // 4) as i:
                    for q in range(4):
                        b, par = i * 4 + q, q % 2
                        v.wait_ge(turned, b + 1)
                        one_hot(c, v, s_buf, b + 2, (q + 2) % 4).then_inc(made, 1)
                        v.wait_ge(expanded, b + 3)
                        for u in range(BATCH):
                            v.wait_ge(landed[q * BATCH + u], i * 16 + 16)
                        v.wait_ge(reduced, b + 1)
                        v.tensor_tensor(prod[:, par], c.ps[:, QPS + par * BW:QPS + (par + 1) * BW],
                                        ring[:, q * BATCH:(q + 1) * BATCH, :].rearrange("p s d -> p (s d)"),
                                        ALU.mult).then_inc(multiplied, 1)
                        v.wait_ge(multiplied, b + 3)
                        v.sem_inc(free, 1)
                        v.tensor_reduce(c.scores[:, bass.ds(b * BATCH * H, BATCH * H)],
                                        prod[:, par].rearrange("p (h k) -> p h k", k=DK), AX.X, ALU.add).then_inc(reduced, 1)
                v.wait_ge(reduced, BATCHES + 2)

            @block.scalar
            def _(a):
                a.sem_inc(copied, 2)
                stage_indices(c, a, idx, staged, free, 0, 0)
                with a.Fori(0, BATCHES // 4) as i:
                    for q in range(4):
                        b, par = i * 4 + q, q % 2
                        a.wait_ge(expanded, b + 1)
                        a.wait_ge(turned, b + 3)
                        a.activation(st_buf[:, par].rearrange("p i n -> p (i n)"), c.ps[:, par * 512:par * 512 + 512],
                                     ACT.Copy).then_inc(copied, 1)
                        if q % 2 == 0:
                            stage_indices(c, a, idx, staged, free, i + q // 2, 1 - q // 2)

            @block.tensor
            def _(pe):
                pe.sem_inc(turned, 2)
                pe.sem_inc(expanded, 2)

                def flip(b, slot):
                    par = slot % 2
                    pe.wait_ge(made, b + 1)
                    pe.wait_ge(copied, b + 1)
                    for u in range(BATCH):
                        mm = pe.transpose(c.ps[:, par * 512 + u * P:par * 512 + u * P + P], s_buf[:, slot, u, :], c.ident[:, :])
                    mm.then_inc(turned, 1)
                flip(0, 0)
                with pe.Fori(0, BATCHES // 4) as i:
                    for q in range(4):
                        b, par = i * 4 + q, q % 2
                        flip(b + 1, (q + 1) % 4)
                        tiles = load_tiles(pe, c, b)
                        pe.wait_ge(copied, b + 3)
                        pe.wait_ge(multiplied, b + 1)
                        for u in range(BATCH):
                            to = QPS + par * BW + u * D
                            mm = pe.matmul(c.ps[:, to:to + D], st_buf[:, par, u, :], c.rows_b[:, bass.ds(tiles[u] * D, D)],
                                           start=True, stop=True)
                        mm.then_inc(expanded, 1)


def segment_masks(c, x):
    nc = c.nc
    n = GROUPS * P
    sid = c.rows_b[:, 0:n]
    sid3 = sid.rearrange("p (g e) -> p g e", e=P)
    c.link = c.rows_c[:, 0:n // 2 + 1].bitcast(BF16)
    c.to_first = c.rows_c[:, n // 2 + 1:n + 1].bitcast(BF16)
    c.to_last = c.rows_c[:, n + 1:n + 1 + n // 2].bitcast(BF16)
    o = n + 1 + n // 2
    c.item_link = c.rows_c[0:H, o:o + ITEMS + 1]
    c.item_whole = c.rows_c[0:H, o + ITEMS + 1:o + 2 * ITEMS + 1]
    assert o + 2 * ITEMS + 1 <= 2 * n
    ends = c.rows_b[0:H, n:n + 2 * ITEMS].rearrange("p (k i) -> p k i", k=2)
    with Semaphores(nc) as s:
        loaded, step, zeroed, x_loaded = (s.sem(n) for n in ("sid_loaded", "mask_step", "pad_zeroed", "x_in_loaded"))
        with nc.Block() as block:
            @block.sync
            def _(sp):
                for h in range(H):
                    sp.dma_start(sid3[h * 16:(h + 1) * 16], c.sid_dram[0:ITEMS, :].rearrange("(g i) e -> i g e", i=16)).then_inc(loaded, 16)
                for h in range(H):
                    sp.dma_start(ends[h:h + 1], c.edge_sid_dram[:, 0:ITEMS].rearrange("(a k) i -> a k i", a=1)).then_inc(loaded, 16)
                sp.wait_ge(zeroed, 1)
                sp.wait_ge(loaded, 32 * H)
                rows = rows3(c.rows_a)
                sp.dma_start(rows[:, 0:FULL_ROWS // P, :],
                             x[0:FULL_ROWS, :].rearrange("(t p) d -> p t d", p=P)).then_inc(x_loaded, 16)
                sp.dma_start(rows[0:LAST_ROWS, FULL_ROWS // P, :], x[FULL_ROWS:N, :]).then_inc(x_loaded, 16)
                sp.wait_ge(x_loaded, 32)

            @block.vector
            def _(v):
                v.memset(c.rows_a[:, FULL_ROWS // P * D:NT * D], 0.0).then_inc(zeroed, 1)
                do = Chain(v, step)
                v.wait_ge(loaded, 32 * H)

                def masked(out, a, b):
                    do(v.tensor_tensor(out, a, b, ALU.is_equal))
                    do(v.tensor_scalar(out, out, 1.0, BIG, ALU.subtract, ALU.mult))
                link3 = c.link[:, 0:n].rearrange("p (g e) -> p g e", e=P)
                do(v.memset(c.link, 0.0))
                masked(link3[:, :, 1:], sid3[:, :, 1:], sid3[:, :, :P - 1])
                do(v.memset(link3[:, :, 0:1], -BIG))
                do(v.memset(c.link[:, n:n + 2], -BIG))
                for out, e in ((c.to_first, 0), (c.to_last, P - 1)):
                    masked(out.rearrange("p (g e) -> p g e", e=P), sid3, bc(sid3[:, :, e:e + 1], [P, GROUPS, P]))
                do(v.memset(c.item_link, -BIG))
                masked(c.item_link[:, 1:ITEMS], ends[:, 0, 1:ITEMS], ends[:, 1, 0:ITEMS - 1])
                masked(c.item_whole, ends[:, 0, :], ends[:, 1, :])


def segment_softmax(c, name):
    nc = c.nc
    n = GROUPS * P
    e = c.rows_b[:, 0:n]
    f = c.rows_b[:, n:2 * n]
    m = c.rows_a[:, 0:n]
    ends = c.rows_a[:, n:n + 2 * GROUPS].rearrange("p (k g) -> p k g", k=2)
    t = [n + 2 * GROUPS]

    def take(k):
        a = c.rows_a[0:H, t[0]:t[0] + k]
        t[0] += k
        return a
    ends_t = take(2 * ITEMS).rearrange("p (k i g) -> p k i g", k=2, i=16)
    seq = take(2 * ITEMS).rearrange("p (k i) -> p k i", k=2)
    spare = c.rows_a[:, t[0]:t[0] + 1024].rearrange("p (b n) -> p b n", b=2)
    assert t[0] + 1024 <= NT * D
    fwd, back = (c.scores[0:H, k * ITEMS:(k + 1) * ITEMS] for k in range(2))
    wl, wr = (c.scores[0:H, (2 + k) * ITEMS:(3 + k) * ITEMS] for k in range(2))
    rounds = GROUPS // 4
    by_group = c.scores[:, 0:ITEMS * H].rearrange("p (g i h) -> p g h i", g=GROUPS, i=16)
    with Semaphores(nc) as s:
        def sem(x):
            return s.sem(f"{name}_{x}")
        arranged, turned, copied, step, saved = sem("arranged"), sem("turned"), sem("copied"), sem("step"), sem("saved")
        sent, carried, seq_done, ready, exped = sem("sent"), sem("carried"), sem("seq_done"), sem("ready"), sem("exped")
        back_turned, back_copied, come = sem("back_turned"), sem("back_copied"), sem("come")
        with nc.Block() as block:
            @block.tensor
            def _(pe):
                for r in range(rounds):
                    pe.wait_ge(arranged, r + 1)
                    if r >= 2:
                        pe.wait_ge(copied, r - 1)
                    for u in range(4):
                        to = (r % 2) * 512 + u * P
                        g = r * 4 + u
                        mm = pe.transpose(c.ps[:, to:to + P], f[:, g * P:(g + 1) * P], c.ident[:, :])
                    mm.then_inc(turned, 1)
                for r in range(rounds):
                    pe.wait_ge(exped, r + 1)
                    if r >= 2:
                        pe.wait_ge(back_copied, r - 1)
                    for u in range(4):
                        to = (r % 2) * 512 + u * P
                        g = r * 4 + u
                        mm = pe.transpose(c.ps[:, to:to + P], e[:, g * P:(g + 1) * P], c.ident[:, :])
                    mm.then_inc(back_turned, 1)

            @block.scalar
            def _(a):
                for r in range(rounds):
                    a.wait_ge(turned, r + 1)
                    a.activation(e[:, r * 512:(r + 1) * 512], c.ps[:, (r % 2) * 512:(r % 2) * 512 + 512], ACT.Copy).then_inc(copied, 1)
                a.wait_ge(copied, rounds)

                def back(r):
                    a.wait_ge(back_turned, r + 1)
                    a.activation(by_group[:, r * 4:(r + 1) * 4],
                                 c.ps[:, (r % 2) * 512:(r % 2) * 512 + 512].rearrange("p (g h i) -> p g h i", g=4, h=H),
                                 ACT.Copy).then_inc(back_copied, 1)
                for r in range(rounds):
                    a.wait_ge(ready, r + 1)
                    a.activation(e[:, r * 512:(r + 1) * 512], e[:, r * 512:(r + 1) * 512], ACT.Exp).then_inc(exped, 1)
                    if r > 0:
                        back(r - 1)
                back(rounds - 1)
                a.wait_ge(back_copied, rounds)

            @block.sync
            def _(sp):
                sp.wait_ge(saved, 1)
                for h in range(H):
                    sp.dma_start(c.ends_dram[:, h, :, :], ends[h * 16:(h + 1) * 16]).then_inc(sent, 16)
                sp.wait_ge(sent, 16 * H)
                for k in range(2):
                    sp.dma_start(ends_t[:, k], c.ends_dram[:, :, k, :].rearrange("i h g -> h i g")).then_inc(carried, 16)
                sp.wait_ge(seq_done, 1)
                for k in range(2):
                    sp.dma_start(c.carry_dram[:, :, k, :].rearrange("i h g -> h i g"), ends_t[:, k]).then_inc(sent, 16)
                sp.wait_ge(sent, 16 * H + 32)
                for h in range(H):
                    sp.dma_start(ends[h * 16:(h + 1) * 16], c.carry_dram[:, h, :, :]).then_inc(carried, 16)
                sp.wait_ge(carried, 32 + 16 * H)

            @block.vector
            def _(v):
                do = Chain(v, step)
                for r in range(rounds):
                    v.tensor_copy(f[:, r * 512:(r + 1) * 512].rearrange("p (g h i) -> p g h i", g=4, h=H),
                                  by_group[:, r * 4:(r + 1) * 4]).then_inc(arranged, 1)
                v.wait_ge(copied, rounds)
                do(v.tensor_tensor_scan(f, c.link[:, 0:n], e, -BIG, ALU.add, ALU.max))
                do(v.tensor_tensor_scan(m[:, ::-1], c.link[:, 1:n + 1][:, ::-1], f[:, ::-1], -BIG, ALU.add, ALU.max))
                m3 = m.rearrange("p (g e) -> p g e", e=P)
                do(v.tensor_copy(ends[:, 0, :], m3[:, :, 0]))
                do(v.tensor_copy(ends[:, 1, :], m3[:, :, P - 1]))
                v.sem_inc(saved, 1)
                do(v.tensor_tensor(wl, c.item_whole, c.item_link[:, 0:ITEMS], ALU.add))
                do(v.tensor_tensor(wr, c.item_whole, c.item_link[:, 1:ITEMS + 1], ALU.add))
                v.wait_ge(carried, 32)
                for k in range(2):
                    do(v.tensor_copy(seq[:, k].rearrange("p (g i) -> p i g", i=16), ends_t[:, k]))
                do(v.tensor_tensor_scan(fwd, wl, seq[:, 1], -BIG, ALU.add, ALU.max))
                do(v.tensor_tensor_scan(back[:, ::-1], wr[:, ::-1], seq[:, 0][:, ::-1], -BIG, ALU.add, ALU.max))
                do(v.memset(seq.rearrange("p k i -> p (k i)"), -BIG))
                do(v.tensor_tensor(seq[:, 0, 1:], fwd[:, 0:ITEMS - 1], c.item_link[:, 1:ITEMS], ALU.add))
                do(v.tensor_tensor(seq[:, 1, 0:ITEMS - 1], back[:, 1:], c.item_link[:, 1:ITEMS], ALU.add))
                for k in range(2):
                    do(v.tensor_copy(ends_t[:, k], seq[:, k].rearrange("p (g i) -> p i g", i=16)))
                v.sem_inc(seq_done, 1)
                v.wait_ge(carried, 32 + 16 * H)
                do(v.memset(c.scores[:, ITEMS * H:(ITEMS + 16) * H], 0.0))
                for r in range(rounds):
                    cols, gs = slice(r * 512, (r + 1) * 512), slice(r * 4, r * 4 + 4)
                    parts = ((c.to_first, f[:, cols]), (c.to_last, spare[:, r % 2]))
                    for k, (mask, to) in enumerate(parts):
                        v.tensor_tensor(to.rearrange("p (g e) -> p g e", e=P),
                                        mask[:, cols].rearrange("p (g e) -> p g e", e=P),
                                        bc(ends[:, k, gs].unsqueeze(2), [P, 4, P]), ALU.add).then_inc(come, 1)
                    for k, (mask, to) in enumerate(parts):
                        v.wait_ge(come, r * 4 + 2 * k + 1 + (k == 0))
                        v.tensor_tensor(m[:, cols], m[:, cols], to, ALU.max).then_inc(come, 1)
                    v.wait_ge(come, r * 4 + 4)
                    v.tensor_tensor(e[:, cols], e[:, cols], m[:, cols], ALU.subtract).then_inc(ready, 1)


SUMW = D + H


def edge_sums(c, table, weighted, name):
    nc = c.nc
    width = D if weighted else D + 2
    ring = c.rows_a[:, 0:RING * SUMW].rearrange("p (s d) -> p s d", d=SUMW)
    o = RING * SUMW
    s_buf = c.rows_a[:, o:o + 2048].rearrange("p (b i n) -> p b i n", b=4, i=BATCH)
    msg = c.rows_a[:, o + 2048:o + 2048 + 4 * BATCH * SUMW].rearrange("p (b i n) -> p b i n", b=4, i=BATCH)
    nw = SUMW if weighted else width
    with Semaphores(nc) as s:
        def sem(n):
            return s.sem(f"{name}_{n}")
        staged, gate, made, weights = sem("idx"), sem("gate"), sem("onehot"), sem("weights")
        msgs, summed, added, cleared = sem("messages"), sem("summed"), sem("added"), sem("cleared")
        ones = sem("ones")
        landed = [sem(f"landed{u}") for u in range(RING)]
        idx = s.enter_context(nc.sbuf_tensor(f"{name}_idx", [P, RING], U32))
        with nc.Block() as block:
            @block.gpsimd
            def _(pool):
                if not weighted:
                    pool.wait_ge(ones, 1)
                    pool.sem_inc(gate, 1)
                gather_rows(pool, table, ring, idx, staged, gate, landed, weighted)

            @block.scalar
            def _(a):
                free, per_batch = (msgs, 2) if weighted else (summed, 1)
                for h in range(2):
                    stage_indices(c, a, idx, staged, free, 0, h, per_batch)
                with a.Fori(0, BATCHES // 4) as i:
                    for q in range(4):
                        if weighted:
                            b = i * 4 + q
                            a.wait_ge(summed, b + 1)
                            a.activation(msg[:, q, :, D:SUMW],
                                         c.scores[:, bass.ds(b * BATCH * H, BATCH * H)].rearrange("p (i h) -> p i h", h=H),
                                         ACT.Copy).then_inc(weights, 1)
                        if q % 2 == 0:
                            stage_indices(c, a, idx, staged, free, i + 1, q // 2, per_batch)

            @block.vector
            def _(v):
                v.sem_inc(added, 2 * BATCH)
                v.sem_inc(msgs, 2 * (RING // BATCH))
                if not weighted:
                    v.memset(ring[:, :, D:SUMW], 1.0).then_inc(ones, 1)
                v.memset(c.rows_b[:, 0:NT * SUMW], 0.0).then_inc(cleared, 1)
                v.wait_ge(cleared, 1)

                def message(i, q, b, half):
                    lo, hi = half * BATCH // 2, (half + 1) * BATCH // 2
                    for u in range(lo, hi):
                        v.wait_ge(landed[q * BATCH + u], i * 16 + 16)
                    v.tensor_tensor(msg[:, q, lo:hi, 0:D].rearrange("p i (h k) -> p i h k", k=DK),
                                    ring[:, q * BATCH + lo:q * BATCH + hi, 0:D].rearrange("p i (h k) -> p i h k", k=DK),
                                    bc(c.scores[:, bass.ds(b * BATCH * H + lo * H, BATCH // 2 * H)]
                                       .rearrange("p (i h) -> p i h", h=H).unsqueeze(3), [P, BATCH // 2, H, DK]),
                                    ALU.mult).then_inc(msgs, 1)

                for b in range(2):
                    one_hot(c, v, s_buf, b, b).then_inc(made, 1)
                    if weighted:
                        message(0, b, b, 0)
                        message(0, b, b, 1)
                with v.Fori(0, BATCHES // 4) as i:
                    for q in range(4):
                        b, par = i * 4 + q, q % 2
                        one_hot(c, v, s_buf, b + 2, (q + 2) % 4).then_inc(made, 1)
                        tiles = load_tiles(v, c, b)
                        v.wait_ge(summed, b + 5)
                        for u in range(BATCH):
                            ps = c.ps[:, (par * BATCH + u) * 512:(par * BATCH + u) * 512 + nw]
                            to = c.rows_b[:, bass.ds(tiles[u] * SUMW, nw)]
                            v.wait_ge(added, b * BATCH + u + 2 * BATCH)
                            v.tensor_tensor(to, to, ps, ALU.add).then_inc(added, 1)
                            if weighted and u < 2:
                                message(i + (q + 2) // 4, (q + 2) % 4, b + 2, u)
                v.wait_ge(added, ITEMS + 2 * BATCH)

            @block.tensor
            def _(pe):
                pe.sem_inc(summed, 4)
                with pe.Fori(0, BATCHES // 4) as i:
                    for q in range(4):
                        b, par = i * 4 + q, q % 2
                        pe.wait_ge(made, b + 1)
                        pe.wait_ge(added, b * BATCH + BATCH)
                        if weighted:
                            pe.wait_ge(weights, b + 1)
                            pe.wait_ge(msgs, b * 2 + 2 + 2 * (RING // BATCH))
                        else:
                            for u in range(BATCH):
                                pe.wait_ge(landed[q * BATCH + u], i * 16 + 16)
                        for u in range(BATCH):
                            to = (par * BATCH + u) * 512
                            rhs = msg[:, q, u, :] if weighted else ring[:, q * BATCH + u, 0:nw]
                            mm = pe.matmul(c.ps[:, to:to + nw], s_buf[:, q, u, :], rhs, start=True, stop=True)
                        mm.then_inc(summed, 1)


def rows3(ap, tiles=NT):
    return ap[:, 0:tiles * D].rearrange("p (t d) -> p t d", d=D)


def row_bc(ap):
    return ap.rearrange("(a n) -> a n", a=1).broadcast_to([P, ap.shape[0]])


def attention_out(c, wo, name, x=None):
    nc = c.nc
    w = c.scores[:, 0:512].rearrange("p (k n) -> p k n", k=2)
    rows = c.scores[:, 512:1536].rearrange("p (b t d) -> p b t d", b=2, t=2)
    rows_t = c.scores[:, 1536:2560].rearrange("p (b n) -> p b n", b=2)
    inv = c.scores[:, 2560:2560 + NT * H]
    with Semaphores(nc) as s:
        def sem(n):
            return s.sem(f"{name}_{n}")
        loaded, staged, turned, copied = sem("loaded"), sem("staged"), sem("turned"), sem("copied")
        used, out_done, step = sem("used"), sem("out_done"), sem("step")
        h_loaded = [sem(f"h_loaded{u}") for u in range(2)]
        zeroed, x_loaded, taken = sem("zeroed"), sem("x_loaded"), sem("stats")
        with nc.Block() as block:
            @block.sync
            def _(sp):
                sp.dma_start(w, wo.rearrange("(k p) n -> p k n", p=P)).then_inc(loaded, 16)

                def reload(g, parity):
                    to = c.rows_a[:, bass.ds(g * 2 * D, 2 * D)].rearrange("p (t d) -> p t d", t=2)
                    sp.dma_start(to, c.h_dram[bass.ds(g * 2 * P, 2 * P), :].rearrange("(t p) d -> p t d", p=P)
                                 ).then_inc(h_loaded[parity], 16)

                def body(g, parity, ahead):
                    if ahead > 1:
                        sp.wait_ge(h_loaded[parity], (g - parity) * 8 + 16)
                        reload(g + 2, parity)
                reload(0, 0)
                reload(1, 1)
                groups_ahead(sp, body)
                if x is not None:
                    sp.wait_ge(zeroed, 1)
                    to = rows3(c.rows_c)
                    sp.dma_start(to[:, 0:FULL_ROWS // P, :],
                                 x[0:FULL_ROWS, :].rearrange("(t p) d -> p t d", p=P)).then_inc(x_loaded, 16)
                    sp.dma_start(to[0:LAST_ROWS, FULL_ROWS // P, :], x[FULL_ROWS:N, :]).then_inc(x_loaded, 16)
                    sp.wait_ge(x_loaded, 32)

            @block.scalar
            def _(a):
                a.sem_inc(copied, 2)

                def body(g, parity, last):
                    a.wait_ge(turned, g + 3)
                    a.wait_ge(used, g + 1)
                    a.activation(rows_t[:, parity], c.ps[:, parity * 512:parity * 512 + 512], ACT.Copy).then_inc(copied, 1)
                groups(a, body)

            @block.tensor
            def _(pe):
                pe.sem_inc(turned, 2)
                pe.sem_inc(used, 2)
                pe.wait_ge(loaded, 16)

                def flip(g, parity):
                    pe.wait_ge(staged, g + 1)
                    pe.wait_ge(copied, g + 1)
                    turn(pe, c, rows[:, parity].rearrange("p t d -> p (t d)"), parity).then_inc(turned, 1)
                flip(0, 0)

                def body(g, parity, last):
                    if not last:
                        flip(g + 1, 1 - parity)
                    pe.wait_ge(copied, g + 3)
                    pe.wait_ge(out_done, g + 1)
                    for u in range(2):
                        for k in range(2):
                            to = (2 + parity) * 512 + u * D
                            x = rows_t[:, parity, k * 2 * P + u * P:k * 2 * P + u * P + P]
                            mm = pe.matmul(c.ps[:, to:to + D], x, w[:, k, :], start=(k == 0), stop=(k == 1))
                    mm.then_inc(used, 1)
                groups(pe, body)

            @block.vector
            def _(v):
                v.sem_inc(out_done, 2)
                if x is not None:
                    v.memset(c.rows_c[:, FULL_ROWS // P * D:NT * D], 0.0).then_inc(zeroed, 1)

                z = c.rows_b[:, 0:NT * SUMW].rearrange("p (t n) -> p t n", n=SUMW)[:, :, D:SUMW]
                inv3 = inv.rearrange("p (t h) -> p t h", h=H)
                do = Chain(v, step)
                do(v.tensor_scalar(inv3, z, 1e-9, None, ALU.add))
                do(v.reciprocal(inv, inv))

                def norm(g, parity):
                    sums = c.rows_b[:, bass.ds(g * 2 * SUMW, 2 * SUMW)].rearrange("p (t n) -> p t n", t=2)
                    v.wait_ge(turned, g + 1)
                    v.tensor_tensor(rows[:, parity].rearrange("p t (h k) -> p t h k", k=DK),
                                    sums[:, :, 0:D].rearrange("p t (h k) -> p t h k", k=DK),
                                    bc(inv[:, bass.ds(g * 2 * H, 2 * H)].rearrange("p (t h) -> p t h", t=2).unsqueeze(3),
                                       [P, 2, H, DK]), ALU.mult).then_inc(staged, 1)
                norm(0, 0)
                norm(1, 1)

                def body(g, parity, ahead):
                    if ahead > 1:
                        norm(g + 2, parity)
                    v.wait_ge(h_loaded[parity], (g - parity) * 8 + 16)
                    v.wait_ge(used, g + 3)
                    to = c.rows_a[:, bass.ds(g * 2 * D, 2 * D)]
                    v.tensor_tensor(to, to, c.ps[:, (2 + parity) * 512:(2 + parity) * 512 + 512], ALU.add).then_inc(out_done, 1)
                    v.wait_ge(out_done, g + 3)
                    for u in range(2):
                        row_stats(v, c, c.rows_a, g * 2 + u, taken)
                groups_ahead(v, body)
                v.wait_ge(taken, NT)


class FfnRoom:

    def __init__(self, c, ctx):
        def sb(name, n, **split):
            a = ctx.enter_context(c.nc.sbuf_tensor(f"ffn_{name}", [P, n], F32))[:, :]
            return a.rearrange(*split.pop("by"), **split) if split else a
        self.raw = sb("raw", 2048)
        self.hidden = self.raw.rearrange("p (j n) -> p j n", j=4)
        self.w1_raw = self.raw.rearrange("p (k n) -> p k n", k=2)
        self.w2_raw = self.raw.rearrange("p (k n) -> p k n", k=8)
        self.rows = [sb(f"rows{u}", 512) for u in range(2)]
        self.b1, self.b2 = sb("b1", 8), sb("b2", D)
        self.w1 = [sb(f"w1_{x}", 2048, by=("p (k n) -> p k n",), k=2) for x in ("high", "low")]
        self.w2 = [sb(f"w2_{x}", 2048, by=("p (k n) -> p k n",), k=8) for x in ("high", "low")]
        self.rows_t = [sb(f"rows_t_{x}", 1024, by=("p (b n) -> p b n",), b=2) for x in ("high", "low")]
        self.hid = [sb(f"hid_{x}", 4096, by=("p (b k n) -> p b k n",), b=2, k=8) for x in ("high", "low")]


def ffn(c, room, func, target, name, clear_slots=False):
    nc = c.nc
    K2 = HID // P
    with Semaphores(nc) as s:
        def sem(n):
            return s.sem(f"{name}_{n}")
        chunk, acted, summed, out_done = sem("chunk"), sem("acted"), sem("summed"), sem("out_done")
        biased, taken, zeroed, filled = sem("biased"), sem("stats"), sem("zeroed"), sem("filled")
        zeros = c.rows_c[:, NT * D:NT * D + D]
        staged, turned, row_high, rows_split, used = (
            sem(n) for n in ("staged", "turned", "row_high", "rows_split", "used"))
        hid_high, hid_split = sem("hid_high"), sem("hid_split")
        with nc.Block() as block:
            if clear_slots:
                @block.sync
                def _(sp):
                    sp.wait_ge(zeroed, 1)
                    sp.dma_start(c.slot_in.rearrange("(t p) d -> p t d", p=P),
                                 bc(zeros.unsqueeze(1), [P, SLOT_TILES, D])).then_inc(filled, 16)
                    sp.wait_ge(filled, 16)

            @block.scalar
            def _(a):
                a.sem_inc(acted, 4)

                def stage(g, parity):
                    a.wait_ge(turned, g + 1)
                    a.activation(room.rows[parity], c.rows_a[:, bass.ds(g * 2 * D, 2 * D)], ACT.Copy).then_inc(staged, 1)

                def hidden(g):
                    for k in range(K2):
                        if k % 2 == 0:
                            a.wait_ge(hid_split, g * (K2 // 2) + k // 2 + 1)
                        a.wait_ge(chunk, g * K2 + k + 1)
                        at = (2 + k % 4) * 512
                        a.activation(room.hidden[:, k // 2, k % 2 * 2 * P:(k % 2 + 1) * 2 * P], c.ps[:, at:at + 2 * P], func,
                                     bias=room.b1[:, k:k + 1]).then_inc(acted, 1)
                stage(0, 0)
                stage(1, 1)
                hidden(0)

                def body(g, parity, ahead):
                    if ahead > 1:
                        stage(g + 2, parity)
                    if ahead > 0:
                        hidden(g + 1)
                groups_ahead(a, body)

            @block.tensor
            def _(pe):
                pe.sem_inc(turned, 2)
                pe.sem_inc(used, 2)
                pe.sem_inc(summed, 2)

                def flip(g, parity):
                    pe.wait_ge(staged, g + 1)
                    pe.wait_ge(rows_split, g + 1)
                    turn(pe, c, room.rows[parity], parity).then_inc(turned, 1)

                def chunks(g, parity):
                    pe.wait_ge(rows_split, g + 3)
                    for n in range(K2):
                        pe.wait_ge(acted, g * K2 + n + 1)
                        at, w = (2 + n % 4) * 512, slice(n * P, (n + 1) * P)
                        for k in range(2):
                            x = slice(k * 2 * P, (k + 1) * 2 * P)
                            mm = split_matmul(pe, c.ps[:, at:at + 2 * P], [m[:, k, w] for m in room.w1],
                                              [m[:, parity, x] for m in room.rows_t], k == 0, k == 1)
                        mm.then_inc(chunk, 1)
                        if n == K2 - 1:
                            pe.sem_inc(used, 1)

                def sums(g, parity):
                    pe.wait_ge(out_done, g + 1)
                    for u in range(2):
                        at, x = (6 + parity) * 512 + u * D, slice(u * P, (u + 1) * P)
                        for n in range(K2):
                            if u == 0 and n % 2 == 0:
                                pe.wait_ge(hid_split, g * (K2 // 2) + n // 2 + 5)
                            mm = split_matmul(pe, c.ps[:, at:at + D], [m[:, parity, n, x] for m in room.hid],
                                              [m[:, n, :] for m in room.w2], n == 0, n == K2 - 1)
                    mm.then_inc(summed, 1)
                flip(0, 0)
                chunks(0, 0)
                flip(1, 1)

                def body(g, parity, ahead):
                    if ahead > 0:
                        chunks(g + 1, 1 - parity)
                    if ahead > 1:
                        flip(g + 2, parity)
                    sums(g, parity)
                groups_ahead(pe, body)

            @block.vector
            def _(v):
                v.sem_inc(rows_split, 2)
                v.sem_inc(out_done, 2)
                v.sem_inc(hid_split, 4)
                if clear_slots:
                    v.memset(zeros, 0.0).then_inc(zeroed, 1)

                def split_rows(g, parity):
                    v.wait_ge(used, g + 1)
                    v.wait_ge(turned, g + 3)
                    ps = c.ps[:, parity * 512:(parity + 1) * 512]
                    take_high(v, room.rows_t[0][:, parity], ps).then_inc(row_high, 1)
                    v.wait_ge(row_high, g + 1)
                    take_low(v, room.rows_t[1][:, parity], ps, room.rows_t[0][:, parity]).then_inc(rows_split, 1)

                def split_hidden(g, parity):
                    v.wait_ge(summed, g + 1)
                    for n in range(K2 // 2):
                        high, low = (x[:, parity, 2 * n:2 * n + 2, :].rearrange("p k n -> p (k n)") for x in room.hid)
                        v.wait_ge(acted, g * K2 + 2 * n + 6)
                        take_high(v, high, room.hidden[:, n]).then_inc(hid_high, 1)
                        v.wait_ge(hid_high, g * (K2 // 2) + n + 1)
                        take_low(v, low, room.hidden[:, n], high).then_inc(hid_split, 1)

                split_rows(0, 0)
                split_hidden(0, 0)
                split_rows(1, 1)

                def body(g, parity, ahead):
                    if ahead > 0:
                        split_hidden(g + 1, 1 - parity)
                    if ahead > 1:
                        split_rows(g + 2, parity)
                    v.wait_ge(summed, g + 3)
                    to = target[:, bass.ds(g * 2 * D, 2 * D)]
                    v.tensor_tensor(to, to, c.ps[:, (6 + parity) * 512:(7 + parity) * 512], ALU.add).then_inc(out_done, 1)
                    v.wait_ge(out_done, g + 3)
                    to3 = to.rearrange("p (t d) -> p t d", t=2)
                    v.tensor_tensor(to3, to3, bc(room.b2.unsqueeze(1), [P, 2, D]), ALU.add).then_inc(biased, 1)
                    v.wait_ge(biased, g + 1)
                    for u in range(2):
                        row_stats(v, c, target, g * 2 + u, taken)
                groups_ahead(v, body)
                v.wait_ge(taken, NT)


def mlp_weights(c, room, w1, b1, w2, b2):
    nc = c.nc
    with Semaphores(nc) as s:
        first, second, bias, w1_split, step = (
            s.sem(f"mlpw_{n}") for n in ("first", "second", "bias", "w1_split", "step"))
        with nc.Block() as block:
            @block.sync
            def _(sp):
                sp.dma_start(room.w1_raw, w1.rearrange("(k p) n -> p k n", p=P)).then_inc(first, 16)
                with nc.allow_non_contiguous_dma("a bias, one number a partition"):
                    sp.dma_start(room.b1, b1.rearrange("(k p) -> p k", p=P)).then_inc(bias, 16)
                sp.dma_start(room.b2, row_bc(b2)).then_inc(bias, 16)
                sp.wait_ge(w1_split, 1)
                sp.dma_start(room.w2_raw, w2.rearrange("(k p) n -> p k n", p=P)).then_inc(second, 16)
                sp.wait_ge(bias, 32)

            @block.vector
            def _(v):
                do = Chain(v, step)
                v.wait_ge(first, 16)
                split(do, v, room.w1, room.w1_raw)
                v.sem_inc(w1_split, 1)
                v.wait_ge(second, 16)
                split(do, v, room.w2, room.w2_raw)


def route_all(c, room, work, wr, br, w1, b1, w2, b2):
    nc = c.nc
    capacity = float(-(-N * 5 // (NE * 4)))
    o = [0]

    def take(n, dt=F32):
        a = work[:, o[0]:o[0] + n]
        o[0] += n
        return a if dt == F32 else a.bitcast(dt)
    total, wr_sb, br_sb, ones = take(D), take(2 * NE).rearrange("p (k n) -> p k n", k=2), take(NE), take(1)
    mean_t, wide = take(2), take(2 * P).rearrange("p (k n) -> p k n", k=2)
    lg, t8, p8, one = take(NE), take(NE), take(NE), take(1)
    best, best_i, best_f = take(8), take(8, U32), take(8)
    weight = take(2)
    row_no = take(4)
    idx1 = take(4).rearrange("p (j k) -> p j k", j=2)
    idx2 = take(8).rearrange("p (j k) -> p j k", j=2)
    idx1u, idx2u = take(4, U32).rearrange("p (j k) -> p j k", j=2), take(8, U32).rearrange("p (j k) -> p j k", j=2)
    b2_rows = take(2 * D).rearrange("p (j n) -> p j n", j=2)
    with Semaphores(nc) as s:
        def sem(n):
            return s.sem(f"route_{n}")
        loaded, step, total_ready, mean_ps, wide_ready = sem("loaded"), sem("step"), sem("total"), sem("mean"), sem("wide")
        logits_ps, ask, exped, idx_ready, landed, rowno = sem("logits"), sem("ask"), sem("exped"), sem("idx"), sem("landed"), sem("rowno")
        w1_landed, w1_split, gate = sem("w1_landed"), sem("w1_split"), sem("gate")
        with nc.Block() as block:
            @block.sync
            def _(sp):
                sp.dma_start(wr_sb, wr.rearrange("(k p) n -> p k n", p=P)).then_inc(loaded, 16)
                sp.dma_start(br_sb, row_bc(br)).then_inc(loaded, 16)

            @block.gpsimd
            def _(pool):
                pool.iota(row_no, [[P, 4]], base=0, channel_multiplier=1, allow_small_or_imprecise_dtypes=True).then_inc(rowno, 1)
                pool.wait_ge(idx_ready, 1)
                w1_rows, w2_rows = w1.rearrange("e d n -> (e d) n"), w2.rearrange("e n d -> (e n) d")
                b1_rows = b1.rearrange("e (n a) -> (e n) a", a=1)

                def fetch(to, table, idx, done=landed):
                    pool.indirect_dma_start(to, None, table, bass.IndirectOffsetOnAxis(ap=idx, axis=0)).then_inc(done, 16)
                for j in range(2):
                    for k in range(2):
                        fetch(room.w1_raw[:, k, j * HE:(j + 1) * HE], w1_rows, idx1u[:, j, k:k + 1], w1_landed)
                for j in range(2):
                    for k in range(4):
                        fetch(room.b1[:, j * 4 + k:j * 4 + k + 1], b1_rows, idx2u[:, j, k:k + 1])
                    fetch(b2_rows[:, j, :], b2, best_i[:, j:j + 1])
                pool.wait_ge(w1_split, 1)
                pool.sem_inc(gate, 1)
                for j in range(2):
                    for k in range(4):
                        fetch(room.w2_raw[:, j * 4 + k, :], w2_rows, idx2u[:, j, k:k + 1])

            @block.tensor
            def _(pe):
                pe.wait_ge(total_ready, 1)
                for k in range(2):
                    mm = pe.matmul(c.ps[:, k:k + 1], total[:, k * P:(k + 1) * P], ones, start=True, stop=True)
                mm.then_inc(mean_ps, 1)
                pe.wait_ge(wide_ready, 1)
                pe.wait_ge(loaded, 32)
                for k in range(2):
                    mm = pe.matmul(c.ps[:, 512:512 + NE], wide[:, k, :], wr_sb[:, k, :], start=(k == 0), stop=(k == 1))
                mm.then_inc(logits_ps, 1)

            @block.scalar
            def _(a):
                for n, x in enumerate((lg, p8, weight[:, 1:2])):
                    a.wait_ge(ask, n + 1)
                    a.activation(x, x, ACT.Exp).then_inc(exped, 1)

            @block.vector
            def _(v):
                do = Chain(v, step)
                do(v.memset(ones, 1.0))
                do(v.tensor_reduce(total, c.rows_a[:, 0:FULL_ROWS // P * D].rearrange("p (t d) -> p d t", d=D), AX.X, ALU.add))
                last = FULL_ROWS // P * D
                do(v.tensor_tensor(total[0:LAST_ROWS], total[0:LAST_ROWS], c.rows_a[0:LAST_ROWS, last:last + D], ALU.add))
                v.sem_inc(total_ready, 1)
                v.wait_ge(mean_ps, 1)
                do(v.tensor_scalar(mean_t, c.ps[:, 0:2], 1.0 / N, None, ALU.mult))
                do(v.tensor_copy(wide, bc(mean_t.unsqueeze(2), [P, 2, P])))
                v.sem_inc(wide_ready, 1)
                v.wait_ge(logits_ps, 1)
                do(v.tensor_tensor(lg, c.ps[:, 512:512 + NE], br_sb, ALU.add))

                def softmax(x, n):
                    do(v.tensor_reduce(one, x, AX.X, ALU.max))
                    do(v.tensor_scalar(x, x, one, None, ALU.subtract))
                    v.sem_inc(ask, 1)
                    v.wait_ge(exped, n)
                    do(v.tensor_reduce(one, x, AX.X, ALU.add))
                    do(v.reciprocal(one, one))
                    do(v.tensor_scalar(x, x, one, None, ALU.mult))
                softmax(lg, 1)
                do(v.tensor_scalar(t8, lg, float(N), capacity, ALU.mult, ALU.max))
                do(v.reciprocal(t8, t8))
                do(v.tensor_scalar(t8, t8, capacity, None, ALU.mult))
                do(v.tensor_tensor(p8, lg, t8, ALU.mult))
                softmax(p8, 2)
                do(v.max(best, p8))
                do(v.max_index(best_i, best, p8))
                do(v.tensor_copy(best_f, best_i))
                do(v.tensor_tensor(weight[:, 1:2], best[:, 1:2], best[:, 0:1], ALU.subtract))
                v.sem_inc(ask, 1)
                v.wait_ge(rowno, 1)
                for j in range(2):
                    do(v.tensor_scalar(one, best_f[:, j:j + 1], float(D), None, ALU.mult))
                    do(v.tensor_scalar(idx1[:, j], row_no[:, 0:2], one, None, ALU.add))
                    do(v.tensor_scalar(one, best_f[:, j:j + 1], float(HE), None, ALU.mult))
                    do(v.tensor_scalar(idx2[:, j], row_no, one, None, ALU.add))
                do(v.tensor_copy(idx1u, idx1))
                do(v.tensor_copy(idx2u, idx2))
                v.sem_inc(idx_ready, 1)
                v.wait_ge(exped, 3)
                do(v.tensor_scalar(one, weight[:, 1:2], 1.0, None, ALU.add))
                do(v.reciprocal(weight[:, 0:1], one))
                do(v.tensor_tensor(weight[:, 1:2], weight[:, 1:2], weight[:, 0:1], ALU.mult))
                v.wait_ge(w1_landed, 4 * 16)
                split(do, v, room.w1, room.w1_raw)
                v.sem_inc(w1_split, 1)
                v.wait_ge(landed, 18 * 16)
                for j in range(2):
                    r = room.w2_raw[:, j * 4:j * 4 + 4, :]
                    do(v.tensor_scalar(r, r, weight[:, j:j + 1], None, ALU.mult))
                    do(v.tensor_scalar(b2_rows[:, j], b2_rows[:, j], weight[:, j:j + 1], None, ALU.mult))
                split(do, v, room.w2, room.w2_raw)
                do(v.tensor_tensor(room.b2, b2_rows[:, 0], b2_rows[:, 1], ALU.add))


def sage_products(c, w_self, w_neigh):
    nc = c.nc
    w = c.scores[:, 0:1024].rearrange("p (k n) -> p k n", k=2)
    rows = [c.scores[:, 1024 + k * 512:1536 + k * 512] for k in range(2)]
    rows_t = c.scores[:, 2048:3072].rearrange("p (b n) -> p b n", b=2)
    neigh = c.scores[:, 3072:4096].rearrange("p (b n) -> p b n", b=4)
    left = c.scores[:, 4096:5120].rearrange("p (b n) -> p b n", b=4)
    top = [c.scores[:, 5120 + 8 * u:5128 + 8 * u] for u in range(2)]
    NEG = -3.0e38
    STEPS = 8
    with Semaphores(nc) as s:
        def sem(n):
            return s.sem(f"sage_{n}")
        loaded, out_done, ready, step, neigh_out = sem("loaded"), sem("out_done"), sem("ready"), sem("step"), sem("neigh_out")
        stored, buf_free, gate = [sem(f"stored{u}") for u in range(4)], sem("buf_free"), sem("gate")
        f = Front(c, s, "sage", rows, rows_t, c.rows_a)
        with nc.Block() as block:
            @block.sync
            def _(sp):
                sp.dma_start(w[:, :, 0:D], w_self.rearrange("(k p) n -> p k n", p=P)).then_inc(loaded, 16)
                sp.dma_start(w[:, :, D:2 * D], w_neigh.rearrange("(k p) n -> p k n", p=P)).then_inc(loaded, 16)

                def body(g, parity, last):
                    for u in range(2):
                        b = 2 * parity + u
                        sp.wait_ge(ready, g * 2 + u + 1)
                        sp.dma_start(c.k_dram[bass.ds(g * 2 * P + u * P, P), :], left[:, b, :]).then_inc(stored[b], 16)
                    for u in range(2):
                        sp.wait_ge(stored[2 * parity + u], (g - parity) * 8 + 16)
                        sp.sem_inc(buf_free, 1)
                groups(sp, body)

            @block.scalar
            def _(a):
                a.sem_inc(neigh_out, 4)
                f.start_copies(a)
                f.stage(a, 0, 0)
                f.copy(a, 0, 0)

                def body(g, parity, last):
                    if not last:
                        f.stage(a, g + 1, 1 - parity)
                        f.copy(a, g + 1, 1 - parity)
                    a.wait_ge(f.used, g + 3)
                    for u in range(2):
                        b = 2 * parity + u
                        a.wait_ge(buf_free, g * 2 + u + 1)
                        at = (4 + parity) * 512 + u * D
                        a.activation(neigh[:, b, :], c.ps[:, at:at + D], ACT.Copy).then_inc(neigh_out, 1)
                groups(a, body)

            @block.tensor
            def _(pe):
                f.start_pe(pe)
                pe.wait_ge(loaded, 32)
                f.turn(pe, 0, 0)

                def body(g, parity, last):
                    if not last:
                        f.turn(pe, g + 1, 1 - parity)
                    pe.wait_ge(f.copied, g + 3)
                    pe.wait_ge(out_done, g + 1)
                    pe.wait_ge(neigh_out, g * 2 + 2)
                    for u in range(2):
                        for half in range(2):
                            at = (2 + 2 * half + parity) * 512 + u * D
                            for k in range(2):
                                x = rows_t[:, parity, k * 2 * P + u * P:k * 2 * P + u * P + P]
                                mm = pe.matmul(c.ps[:, at:at + D], x, w[:, k, half * D:(half + 1) * D],
                                               start=(k == 0), stop=(k == 1))
                    mm.then_inc(f.used, 1)
                groups(pe, body)

            @block.vector
            def _(v):
                v.sem_inc(out_done, 2)
                v.sem_inc(buf_free, 4)
                def body(g, parity, last):
                    v.wait_ge(f.used, g + 3)
                    to = c.rows_c[:, bass.ds(g * 2 * D, 2 * D)]
                    v.tensor_tensor(to, to, c.ps[:, (2 + parity) * 512:(3 + parity) * 512], ALU.add).then_inc(out_done, 1)
                    v.wait_ge(neigh_out, g * 2 + 6)
                    tiles = [(u, 2 * parity + u) for u in range(2)]
                    for r in range(4):
                        n = g * 2 * STEPS + 4 * r
                        for u, b in tiles:
                            v.sem_inc(gate, 1)
                            v.max(top[u], neigh[:, b, :] if r == 0 else left[:, b, :]).then_inc(step, 1)
                            if u == 0 and r > 0:
                                v.wait_ge(step, n)
                        for u, b in tiles:
                            v.wait_ge(step, n + 1 + u)
                            v.sem_inc(gate, 1)
                            v.match_replace(left[:, b, :], top[u], neigh[:, b, :] if r == 0 else left[:, b, :],
                                            NEG).then_inc(step, 1)
                        v.wait_ge(step, n + 3)
                    v.wait_ge(step, (g + 1) * 2 * STEPS)
                    for u, b in tiles:
                        v.scalar_tensor_tensor(left[:, b, :], left[:, b, :], NEG, neigh[:, b, :], ALU.is_equal,
                                               ALU.mult).then_inc(ready, 1)
                groups(v, body)
                v.wait_ge(ready, NT)


def add_neighbours(c):
    nc = c.nc
    sums = c.rows_b[:, 0:NT * SUMW].rearrange("p (t n) -> p t n", t=NT)
    inv = c.small[:, 0:NT]
    with Semaphores(nc) as s:
        step, added = s.sem("neigh_step"), s.sem("neigh_added")
        with nc.Block() as block:
            @block.vector
            def _(v):
                do = Chain(v, step)
                do(v.tensor_scalar(inv, sums[:, :, D], 1.0, None, ALU.max))
                do(v.reciprocal(inv, inv))

                def add(t):
                    to = c.rows_c[:, bass.ds(t * D, D)]
                    v.scalar_tensor_tensor(to, c.rows_b[:, bass.ds(t * SUMW, D)], inv[:, bass.ds(t, 1)], to,
                                           ALU.mult, ALU.add).then_inc(added, 1)
                tiles_of_ten(v, 0, NT, add)
                v.wait_ge(added, NT)


def token_routes(c, gates, wr, br, w1):
    nc = c.nc
    wr_sb = c.scores[:, 0:16].rearrange("p (k n) -> p k n", k=2)
    br_sb = c.scores[:, 16:24]
    lg = c.scores[:, 24:56].rearrange("p (b t n) -> p b t n", b=2, t=2)
    mx = c.scores[:, 56:88].rearrange("p (b t n) -> p b t n", b=2, t=2)
    mi = c.scores[:, 88:120].bitcast(U32).rearrange("p (b t n) -> p b t n", b=2, t=2)
    rows = [c.scores[:, 128 + k * 512:640 + k * 512] for k in range(2)]
    rows_t = c.scores[:, 1152:2176].rearrange("p (b n) -> p b n", b=2)
    iota8 = c.scores[:, 2176:2184]
    val = c.scores[:, 2184:2184 + 2 * NT].rearrange("p (t n) -> p t n", n=2)
    sel = c.scores[:, 2284:2284 + 2 * NT].rearrange("p (t n) -> p t n", n=2)
    w0, w1_ = c.small[:, 0:NT], c.small[:, NT:2 * NT]
    pick = c.scores[:, 2384:2384 + NT * NE].rearrange("p (t n) -> p t n", n=NE)
    g3 = gates.rearrange("p (t n) -> p t n", n=NE)
    at = [3584]

    def take(size, shape=None, **k):
        a = c.scores[:, at[0]:at[0] + size]
        at[0] += size
        return a.rearrange(shape, **k) if shape else a
    hot = [take(NT * NE, "p (t n) -> p t n", n=NE) for _ in range(2)]
    chosen = take(NT * NE)
    before = take(P)
    ones = take(P)
    real = take(NT)
    per_tile = take(NT * NE, "p (n t) -> p n t", n=NE)
    upto = take(NT * NE, "p (n t) -> p n t", n=NE)
    n_rows, n_tiles, start, tiles_to = (take(NE) for _ in range(4))
    limit = c.small[:, 3 * NT:4 * NT]
    slot_no = c.stats[:, 0:SLOT_TILES]
    ended = c.rows_b[:, 8192:8192 + SLOT_TILES * NE].rearrange("p (s n) -> p s n", n=NE)
    wider = c.rows_b[:, 9216:9216 + NT * NE].rearrange("p (n t) -> p n t", n=NE)
    expert_f = c.rows_b[:, 9728:9728 + 4 * (SLOT_ROUNDS + 1)]
    place_f = c.rows_b[:, 9856:9856 + NT]
    packed = c.rows_b[0:1, 9984:9984 + SLOT_ROUNDS]
    assert at[0] <= (ITEMS + 16) * H
    with Semaphores(nc) as s:
        def sem(n):
            return s.sem(f"tok_{n}")
        loaded, iotas, lg_done, step = sem("loaded"), sem("iotas"), sem("lg_done"), sem("step")
        gate = sem("gate")
        ranked, marked, w_loaded = sem("ranked"), sem("marked"), sem("w_loaded")
        s1, ask, exped = sem("s1"), sem("ask"), sem("exped")
        f = Front(c, s, "tok", rows, rows_t, c.rows_a)
        with nc.Block() as block:
            @block.sync
            def _(sp):
                sp.dma_start(wr_sb, wr.rearrange("(k p) n -> p k n", p=P)).then_inc(loaded, 16)
                sp.dma_start(br_sb, row_bc(br)).then_inc(loaded, 16)
                sp.dma_start(c.rows_b[:, 0:NE * 2 * HE].rearrange("p (e k n) -> p e k n", e=NE, k=2),
                             w1.rearrange("e (k p) n -> p e k n", p=P)).then_inc(w_loaded, 16)
                sp.wait_ge(w_loaded, 16)

            @block.gpsimd
            def _(pool):
                pool.iota(real, [[P, NT]], base=0, channel_multiplier=1, allow_small_or_imprecise_dtypes=True).then_inc(iotas, 1)
                pool.iota(limit, [[P, NT]], base=0, channel_multiplier=0, allow_small_or_imprecise_dtypes=True).then_inc(iotas, 1)
                pool.iota(slot_no, [[1, SLOT_TILES]], base=0, channel_multiplier=0,
                          allow_small_or_imprecise_dtypes=True).then_inc(iotas, 1)
                pool.iota(iota8, [[1, NE]], base=0, channel_multiplier=0, allow_small_or_imprecise_dtypes=True).then_inc(iotas, 1)

            @block.scalar
            def _(a):
                groups(a, lambda g, parity, last: f.stage(a, g, parity))
                a.wait_ge(ask, 1)
                a.activation(w1_, w1_, ACT.Exp).then_inc(exped, 1)

            @block.tensor
            def _(pe):
                f.start_pe(pe)
                pe.wait_ge(loaded, 32)
                f.turn(pe, 0, 0)

                def body(g, parity, last):
                    if not last:
                        f.turn(pe, g + 1, 1 - parity)
                    pe.wait_ge(f.copied, g + 3)
                    pe.wait_ge(lg_done, g + 1)
                    for u in range(2):
                        at = (2 + parity) * 512 + u * NE
                        for k in range(2):
                            x = rows_t[:, parity, k * 2 * P + u * P:k * 2 * P + u * P + P]
                            mm = pe.matmul(c.ps[:, at:at + NE], x, wr_sb[:, k, :], start=(k == 0), stop=(k == 1))
                    mm.then_inc(f.used, 1)
                groups(pe, body)

                pe.wait_ge(marked, 1)
                pe.matmul(c.ps[:, 1024:1024 + NT * NE], before, chosen, start=True, stop=True)
                pe.matmul(c.ps[:, 1536:1536 + NT * NE], ones, chosen, start=True, stop=True).then_inc(ranked, 1)

            @block.vector
            def _(v):
                do = Chain(v, step)
                f.start_copies(v)
                v.sem_inc(lg_done, 2)
                v.wait_ge(loaded, 32)
                v.wait_ge(iotas, 4)
                f.copy(v, 0, 0)
                S1 = 6

                def body(g, parity, last):
                    if not last:
                        f.copy(v, g + 1, 1 - parity)
                    v.wait_ge(f.used, g + 3)
                    at = (2 + parity) * 512
                    v.tensor_tensor(lg[:, parity], c.ps[:, at:at + 2 * NE].rearrange("p (t n) -> p t n", t=2),
                                    bc(br_sb.unsqueeze(1), [P, 2, NE]), ALU.add).then_inc(lg_done, 1)
                    v.wait_ge(lg_done, g + 3)
                    v.sem_inc(gate, 1)
                    for u in range(2):
                        v.max(mx[:, parity, u, :], lg[:, parity, u, :]).then_inc(s1, 1)
                    v.wait_ge(s1, g * S1 + 2)
                    v.sem_inc(gate, 1)
                    for u in range(2):
                        v.max_index(mi[:, parity, u, :], mx[:, parity, u, :], lg[:, parity, u, :]).then_inc(s1, 1)
                    v.wait_ge(s1, g * S1 + 4)
                    v.tensor_copy(val[:, bass.ds(g * 2, 2), :], mx[:, parity, :, 0:2]).then_inc(s1, 1)
                    v.tensor_copy(sel[:, bass.ds(g * 2, 2), :], mi[:, parity, :, 0:2]).then_inc(s1, 1)
                groups(v, body)
                v.wait_ge(s1, GROUPS2 * S1)
                do(v.tensor_tensor(w1_, val[:, :, 1], val[:, :, 0], ALU.subtract))
                v.sem_inc(ask, 1)
                v.wait_ge(exped, 1)
                do(v.tensor_scalar(w0, w1_, 1.0, None, ALU.add))
                do(v.reciprocal(w0, w0))
                do(v.tensor_tensor(w1_, w1_, w0, ALU.mult))
                wide8 = bc(iota8.unsqueeze(1), [P, NT, NE])
                for j in range(2):
                    do(v.tensor_tensor(hot[j], wide8, bc(sel[:, :, j:j + 1], [P, NT, NE]), ALU.is_equal))
                do(v.tensor_scalar(real, real, float(N), None, ALU.is_lt))
                chosen3 = chosen.rearrange("p (t n) -> p t n", n=NE)
                do(v.tensor_tensor(chosen3, hot[0], hot[1], ALU.add))
                do(v.tensor_tensor(chosen3, chosen3, bc(real.unsqueeze(2), [P, NT, NE]), ALU.mult))
                do(v.tensor_scalar(before, c.iota_n[:, :], c.iota_p[:, 0:1], None, ALU.is_gt))
                do(v.memset(ones, 1.0))
                v.sem_inc(marked, 1)
                do(v.tensor_tensor(g3, hot[0], bc(w0.unsqueeze(2), [P, NT, NE]), ALU.mult))
                do(v.tensor_tensor(pick, hot[1], bc(w1_.unsqueeze(2), [P, NT, NE]), ALU.mult))
                do(v.tensor_tensor(g3, g3, pick, ALU.add))

                v.wait_ge(ranked, 1)
                flat = upto.rearrange("p n t -> p (n t)")
                do(v.tensor_copy(per_tile, c.ps[:, 1536:1536 + NT * NE].rearrange("p (t n) -> p n t", n=NE)))
                do(v.memset(wider, 1.0))
                do(v.tensor_tensor_scan(flat, wider.rearrange("p n t -> p (n t)"), per_tile.rearrange("p n t -> p (n t)"),
                                        0.0, ALU.mult, ALU.add))
                do(v.tensor_copy(n_rows, upto[:, :, NT - 1]))
                do(v.tensor_tensor(upto, upto, per_tile, ALU.subtract))
                do(v.memset(start, 0.0))
                do(v.tensor_copy(start[:, 1:], n_rows[:, :NE - 1]))
                do(v.tensor_tensor(n_rows, n_rows, start, ALU.subtract))
                do(v.tensor_tensor(upto, upto, bc(start.unsqueeze(2), [P, NE, NT]), ALU.subtract))
                do(v.tensor_tensor(wider, bc(n_rows.unsqueeze(2), [P, NE, NT]), bc(limit.unsqueeze(1), [P, NE, NT]), ALU.is_gt))
                do(v.tensor_reduce(n_tiles, wider, AX.X, ALU.add))
                do(v.tensor_tensor_scan(tiles_to, ones[:, 0:NE], n_tiles, 0.0, ALU.mult, ALU.add))
                do(v.tensor_tensor(start, tiles_to, n_tiles, ALU.subtract))
                do(v.tensor_scalar(start, start, float(P), None, ALU.mult))
                do(v.tensor_tensor(upto, upto, bc(start.unsqueeze(2), [P, NE, NT]), ALU.add))
                do(v.tensor_tensor(chosen3, c.ps[:, 1024:1024 + NT * NE].rearrange("p (t n) -> p t n", n=NE),
                                   upto.rearrange("p n t -> p t n"), ALU.add))
                place = c.slots[:, :].rearrange("p (t j) -> p t j", j=2)
                for j in range(2):
                    do(v.tensor_tensor(hot[j], hot[j], chosen3, ALU.mult))
                    do(v.tensor_reduce(place_f, hot[j], AX.X, ALU.add))
                    do(v.tensor_copy(place[:, :, j], place_f))
                do(v.tensor_tensor(ended, bc(tiles_to.unsqueeze(1), [P, SLOT_TILES, NE]),
                                   bc(slot_no.unsqueeze(2), [P, SLOT_TILES, NE]), ALU.is_le))
                do(v.memset(expert_f, float(NE - 1)))
                do(v.tensor_reduce(expert_f[:, 0:SLOT_TILES], ended, AX.X, ALU.add))
                do(v.tensor_scalar(expert_f, expert_f, float(NE - 1), None, ALU.min))
                each = expert_f[0:1].rearrange("p (r u) -> p u r", u=4)
                do(v.tensor_copy(packed, each[:, 0, 0:SLOT_ROUNDS]))
                for u in range(1, 5):
                    source = each[:, u % 4, u // 4:u // 4 + SLOT_ROUNDS]
                    do(v.scalar_tensor_tensor(packed, source, float(1 << (EXPERT_BITS * u)), packed, ALU.mult, ALU.add))
                do(v.tensor_copy(c.slot_experts[:, :], packed))


def dispatch(c, gates, b2, b1_sb, b1):
    nc = c.nc
    rows = [c.scores[:, k * 512:(k + 1) * 512] for k in range(2)]
    b2_sb = c.scores[0:NE, 1024:1024 + D]
    g_buf = c.scores[:, 1280:1312].rearrange("p (b t n) -> p b t n", b=2, t=2)
    g_t = c.scores[0:NE, 1312:1824].rearrange("p (b n) -> p b n", b=2)
    with Semaphores(nc) as s:
        def sem(n):
            return s.sem(f"disp_{n}")
        staged, idx_ready, gate, sent, loaded = sem("staged"), sem("idx"), sem("gate"), sem("free"), sem("b2_loaded")
        g_staged, g_turned, g_copied, b_summed, b_added = (
            sem(n) for n in ("gates_staged", "gates_turned", "gates_copied", "bias_summed", "bias_added"))
        landed, b1_loaded = [sem(f"landed{u}") for u in range(2)], sem("b1_loaded")
        idx = s.enter_context(nc.sbuf_tensor("disp_idx_buf", [P, 8], U32))
        with nc.Block() as block:
            @block.scalar
            def _(a):
                def body(g, parity, last):
                    a.wait_ge(g_turned, g + 1)
                    a.activation(g_buf[:, parity], gates[:, bass.ds(g * 2 * NE, 2 * NE)].rearrange("p (t n) -> p t n", n=NE),
                                 ACT.Copy).then_inc(g_staged, 1)
                    a.wait_ge(sent, g + 1)
                    a.activation(rows[parity], c.rows_a[:, bass.ds(g * 2 * D, 2 * D)], ACT.Copy).then_inc(staged, 1)
                groups(a, body)

            @block.gpsimd
            def _(pool):
                def body(g, parity, last):
                    pool.wait_ge(sent, g + 1)
                    pool.sem_inc(gate, 1)
                    pool.tensor_copy(idx[:, parity * 4:parity * 4 + 4], c.slots[:, bass.ds(g * 4, 4)]).then_inc(idx_ready, 1)
                    pool.wait_ge(idx_ready, g + 1)
                    pool.wait_ge(staged, g + 1)
                    pool.sem_inc(gate, 1)
                    n = LAST_ROWS if last else P
                    for u in range(1 if last else 2):
                        for j in range(2):
                            k = parity * 4 + u * 2 + j
                            pool.indirect_dma_start(c.slot_in[:, :], bass.IndirectOffsetOnAxis(ap=idx[0:n, k:k + 1], axis=0),
                                                    rows[parity][0:n, u * D:(u + 1) * D], None).then_inc(landed[parity], 16)
                groups(pool, body)

            @block.sync
            def _(sp):
                sp.dma_start(b2_sb, b2).then_inc(loaded, 16)
                sp.dma_start(b1_sb.rearrange("p (e n) -> p e n", e=NE),
                             b1.rearrange("(a e) n -> a e n", a=1).broadcast_to([P, NE, HE])).then_inc(b1_loaded, 16)
                sp.sem_inc(sent, 2)

                def body(g, parity, last):
                    if last:
                        sp.wait_ge(landed[parity], (g - parity) * 32 + 32)
                    else:
                        sp.wait_ge(landed[parity], (g - parity) * 32 + 64)
                    sp.sem_inc(sent, 1)
                groups(sp, body)
                sp.wait_ge(b1_loaded, 16)

            @block.tensor
            def _(pe):
                pe.sem_inc(g_turned, 2)
                pe.sem_inc(b_summed, 2)
                pe.wait_ge(loaded, 16)

                def body(g, parity, last):
                    pe.wait_ge(g_staged, g + 1)
                    pe.wait_ge(g_copied, g + 1)
                    for u in range(2):
                        at = parity * 512 + u * P
                        mm = pe.transpose(c.ps[0:NE, at:at + P], g_buf[:, parity, u, :], c.ident[:, :])
                    mm.then_inc(g_turned, 1)
                    pe.wait_ge(g_copied, g + 3)
                    pe.wait_ge(b_added, g + 1)
                    for u in range(2):
                        at = (2 + parity) * 512 + u * D
                        mm = pe.matmul(c.ps[:, at:at + D], g_t[:, parity, u * P:(u + 1) * P], b2_sb, start=True, stop=True)
                    mm.then_inc(b_summed, 1)
                groups(pe, body)

            @block.vector
            def _(v):
                v.sem_inc(g_copied, 2)
                v.sem_inc(b_added, 2)

                def body(g, parity, last):
                    v.wait_ge(g_turned, g + 3)
                    v.wait_ge(b_summed, g + 1)
                    v.tensor_copy(g_t[:, parity, :], c.ps[0:NE, parity * 512:parity * 512 + 2 * P]).then_inc(g_copied, 1)
                    v.wait_ge(b_summed, g + 3)
                    to = c.rows_c[:, bass.ds(g * 2 * D, 2 * D)]
                    v.tensor_tensor(to, to, c.ps[:, (2 + parity) * 512:(3 + parity) * 512], ALU.add).then_inc(b_added, 1)
                groups(v, body)
                v.wait_ge(b_added, GROUPS2 + 2)


def expert_rows(c, b1_sb, w2):
    nc = c.nc
    K2 = HE // P
    TB = NE * 2 * HE
    w1_sb = c.rows_b[:, 0:TB]
    w2_sb = c.rows_a[:, 0:NE * K2 * D]
    o = NE * K2 * D
    x_in = c.rows_a[:, o:o + 4 * D].rearrange("p (b n) -> p b n", b=4)
    x_t = c.rows_a[:, o + 1024:o + 1536].rearrange("p (b n) -> p b n", b=2)
    y_out = c.rows_a[:, o + 1536:o + 2560].rearrange("p (b n) -> p b n", b=4)
    hid = c.scores[:, 0:1024].rearrange("p (b n) -> p b n", b=2)
    act = c.scores[:, 1024:2048].rearrange("p (b n) -> p b n", b=2)
    act_t = c.scores[:, 2048:3072].rearrange("p (b n) -> p b n", b=2)
    S = SLOT_TILES
    with Semaphores(nc) as s:
        def sem(n):
            return s.sem(f"exp_{n}")
        w_loaded, gate = sem("w_loaded"), sem("gate")
        arrived = [sem(f"arrived{u}") for u in range(4)]
        turned, copied, up, biased, acted, act_turned, act_copied, down, out_ready, out_free = (
            sem(n) for n in ("turned", "copied", "up", "biased", "acted", "act_turned", "act_copied", "down", "out_ready", "out_free"))
        stored = [sem(f"stored{u}") for u in range(4)]

        def load_experts(eng, r):
            packed = eng.value_load(c.slot_experts[0:1, bass.ds(r, 1)], min_val=0, max_val=(1 << EXPERT_BITS * 5) - 1)
            why = "three bits cannot hold more"
            return [nc.s_assert_within((packed >> (EXPERT_BITS * u)) & (NE - 1), 0, NE - 1,
                                       skip_runtime_bounds_check_because=why) for u in range(5)]

        def tiles(eng, n, body):
            with eng.Fori(0, S // n) as i:
                for u in range(n):
                    body(i * n + u, u)
            for t in range(S // n * n, S):
                body(t, t % n)
        with nc.Block() as block:
            @block.sync
            def _(sp):
                def body(t, u):
                    sp.wait_ge(turned, t + 1)
                    sp.dma_start(x_in[:, u, :], c.slot_in[bass.ds(t * P, P), :]).then_inc(arrived[u], 16)
                sp.dma_start(w2_sb.rearrange("p (e k n) -> p e k n", e=NE, k=K2),
                             w2.rearrange("e (k p) n -> p e k n", p=P)).then_inc(w_loaded, 16)
                tiles(sp, 4, body)

            @block.scalar
            def _(a):
                a.sem_inc(act_copied, 2)
                a.sem_inc(acted, 2)

                def gelu(t, u):
                    a.wait_ge(act_turned, t + 1)
                    a.wait_ge(biased, t + 3)
                    a.activation(act[:, u, :], hid[:, u, :], ACT.Gelu).then_inc(acted, 1)

                def body(t, u):
                    gelu(t, u)
                    a.wait_ge(down, t + 1)
                    a.wait_ge(act_turned, t + 3)
                    a.activation(act_t[:, u, :], c.ps[:, (4 + u) * 512:(5 + u) * 512], ACT.Copy).then_inc(act_copied, 1)
                tiles(a, 2, body)

            @block.tensor
            def _(pe):
                for x, n in ((turned, 4), (up, 2), (act_turned, 2), (down, 2)):
                    pe.sem_inc(x, n)

                def flip(t, u, slot):
                    pe.wait_ge(arrived[slot], (t - slot) * 4 + 16)
                    pe.wait_ge(copied, t + 1)
                    for k in range(2):
                        mm = pe.transpose(c.ps[:, u * 512 + k * P:u * 512 + (k + 1) * P], x_in[:, slot, k * P:(k + 1) * P], c.ident[:, :])
                    mm.then_inc(turned, 1)

                def first(t, u, e):
                    pe.wait_ge(copied, t + 3)
                    pe.wait_ge(biased, t + 1)
                    for k in range(2):
                        mm = pe.matmul(c.ps[:, (2 + u) * 512:(3 + u) * 512], x_t[:, u, k * P:(k + 1) * P],
                                       w1_sb[:, bass.ds(e * 2 * HE + k * HE, HE)], start=(k == 0), stop=(k == 1))
                    mm.then_inc(up, 1)

                def second(t, u):
                    pe.wait_ge(acted, t + 3)
                    pe.wait_ge(act_copied, t + 1)
                    for k in range(K2):
                        mm = pe.transpose(c.ps[:, (4 + u) * 512 + k * P:(4 + u) * 512 + (k + 1) * P], act[:, u, k * P:(k + 1) * P], c.ident[:, :])
                    mm.then_inc(act_turned, 1)

                def third(t, u, e):
                    pe.wait_ge(act_copied, t + 3)
                    pe.wait_ge(out_ready, t + 1)
                    for k in range(K2):
                        mm = pe.matmul(c.ps[:, (6 + u) * 512:(6 + u) * 512 + D], act_t[:, u, k * P:(k + 1) * P],
                                       w2_sb[:, bass.ds(e * K2 * D + k * D, D)], start=(k == 0), stop=(k == K2 - 1))
                    mm.then_inc(down, 1)
                flip(0, 0, 0)
                first(0, 0, load_experts(pe, 0)[0])
                flip(1, 1, 1)
                pe.wait_ge(w_loaded, 16)

                def body(t, q, experts, ahead=2):
                    u = q % 2
                    second(t, u)
                    if ahead > 0:
                        first(t + 1, 1 - u, experts[q + 1])
                    if ahead > 1:
                        flip(t + 2, u, (q + 2) % 4)
                    third(t, u, experts[q])
                with pe.Fori(0, (S - 2) // 4) as i:
                    experts = load_experts(pe, i)
                    for q in range(4):
                        body(i * 4 + q, q, experts)
                experts = load_experts(pe, (S - 2) // 4)
                for t in range((S - 2) // 4 * 4, S):
                    body(t, t % 4, experts, min(2, S - 1 - t))

            @block.vector
            def _(v):
                for x, n in ((copied, 2), (biased, 2), (out_ready, 2)):
                    v.sem_inc(x, n)

                def copy(t, u):
                    v.wait_ge(up, t + 1)
                    v.wait_ge(turned, t + 5)
                    v.tensor_copy(x_t[:, u, :], c.ps[:, u * 512:u * 512 + D]).then_inc(copied, 1)

                def bias(t, u, e):
                    v.wait_ge(acted, t + 1)
                    v.wait_ge(up, t + 3)
                    v.tensor_tensor(hid[:, u, :], c.ps[:, (2 + u) * 512:(3 + u) * 512], b1_sb[:, bass.ds(e * HE, HE)],
                                    ALU.add).then_inc(biased, 1)

                def result(t, u, slot):
                    v.wait_ge(out_free, t + 1)
                    v.wait_ge(down, t + 3)
                    v.tensor_copy(y_out[:, slot, :], c.ps[:, (6 + u) * 512:(6 + u) * 512 + D]).then_inc(out_ready, 1)
                copy(0, 0)
                bias(0, 0, load_experts(v, 0)[0])
                copy(1, 1)

                def body(t, q, experts, ahead=2):
                    u = q % 2
                    if ahead > 0:
                        bias(t + 1, 1 - u, experts[q + 1])
                    if ahead > 1:
                        copy(t + 2, u)
                    result(t, u, q)
                with v.Fori(0, (S - 2) // 4) as i:
                    experts = load_experts(v, i)
                    for q in range(4):
                        body(i * 4 + q, q, experts)
                experts = load_experts(v, (S - 2) // 4)
                for t in range((S - 2) // 4 * 4, S):
                    body(t, t % 4, experts, min(2, S - 1 - t))

            @block.gpsimd
            def _(pool):
                pool.sem_inc(out_free, 4)

                def body(t, slot):
                    pool.wait_ge(out_ready, t + 3)
                    pool.sem_inc(gate, 1)
                    pool.dma_start(c.slot_out[bass.ds(t * P, P), :], y_out[:, slot, :]).then_inc(stored[slot], 16)
                    pool.wait_ge(stored[slot], (t - slot) * 4 + 16)
                    pool.sem_inc(out_free, 1)
                tiles(pool, 4, body)


def combine(c, out):
    nc = c.nc
    RG = 8
    ring = c.scores[:, 0:RG * D].rearrange("p (s d) -> p s d", d=D)
    w0, w1 = c.small[:, 0:NT], c.small[:, NT:2 * NT]
    with Semaphores(nc) as s:
        def sem(n):
            return s.sem(f"comb_{n}")
        idx_ready, gate, added, written = sem("idx"), sem("gate"), sem("added"), sem("written")
        landed = [sem(f"landed{u}") for u in range(RG)]
        idx = s.enter_context(nc.sbuf_tensor("comb_idx_buf", [P, RG], U32))
        with nc.Block() as block:
            @block.gpsimd
            def _(pool):
                def body(g, parity, last):
                    pool.wait_ge(added, g * 4 + 4)
                    pool.sem_inc(gate, 1)
                    pool.tensor_copy(idx[:, parity * 4:parity * 4 + 4], c.slots[:, bass.ds(g * 4, 4)]).then_inc(idx_ready, 1)
                    pool.wait_ge(idx_ready, g + 1)
                    pool.sem_inc(gate, 1)
                    n = LAST_ROWS if last else P
                    for k in range(2 if last else 4):
                        slot = parity * 4 + k
                        pool.indirect_dma_start(ring[0:n, slot, :], None, c.slot_out[:, :],
                                                bass.IndirectOffsetOnAxis(ap=idx[0:n, slot:slot + 1], axis=0)).then_inc(landed[slot], 16)
                groups(pool, body)

            @block.vector
            def _(v):
                v.sem_inc(added, 8)

                def body(g, parity, last):
                    n = LAST_ROWS if last else P
                    for u in range(1 if last else 2):
                        to = c.rows_c[0:n, bass.ds(g * 2 * D + u * D, D)]
                        for j, w in enumerate((w0, w1)):
                            slot = parity * 4 + u * 2 + j
                            v.wait_ge(landed[slot], (g - parity) * 8 + 16)
                            v.wait_ge(added, g * 4 + u * 2 + j + 8)
                            v.scalar_tensor_tensor(to, ring[0:n, slot, :], w[0:n, bass.ds(g * 2 + u, 1)], to,
                                                   ALU.mult, ALU.add).then_inc(added, 1)
                groups(v, body)

            @block.sync
            def _(sp):
                def body(g, parity, last):
                    for u in range(1 if last else 2):
                        sp.wait_ge(added, g * 4 + u * 2 + 10)
                        n = LAST_ROWS if last else P
                        sp.dma_start(out[bass.ds(g * 2 * P + u * P, n), :],
                                     c.rows_c[0:n, bass.ds(g * 2 * D + u * D, D)]).then_inc(written, 16)
                groups(sp, body)
                sp.wait_ge(written, 16 * NODE_TILES)


def build(nc, x, src, dst, L0_gnn_Wq, L0_gnn_Wk, L0_gnn_Wv, L0_gnn_Wo, L0_gnn_ln_g, L0_gnn_ln_b, L0_gnn_w1, L0_gnn_b1,
          L0_gnn_w2, L0_gnn_b2, L0_ffn_Wr, L0_ffn_br, L0_ffn_W1, L0_ffn_b1, L0_ffn_W2, L0_ffn_b2, L0_ffn_gamma,
          L0_ffn_beta, L1_gnn_W_self, L1_gnn_W_neigh, L1_ffn_gamma, L1_ffn_beta, L1_ffn_Wr, L1_ffn_br, L1_ffn_W1,
          L1_ffn_b1, L1_ffn_W2, L1_ffn_b2, out, probe=None):
    with ExitStack() as ctx:
        c = Core(nc, ctx)
        say = probe or (lambda c, what: None)
        layers = L0_gnn_Wq.shape[0]
        with ExitStack() as memory:
            c.rows_room(memory, "attention")
            constants(c)
            item_tables(c, src, dst)
            say(c, "tables")
            segment_masks(c, x)
            layer_norm(c, c.rows_a, c.rows_a, "ln_in")
            say(c, "ln_in")
            for l in range(layers):
                qkv(c, L0_gnn_Wq[l], L0_gnn_Wk[l], L0_gnn_Wv[l], f"qkv{l}")
                say(c, f"qkv{l}")
                with ExitStack() as layer_memory:
                    c.scores_room(layer_memory, f"layer{l}")
                    edge_scores(c, f"score{l}")
                    say(c, f"score{l}")
                    segment_softmax(c, f"soft{l}")
                    say(c, f"soft{l}")
                    edge_sums(c, c.v_dram[:, :], True, f"sum{l}")
                    say(c, f"sum{l}")
                    attention_out(c, L0_gnn_Wo[l], f"out{l}", x if l == layers - 1 else None)
                    layer_norm(c, c.rows_a, c.rows_a, f"ln_l{l}", True, L0_gnn_ln_g[l], L0_gnn_ln_b[l])
                    say(c, f"layer{l}")
        with ExitStack() as memory:
            room = FfnRoom(c, memory)
            mlp_weights(c, room, L0_gnn_w1, L0_gnn_b1, L0_gnn_w2, L0_gnn_b2)
            ffn(c, room, ACT.Relu, c.rows_c, "mlp")
            say(c, "x1")
            layer_norm(c, c.rows_c, c.rows_a, "ln_x1", True)
            work = memory.enter_context(nc.sbuf_tensor("route_work", [P, 1152], F32))
            route_all(c, room, work, L0_ffn_Wr, L0_ffn_br, L0_ffn_W1, L0_ffn_b1, L0_ffn_W2, L0_ffn_b2)
            say(c, "route")
            ffn(c, room, ACT.Gelu, c.rows_a, "moe_all", clear_slots=True)
        with ExitStack() as memory:
            c.rows_room(memory, "sage")
            c.scores_room(memory, "sage")
            layer_norm(c, c.rows_a, c.rows_a, "ln_ffn", True, L0_ffn_gamma, L0_ffn_beta, c.rows_c)
            say(c, "x2")
            layer_norm(c, c.rows_c, c.rows_a, "ln_x2")
            sage_products(c, L1_gnn_W_self, L1_gnn_W_neigh)
            edge_sums(c, c.k_dram[:, :], False, "sage_sum")
            add_neighbours(c)
            say(c, "x3")
            layer_norm(c, c.rows_c, c.rows_a, "ln_x3")
            layer_norm(c, c.rows_a, c.rows_a, "ln_tok", False, L1_ffn_gamma, L1_ffn_beta)
            gates = memory.enter_context(nc.sbuf_tensor("gates", [P, NT * 8], F32))
            token_routes(c, gates[:, :], L1_ffn_Wr, L1_ffn_br, L1_ffn_W1)
            b1_sb = c.rows_b[:, NE * 2 * HE:NE * 3 * HE]
            dispatch(c, gates[:, :], L1_ffn_b2, b1_sb, L1_ffn_b1)
            expert_rows(c, b1_sb, L1_ffn_W2)
            combine(c, out)


_INS = ['x', 'src', 'dst', 'L0_gnn_Wq', 'L0_gnn_Wk', 'L0_gnn_Wv', 'L0_gnn_Wo', 'L0_gnn_ln_g', 'L0_gnn_ln_b',
        'L0_gnn_w1', 'L0_gnn_b1', 'L0_gnn_w2', 'L0_gnn_b2', 'L0_ffn_Wr', 'L0_ffn_br', 'L0_ffn_W1', 'L0_ffn_b1',
        'L0_ffn_W2', 'L0_ffn_b2', 'L0_ffn_gamma', 'L0_ffn_beta', 'L1_gnn_W_self', 'L1_gnn_W_neigh', 'L1_ffn_gamma',
        'L1_ffn_beta', 'L1_ffn_Wr', 'L1_ffn_br', 'L1_ffn_W1', 'L1_ffn_b1', 'L1_ffn_W2', 'L1_ffn_b2']
_OUTS = [((N, D), 'float32')]


def kernel(**inputs):
    import numpy as _np
    import concourse.bacc as _bacc
    from concourse import mybir as _mybir
    from concourse.bass_utils import run_bass_kernel_spmd as _run

    nc = _bacc.Bacc("TRN2", target_bir_lowering=False, num_devices=1)
    arrays, args = {}, []
    for name in _INS:
        a = _np.ascontiguousarray(inputs[name])
        arrays[f"in_{name}_dram"] = a
        args.append(nc.dram_tensor(f"in_{name}_dram", a.shape, _mybir.dt.from_np(a.dtype), kind="ExternalInput").ap())
    for i, (shape, dtype) in enumerate(_OUTS):
        dt = _mybir.dt.from_np(_np.dtype(dtype))
        args.append(nc.dram_tensor(f"out_{i}_dram", shape, dt, kind="ExternalOutput").ap())
    build(nc, *args)
    r = _run(nc, [arrays], core_ids=[0])
    return r.results[0]["out_0_dram"]
```
